# Optimizing a Trainium2 kernel written in Bass

```python
import numpy as np
import jax
import jax.numpy as jnp

def _softmax(x, axis=-1):
    return jax.nn.softmax(x, axis=axis)

def _gelu(x):
    return jax.nn.gelu(x, approximate=True)

def _silu(x):
    return jax.nn.silu(x)

def _sigmoid(x):
    return jax.nn.sigmoid(x)

def _layernorm(x, axis=-1, eps=1e-05):
    m = jnp.mean(x, axis=axis, keepdims=True)
    v = jnp.var(x, axis=axis, keepdims=True)
    return (x - m) / jnp.sqrt(v + eps)

def _scatter_add(tgt, idx, src, axis=0):
    return tgt.at[idx].add(src)

def _segment_sum(src, seg, n):
    return jax.ops.segment_sum(src, seg, n)
kernel_name = 'mk_xattn_seq_d4_seqx_r8_7ac407'

def setup_inputs(seed: int=0):
    np.random.seed(seed)
    _w = jnp.asarray

    def _rec_inputs():
        import jax
        import jax.numpy as jnp
        _rk = jax.random.key(seed)
        x = -0.000125 + 0.9999 * jax.random.normal(jax.random.fold_in(_rk, 1), (8, 256, 256), jnp.float32)
        _lenS = 256 - jax.random.randint(jax.random.fold_in(_rk, 7), (8,), 0, max(1, 256 // 4) + 1, jnp.int32)
        _lenS2 = 64 - jax.random.randint(jax.random.fold_in(_rk, 8), (8,), 0, max(1, 64 // 4) + 1, jnp.int32)
        _ctx_1024P = jax.random.normal(jax.random.fold_in(_rk, 11), (8, 16, 128), jnp.float32)
        _ctx_1024c = jax.random.dirichlet(jax.random.fold_in(_rk, 511), 0.3 * jnp.ones((16,), jnp.float32), (8, 64))
        _ctx_1024t = jnp.einsum('bsk,bkd->bsd', _ctx_1024c, _ctx_1024P)
        _ctx_1024t = _ctx_1024t * jax.lax.rsqrt(jnp.mean(jnp.square(_ctx_1024t)) + 1e-12) * 0.953939
        ctx_1024 = 4.13588e-05 + 0.999923 * (_ctx_1024t + 0.3 * jax.random.normal(jax.random.fold_in(_rk, 611), (8, 64, 128), jnp.float32))
        pos_1xS = jnp.broadcast_to(jnp.arange(256, dtype=jnp.int32), (1, 256))
        _validS = jnp.arange(256)[None, :] < _lenS[:, None]
        _validS2 = jnp.arange(64)[None, :] < _lenS2[:, None]
        _causal = jnp.tril(jnp.ones((256, 256), dtype=bool))
        mask_BxS_ik0 = jnp.where(jnp.broadcast_to(_validS[:, :], (8, 256)), 0, 1).astype(jnp.int32)
        mask_BxS2_bk0 = jnp.logical_not(jnp.broadcast_to(_validS2[:, :], (8, 64)))
        return (x, ctx_1024, pos_1xS, mask_BxS_ik0, mask_BxS2_bk0)
    x, ctx_1024, pos_1xS, mask_BxS_ik0, mask_BxS2_bk0 = _rec_inputs()

    def _L0_xattn_setup():
        import jax, jax.numpy as jnp
        import numpy as np
        EPS = 1e-06

        def _rmsnorm(x, w):
            var = jnp.mean(jnp.square(x), axis=-1, keepdims=True)
            return x * jax.lax.rsqrt(var + EPS) * w
        key = jax.random.key(seed)
        ks = jax.random.split(key, 6)
        B, N, M = (4, 512, 256)
        d_model, memory_dim = (256, 128)
        hidden_states = jax.random.normal(ks[0], (B, N, d_model), dtype=jnp.float32)
        memory = jax.random.normal(ks[1], (B, M, memory_dim), dtype=jnp.float32)
        W_mem = jax.random.normal(ks[2], (d_model, memory_dim), dtype=jnp.float32) / np.sqrt(memory_dim)
        W_gate = jax.random.normal(ks[3], (d_model, 2 * d_model), dtype=jnp.float32) / np.sqrt(2 * d_model)
        b_gate = jax.random.normal(ks[4], (d_model,), dtype=jnp.float32) * 0.01
        norm_w = jnp.ones((d_model,), dtype=jnp.float32)
        return {'hidden_states': hidden_states, 'memory': memory, 'W_mem': W_mem, 'W_gate': W_gate, 'b_gate': b_gate, 'norm_w': norm_w}
    _L0_xattn_all = _L0_xattn_setup()
    _L0_xattn_in = {k: v for k, v in _L0_xattn_all.items() if k in ('W_mem', 'W_gate', 'b_gate', 'norm_w')}
    del _L0_xattn_all

    def _L1_xattn_setup():
        import jax, jax.numpy as jnp
        import numpy as np
        H = 256
        NH = 16
        HD = H // NH
        CH = 128
        CC = 128
        CHD = CC // NH
        I = 688
        B = 2
        L = 256
        LE = 128
        EPS = 1e-06

        def rms_norm(x, w):
            xf = x.astype(jnp.float32)
            var = jnp.mean(xf * xf, axis=-1, keepdims=True)
            return (w * (xf * jax.lax.rsqrt(var + EPS))).astype(x.dtype)

        def expert_mask(tt):
            vm = jnp.zeros(tt.shape, dtype=bool)
            vm = vm.at[:, :-1].set((tt[:, :-1] == 1) & (tt[:, 1:] == 1))
            return vm

        def rotate_half(x):
            d = x.shape[-1] // 2
            return jnp.concatenate([-x[..., d:], x[..., :d]], axis=-1)

        def apply_rotary(q, k, position_ids, seq_len):
            inv = 1.0 / 10000.0 ** (jnp.arange(0, HD, 2, dtype=jnp.float32) / HD)
            t = jnp.arange(seq_len, dtype=jnp.float32)
            freqs = jnp.outer(t, inv)
            emb = jnp.concatenate([freqs, freqs], axis=-1)
            cos = jnp.cos(emb)[position_ids][:, None].astype(q.dtype)
            sin = jnp.sin(emb)[position_ids][:, None].astype(q.dtype)
            return (q * cos + rotate_half(q) * sin, k * cos + rotate_half(k) * sin)

        def sdpa(q, k, v, causal):
            scale = 1.0 / np.sqrt(q.shape[-1])
            scores = jnp.einsum('bhqd,bhkd->bhqk', q * scale, k)
            if causal:
                mask = jnp.tril(jnp.ones((q.shape[-2], k.shape[-2]), dtype=bool))
                scores = jnp.where(mask, scores, jnp.finfo(jnp.float32).min)
            p = jax.nn.softmax(scores.astype(jnp.float32), axis=-1).astype(q.dtype)
            return jnp.einsum('bhqk,bhkd->bhqd', p, v)

        def heads(x, nh, hd):
            b, l, _ = x.shape
            return x.reshape(b, l, nh, hd).transpose(0, 2, 1, 3)
        key = jax.random.key(seed)
        ks = jax.random.split(key, 20)
        s = 0.02
        f32 = jnp.float32
        return {'hidden_states': jax.random.normal(ks[0], (B, L, H), f32), 'encoder_outputs': jax.random.normal(ks[1], (B, LE, CH), f32), 'token_type_ids': jax.random.randint(ks[2], (B, L), 0, 2, jnp.int32), 'position_ids': jnp.arange(L, dtype=jnp.int32)[None, :], 'ln_in_w': jnp.ones((H,), f32), 'ln_post_attn_w': jnp.ones((H,), f32), 'ln_post_cross_w': jnp.ones((H,), f32), 'v_qkv': jax.random.normal(ks[3], (H, 3 * H), f32) * s, 'l_qkv': jax.random.normal(ks[4], (H, 3 * H), f32) * s, 'v_dense': jax.random.normal(ks[5], (H, H), f32) * s, 'l_dense': jax.random.normal(ks[6], (H, H), f32) * s, 'cq_w': jax.random.normal(ks[7], (H, CC), f32) * s, 'ckv_w': jax.random.normal(ks[8], (CH, 2 * CC), f32) * s, 'cdense_w': jax.random.normal(ks[9], (CC, H), f32) * s, 'v_gate': jax.random.normal(ks[10], (H, I), f32) * s, 'v_up': jax.random.normal(ks[11], (H, I), f32) * s, 'v_down': jax.random.normal(ks[12], (I, H), f32) * s, 'l_gate': jax.random.normal(ks[13], (H, I), f32) * s, 'l_up': jax.random.normal(ks[14], (H, I), f32) * s, 'l_down': jax.random.normal(ks[15], (I, H), f32) * s}
    _L1_xattn_all = _L1_xattn_setup()
    _L1_xattn_in = {k: v for k, v in _L1_xattn_all.items() if k in ('ln_in_w', 'ln_post_attn_w', 'ln_post_cross_w', 'v_qkv', 'l_qkv', 'v_dense', 'l_dense', 'cq_w', 'ckv_w', 'cdense_w', 'v_gate', 'v_up', 'v_down', 'l_gate', 'l_up', 'l_down')}
    del _L1_xattn_all

    def _L2_xattn_setup():
        import jax, jax.numpy as jnp
        import numpy as np
        DIM = 256
        DIM_MEDIA = 128
        HEADS = 16
        DIM_HEAD = 64
        INNER = HEADS * DIM_HEAD
        FF_INNER = 4 * DIM
        B, N_TOK, N_LAT = (4, 256, 64)
        EPS = 1e-05

        def layernorm(x, g, b):
            mu = jnp.mean(x, axis=-1, keepdims=True)
            var = jnp.var(x, axis=-1, keepdims=True)
            return (x - mu) * jax.lax.rsqrt(var + EPS) * g + b
        key = jax.random.key(seed)
        ks = jax.random.split(key, 12)
        x = jax.random.normal(ks[0], (B, N_TOK, DIM), dtype=jnp.float32)
        media = jax.random.normal(ks[1], (B, N_LAT, DIM_MEDIA), dtype=jnp.float32)
        media_mask = jax.random.randint(ks[2], (B, N_LAT), 0, 2).astype(bool)
        media_mask = media_mask.at[:, 0].set(True)
        s = lambda d: 1.0 / np.sqrt(d)
        Wq = jax.random.normal(ks[3], (DIM, INNER), dtype=jnp.float32) * s(DIM)
        Wkv = jax.random.normal(ks[4], (DIM_MEDIA, 2 * INNER), dtype=jnp.float32) * s(DIM_MEDIA)
        Wo = jax.random.normal(ks[5], (INNER, DIM), dtype=jnp.float32) * s(INNER)
        W1 = jax.random.normal(ks[6], (DIM, FF_INNER), dtype=jnp.float32) * s(DIM)
        W2 = jax.random.normal(ks[7], (FF_INNER, DIM), dtype=jnp.float32) * s(FF_INNER)
        return {'x': x, 'media': media, 'media_mask': media_mask, 'ln_q_g': jnp.ones((DIM,), jnp.float32), 'ln_q_b': jnp.zeros((DIM,), jnp.float32), 'Wq': Wq, 'Wkv': Wkv, 'Wo': Wo, 'attn_gate': jax.random.normal(ks[8], (1,), jnp.float32) * 0.5, 'ln_ff_g': jnp.ones((DIM,), jnp.float32), 'ln_ff_b': jnp.zeros((DIM,), jnp.float32), 'W1': W1, 'W2': W2, 'ff_gate': jax.random.normal(ks[9], (1,), jnp.float32) * 0.5}
    _L2_xattn_all = _L2_xattn_setup()
    _L2_xattn_in = {k: v for k, v in _L2_xattn_all.items() if k in ('ln_q_g', 'ln_q_b', 'Wq', 'Wkv', 'Wo', 'attn_gate', 'ln_ff_g', 'ln_ff_b', 'W1', 'W2', 'ff_gate')}
    del _L2_xattn_all

    def _L3_xattn_setup():
        import jax, jax.numpy as jnp
        import numpy as np
        H = 256
        NH = 16
        HD = H // NH
        CH = 128
        CC = 128
        CHD = CC // NH
        I = 688
        B = 2
        L = 256
        LE = 128
        EPS = 1e-06

        def rms_norm(x, w):
            xf = x.astype(jnp.float32)
            var = jnp.mean(xf * xf, axis=-1, keepdims=True)
            return (w * (xf * jax.lax.rsqrt(var + EPS))).astype(x.dtype)

        def expert_mask(tt):
            vm = jnp.zeros(tt.shape, dtype=bool)
            vm = vm.at[:, :-1].set((tt[:, :-1] == 1) & (tt[:, 1:] == 1))
            return vm

        def rotate_half(x):
            d = x.shape[-1] // 2
            return jnp.concatenate([-x[..., d:], x[..., :d]], axis=-1)

        def apply_rotary(q, k, position_ids, seq_len):
            inv = 1.0 / 10000.0 ** (jnp.arange(0, HD, 2, dtype=jnp.float32) / HD)
            t = jnp.arange(seq_len, dtype=jnp.float32)
            freqs = jnp.outer(t, inv)
            emb = jnp.concatenate([freqs, freqs], axis=-1)
            cos = jnp.cos(emb)[position_ids][:, None].astype(q.dtype)
            sin = jnp.sin(emb)[position_ids][:, None].astype(q.dtype)
            return (q * cos + rotate_half(q) * sin, k * cos + rotate_half(k) * sin)

        def sdpa(q, k, v, causal):
            scale = 1.0 / np.sqrt(q.shape[-1])
            scores = jnp.einsum('bhqd,bhkd->bhqk', q * scale, k)
            if causal:
                mask = jnp.tril(jnp.ones((q.shape[-2], k.shape[-2]), dtype=bool))
                scores = jnp.where(mask, scores, jnp.finfo(jnp.float32).min)
            p = jax.nn.softmax(scores.astype(jnp.float32), axis=-1).astype(q.dtype)
            return jnp.einsum('bhqk,bhkd->bhqd', p, v)

        def heads(x, nh, hd):
            b, l, _ = x.shape
            return x.reshape(b, l, nh, hd).transpose(0, 2, 1, 3)
        key = jax.random.key(seed)
        ks = jax.random.split(key, 20)
        s = 0.02
        f32 = jnp.float32
        return {'hidden_states': jax.random.normal(ks[0], (B, L, H), f32), 'encoder_outputs': jax.random.normal(ks[1], (B, LE, CH), f32), 'token_type_ids': jax.random.randint(ks[2], (B, L), 0, 2, jnp.int32), 'position_ids': jnp.arange(L, dtype=jnp.int32)[None, :], 'ln_in_w': jnp.ones((H,), f32), 'ln_post_attn_w': jnp.ones((H,), f32), 'ln_post_cross_w': jnp.ones((H,), f32), 'v_qkv': jax.random.normal(ks[3], (H, 3 * H), f32) * s, 'l_qkv': jax.random.normal(ks[4], (H, 3 * H), f32) * s, 'v_dense': jax.random.normal(ks[5], (H, H), f32) * s, 'l_dense': jax.random.normal(ks[6], (H, H), f32) * s, 'cq_w': jax.random.normal(ks[7], (H, CC), f32) * s, 'ckv_w': jax.random.normal(ks[8], (CH, 2 * CC), f32) * s, 'cdense_w': jax.random.normal(ks[9], (CC, H), f32) * s, 'v_gate': jax.random.normal(ks[10], (H, I), f32) * s, 'v_up': jax.random.normal(ks[11], (H, I), f32) * s, 'v_down': jax.random.normal(ks[12], (I, H), f32) * s, 'l_gate': jax.random.normal(ks[13], (H, I), f32) * s, 'l_up': jax.random.normal(ks[14], (H, I), f32) * s, 'l_down': jax.random.normal(ks[15], (I, H), f32) * s}
    _L3_xattn_all = _L3_xattn_setup()
    _L3_xattn_in = {k: v for k, v in _L3_xattn_all.items() if k in ('ln_in_w', 'ln_post_attn_w', 'ln_post_cross_w', 'v_qkv', 'l_qkv', 'v_dense', 'l_dense', 'cq_w', 'ckv_w', 'cdense_w', 'v_gate', 'v_up', 'v_down', 'l_gate', 'l_up', 'l_down')}
    del _L3_xattn_all
    return {'x': x, 'ctx_1024': ctx_1024, 'pos_1xS': pos_1xS, 'mask_BxS_ik0': mask_BxS_ik0, 'mask_BxS2_bk0': mask_BxS2_bk0, 'L0_xattn_W_mem': _L0_xattn_in['W_mem'], 'L0_xattn_W_gate': _L0_xattn_in['W_gate'], 'L0_xattn_b_gate': _L0_xattn_in['b_gate'], 'L0_xattn_norm_w': _L0_xattn_in['norm_w'], 'L1_xattn_ln_in_w': _L1_xattn_in['ln_in_w'], 'L1_xattn_ln_post_attn_w': _L1_xattn_in['ln_post_attn_w'], 'L1_xattn_ln_post_cross_w': _L1_xattn_in['ln_post_cross_w'], 'L1_xattn_v_qkv': _L1_xattn_in['v_qkv'], 'L1_xattn_l_qkv': _L1_xattn_in['l_qkv'], 'L1_xattn_v_dense': _L1_xattn_in['v_dense'], 'L1_xattn_l_dense': _L1_xattn_in['l_dense'], 'L1_xattn_cq_w': _L1_xattn_in['cq_w'], 'L1_xattn_ckv_w': _L1_xattn_in['ckv_w'], 'L1_xattn_cdense_w': _L1_xattn_in['cdense_w'], 'L1_xattn_v_gate': _L1_xattn_in['v_gate'], 'L1_xattn_v_up': _L1_xattn_in['v_up'], 'L1_xattn_v_down': _L1_xattn_in['v_down'], 'L1_xattn_l_gate': _L1_xattn_in['l_gate'], 'L1_xattn_l_up': _L1_xattn_in['l_up'], 'L1_xattn_l_down': _L1_xattn_in['l_down'], 'L2_xattn_ln_q_g': _L2_xattn_in['ln_q_g'], 'L2_xattn_ln_q_b': _L2_xattn_in['ln_q_b'], 'L2_xattn_Wq': _L2_xattn_in['Wq'], 'L2_xattn_Wkv': _L2_xattn_in['Wkv'], 'L2_xattn_Wo': _L2_xattn_in['Wo'], 'L2_xattn_attn_gate': _L2_xattn_in['attn_gate'], 'L2_xattn_ln_ff_g': _L2_xattn_in['ln_ff_g'], 'L2_xattn_ln_ff_b': _L2_xattn_in['ln_ff_b'], 'L2_xattn_W1': _L2_xattn_in['W1'], 'L2_xattn_W2': _L2_xattn_in['W2'], 'L2_xattn_ff_gate': _L2_xattn_in['ff_gate'], 'L3_xattn_ln_in_w': _L3_xattn_in['ln_in_w'], 'L3_xattn_ln_post_attn_w': _L3_xattn_in['ln_post_attn_w'], 'L3_xattn_ln_post_cross_w': _L3_xattn_in['ln_post_cross_w'], 'L3_xattn_v_qkv': _L3_xattn_in['v_qkv'], 'L3_xattn_l_qkv': _L3_xattn_in['l_qkv'], 'L3_xattn_v_dense': _L3_xattn_in['v_dense'], 'L3_xattn_l_dense': _L3_xattn_in['l_dense'], 'L3_xattn_cq_w': _L3_xattn_in['cq_w'], 'L3_xattn_ckv_w': _L3_xattn_in['ckv_w'], 'L3_xattn_cdense_w': _L3_xattn_in['cdense_w'], 'L3_xattn_v_gate': _L3_xattn_in['v_gate'], 'L3_xattn_v_up': _L3_xattn_in['v_up'], 'L3_xattn_v_down': _L3_xattn_in['v_down'], 'L3_xattn_l_gate': _L3_xattn_in['l_gate'], 'L3_xattn_l_up': _L3_xattn_in['l_up'], 'L3_xattn_l_down': _L3_xattn_in['l_down']}

def reference(x, ctx_1024, pos_1xS, mask_BxS_ik0, mask_BxS2_bk0, L0_xattn_W_mem, L0_xattn_W_gate, L0_xattn_b_gate, L0_xattn_norm_w, L1_xattn_ln_in_w, L1_xattn_ln_post_attn_w, L1_xattn_ln_post_cross_w, L1_xattn_v_qkv, L1_xattn_l_qkv, L1_xattn_v_dense, L1_xattn_l_dense, L1_xattn_cq_w, L1_xattn_ckv_w, L1_xattn_cdense_w, L1_xattn_v_gate, L1_xattn_v_up, L1_xattn_v_down, L1_xattn_l_gate, L1_xattn_l_up, L1_xattn_l_down, L2_xattn_ln_q_g, L2_xattn_ln_q_b, L2_xattn_Wq, L2_xattn_Wkv, L2_xattn_Wo, L2_xattn_attn_gate, L2_xattn_ln_ff_g, L2_xattn_ln_ff_b, L2_xattn_W1, L2_xattn_W2, L2_xattn_ff_gate, L3_xattn_ln_in_w, L3_xattn_ln_post_attn_w, L3_xattn_ln_post_cross_w, L3_xattn_v_qkv, L3_xattn_l_qkv, L3_xattn_v_dense, L3_xattn_l_dense, L3_xattn_cq_w, L3_xattn_ckv_w, L3_xattn_cdense_w, L3_xattn_v_gate, L3_xattn_v_up, L3_xattn_v_down, L3_xattn_l_gate, L3_xattn_l_up, L3_xattn_l_down):
    import jax
    import jax.numpy as jnp

    def _L0_xattn_ref(hidden_states, memory, W_mem, W_gate, b_gate, norm_w):
        import jax, jax.numpy as jnp
        import numpy as np
        EPS = 1e-06

        def _rmsnorm(x, w):
            var = jnp.mean(jnp.square(x), axis=-1, keepdims=True)
            return x * jax.lax.rsqrt(var + EPS) * w
        D = hidden_states.shape[-1]
        memory_proj = jnp.einsum('bme,de->bmd', memory, W_mem)
        scores = jnp.einsum('bnd,bmd->bnm', hidden_states, memory_proj) / jnp.sqrt(jnp.float32(D))
        attn = jax.nn.softmax(scores, axis=-1)
        memory_context = jnp.einsum('bnm,bmd->bnd', attn, memory_proj)
        gate_input = jnp.concatenate([hidden_states, memory_context], axis=-1)
        gate = jax.nn.sigmoid(jnp.einsum('bnf,df->bnd', gate_input, W_gate) + b_gate)
        fused = hidden_states + gate * memory_context
        return _rmsnorm(fused, norm_w)

    def _L1_xattn_ref(hidden_states, encoder_outputs, token_type_ids, position_ids, ln_in_w, ln_post_attn_w, ln_post_cross_w, v_qkv, l_qkv, v_dense, l_dense, cq_w, ckv_w, cdense_w, v_gate, v_up, v_down, l_gate, l_up, l_down):
        import jax, jax.numpy as jnp
        import numpy as np
        H = 256
        NH = 16
        HD = H // NH
        CH = 128
        CC = 128
        CHD = CC // NH
        I = 688
        B = 2
        L = 256
        LE = 128
        EPS = 1e-06

        def rms_norm(x, w):
            xf = x.astype(jnp.float32)
            var = jnp.mean(xf * xf, axis=-1, keepdims=True)
            return (w * (xf * jax.lax.rsqrt(var + EPS))).astype(x.dtype)

        def expert_mask(tt):
            vm = jnp.zeros(tt.shape, dtype=bool)
            vm = vm.at[:, :-1].set((tt[:, :-1] == 1) & (tt[:, 1:] == 1))
            return vm

        def rotate_half(x):
            d = x.shape[-1] // 2
            return jnp.concatenate([-x[..., d:], x[..., :d]], axis=-1)

        def apply_rotary(q, k, position_ids, seq_len):
            inv = 1.0 / 10000.0 ** (jnp.arange(0, HD, 2, dtype=jnp.float32) / HD)
            t = jnp.arange(seq_len, dtype=jnp.float32)
            freqs = jnp.outer(t, inv)
            emb = jnp.concatenate([freqs, freqs], axis=-1)
            cos = jnp.cos(emb)[position_ids][:, None].astype(q.dtype)
            sin = jnp.sin(emb)[position_ids][:, None].astype(q.dtype)
            return (q * cos + rotate_half(q) * sin, k * cos + rotate_half(k) * sin)

        def sdpa(q, k, v, causal):
            scale = 1.0 / np.sqrt(q.shape[-1])
            scores = jnp.einsum('bhqd,bhkd->bhqk', q * scale, k)
            if causal:
                mask = jnp.tril(jnp.ones((q.shape[-2], k.shape[-2]), dtype=bool))
                scores = jnp.where(mask, scores, jnp.finfo(jnp.float32).min)
            p = jax.nn.softmax(scores.astype(jnp.float32), axis=-1).astype(q.dtype)
            return jnp.einsum('bhqk,bhkd->bhqd', p, v)

        def heads(x, nh, hd):
            b, l, _ = x.shape
            return x.reshape(b, l, nh, hd).transpose(0, 2, 1, 3)
        b, l, _ = hidden_states.shape
        vm = expert_mask(token_type_ids)[..., None]
        residual = hidden_states
        x = rms_norm(hidden_states, ln_in_w)
        mixed = jnp.where(vm, x @ v_qkv, x @ l_qkv)
        q, k, v = jnp.split(mixed, 3, axis=-1)
        q, k, v = (heads(q, NH, HD), heads(k, NH, HD), heads(v, NH, HD))
        q, k = apply_rotary(q, k, position_ids, l)
        ctx = sdpa(q, k, v, causal=True)
        ctx = ctx.transpose(0, 2, 1, 3).reshape(b, l, H)
        attn_out = jnp.where(vm, ctx @ v_dense, ctx @ l_dense)
        hidden_states = residual + attn_out
        ci = rms_norm(hidden_states, ln_post_cross_w)
        cq = heads(ci @ cq_w, NH, CHD)
        ckv = encoder_outputs @ ckv_w
        ck, cv = jnp.split(ckv, 2, axis=-1)
        ck, cv = (heads(ck, NH, CHD), heads(cv, NH, CHD))
        cctx = sdpa(cq, ck, cv, causal=False)
        cctx = cctx.transpose(0, 2, 1, 3).reshape(b, l, CC)
        hidden_states = hidden_states + cctx @ cdense_w
        mi = rms_norm(hidden_states, ln_post_attn_w)
        v_out = jax.nn.silu(mi @ v_gate) * (mi @ v_up) @ v_down
        l_out = jax.nn.silu(mi @ l_gate) * (mi @ l_up) @ l_down
        hidden_states = hidden_states + jnp.where(vm, v_out, l_out)
        return hidden_states

    def _L2_xattn_ref(x, media, media_mask, ln_q_g, ln_q_b, Wq, Wkv, Wo, attn_gate, ln_ff_g, ln_ff_b, W1, W2, ff_gate):
        import jax, jax.numpy as jnp
        import numpy as np
        DIM = 256
        DIM_MEDIA = 128
        HEADS = 16
        DIM_HEAD = 64
        INNER = HEADS * DIM_HEAD
        FF_INNER = 4 * DIM
        B, N_TOK, N_LAT = (4, 256, 64)
        EPS = 1e-05

        def layernorm(x, g, b):
            mu = jnp.mean(x, axis=-1, keepdims=True)
            var = jnp.var(x, axis=-1, keepdims=True)
            return (x - mu) * jax.lax.rsqrt(var + EPS) * g + b
        scale = DIM_HEAD ** (-0.5)
        qn = layernorm(x, ln_q_g, ln_q_b)
        q = qn @ Wq * scale
        kv = media @ Wkv
        k, v = jnp.split(kv, 2, axis=-1)
        split_heads = lambda t: t.reshape(t.shape[0], t.shape[1], HEADS, DIM_HEAD).transpose(0, 2, 1, 3)
        q, k, v = (split_heads(q), split_heads(k), split_heads(v))
        sim = jnp.einsum('bhid,bhjd->bhij', q, k)
        neg_inf = jnp.finfo(sim.dtype).min
        sim = jnp.where(media_mask[:, None, None, :], sim, neg_inf)
        attn = jax.nn.softmax(sim, axis=-1)
        out = jnp.einsum('bhij,bhjd->bhid', attn, v)
        out = out.transpose(0, 2, 1, 3).reshape(x.shape[0], x.shape[1], INNER)
        attn_out = out @ Wo
        x = x + jnp.tanh(attn_gate) * attn_out
        h = layernorm(x, ln_ff_g, ln_ff_b)
        h = jax.nn.gelu(h @ W1, approximate=False) @ W2
        x = x + jnp.tanh(ff_gate) * h
        return x

    def _L3_xattn_ref(hidden_states, encoder_outputs, token_type_ids, position_ids, ln_in_w, ln_post_attn_w, ln_post_cross_w, v_qkv, l_qkv, v_dense, l_dense, cq_w, ckv_w, cdense_w, v_gate, v_up, v_down, l_gate, l_up, l_down):
        import jax, jax.numpy as jnp
        import numpy as np
        H = 256
        NH = 16
        HD = H // NH
        CH = 128
        CC = 128
        CHD = CC // NH
        I = 688
        B = 2
        L = 256
        LE = 128
        EPS = 1e-06

        def rms_norm(x, w):
            xf = x.astype(jnp.float32)
            var = jnp.mean(xf * xf, axis=-1, keepdims=True)
            return (w * (xf * jax.lax.rsqrt(var + EPS))).astype(x.dtype)

        def expert_mask(tt):
            vm = jnp.zeros(tt.shape, dtype=bool)
            vm = vm.at[:, :-1].set((tt[:, :-1] == 1) & (tt[:, 1:] == 1))
            return vm

        def rotate_half(x):
            d = x.shape[-1] // 2
            return jnp.concatenate([-x[..., d:], x[..., :d]], axis=-1)

        def apply_rotary(q, k, position_ids, seq_len):
            inv = 1.0 / 10000.0 ** (jnp.arange(0, HD, 2, dtype=jnp.float32) / HD)
            t = jnp.arange(seq_len, dtype=jnp.float32)
            freqs = jnp.outer(t, inv)
            emb = jnp.concatenate([freqs, freqs], axis=-1)
            cos = jnp.cos(emb)[position_ids][:, None].astype(q.dtype)
            sin = jnp.sin(emb)[position_ids][:, None].astype(q.dtype)
            return (q * cos + rotate_half(q) * sin, k * cos + rotate_half(k) * sin)

        def sdpa(q, k, v, causal):
            scale = 1.0 / np.sqrt(q.shape[-1])
            scores = jnp.einsum('bhqd,bhkd->bhqk', q * scale, k)
            if causal:
                mask = jnp.tril(jnp.ones((q.shape[-2], k.shape[-2]), dtype=bool))
                scores = jnp.where(mask, scores, jnp.finfo(jnp.float32).min)
            p = jax.nn.softmax(scores.astype(jnp.float32), axis=-1).astype(q.dtype)
            return jnp.einsum('bhqk,bhkd->bhqd', p, v)

        def heads(x, nh, hd):
            b, l, _ = x.shape
            return x.reshape(b, l, nh, hd).transpose(0, 2, 1, 3)
        b, l, _ = hidden_states.shape
        vm = expert_mask(token_type_ids)[..., None]
        residual = hidden_states
        x = rms_norm(hidden_states, ln_in_w)
        mixed = jnp.where(vm, x @ v_qkv, x @ l_qkv)
        q, k, v = jnp.split(mixed, 3, axis=-1)
        q, k, v = (heads(q, NH, HD), heads(k, NH, HD), heads(v, NH, HD))
        q, k = apply_rotary(q, k, position_ids, l)
        ctx = sdpa(q, k, v, causal=True)
        ctx = ctx.transpose(0, 2, 1, 3).reshape(b, l, H)
        attn_out = jnp.where(vm, ctx @ v_dense, ctx @ l_dense)
        hidden_states = residual + attn_out
        ci = rms_norm(hidden_states, ln_post_cross_w)
        cq = heads(ci @ cq_w, NH, CHD)
        ckv = encoder_outputs @ ckv_w
        ck, cv = jnp.split(ckv, 2, axis=-1)
        ck, cv = (heads(ck, NH, CHD), heads(cv, NH, CHD))
        cctx = sdpa(cq, ck, cv, causal=False)
        cctx = cctx.transpose(0, 2, 1, 3).reshape(b, l, CC)
        hidden_states = hidden_states + cctx @ cdense_w
        mi = rms_norm(hidden_states, ln_post_attn_w)
        v_out = jax.nn.silu(mi @ v_gate) * (mi @ v_up) @ v_down
        l_out = jax.nn.silu(mi @ l_gate) * (mi @ l_up) @ l_down
        hidden_states = hidden_states + jnp.where(vm, v_out, l_out)
        return hidden_states
    x = _L0_xattn_ref(x, ctx_1024, L0_xattn_W_mem, L0_xattn_W_gate, L0_xattn_b_gate, L0_xattn_norm_w)
    x = _L1_xattn_ref(x, ctx_1024, mask_BxS_ik0, pos_1xS, L1_xattn_ln_in_w, L1_xattn_ln_post_attn_w, L1_xattn_ln_post_cross_w, L1_xattn_v_qkv, L1_xattn_l_qkv, L1_xattn_v_dense, L1_xattn_l_dense, L1_xattn_cq_w, L1_xattn_ckv_w, L1_xattn_cdense_w, L1_xattn_v_gate, L1_xattn_v_up, L1_xattn_v_down, L1_xattn_l_gate, L1_xattn_l_up, L1_xattn_l_down)
    x = _L2_xattn_ref(x, ctx_1024, mask_BxS2_bk0, L2_xattn_ln_q_g, L2_xattn_ln_q_b, L2_xattn_Wq, L2_xattn_Wkv, L2_xattn_Wo, L2_xattn_attn_gate, L2_xattn_ln_ff_g, L2_xattn_ln_ff_b, L2_xattn_W1, L2_xattn_W2, L2_xattn_ff_gate)
    x = _L3_xattn_ref(x, ctx_1024, mask_BxS_ik0, pos_1xS, L3_xattn_ln_in_w, L3_xattn_ln_post_attn_w, L3_xattn_ln_post_cross_w, L3_xattn_v_qkv, L3_xattn_l_qkv, L3_xattn_v_dense, L3_xattn_l_dense, L3_xattn_cq_w, L3_xattn_ckv_w, L3_xattn_cdense_w, L3_xattn_v_gate, L3_xattn_v_up, L3_xattn_v_down, L3_xattn_l_gate, L3_xattn_l_up, L3_xattn_l_down)
    return x

_drawn_inputs = setup_inputs


def setup_inputs(seed=0):
    import zlib

    import numpy as np

    out = dict(_drawn_inputs(seed))
    spreads = {'L0_xattn_norm_w': (1.0, 0.2),
     'L1_xattn_ln_in_w': (1.0, 0.6),
     'L1_xattn_ln_post_attn_w': (1.0, 0.6),
     'L1_xattn_ln_post_cross_w': (1.0, 0.6),
     'L2_xattn_ln_q_g': (1.0, 0.6),
     'L2_xattn_ln_q_b': (0.0, 2.0),
     'L2_xattn_ln_ff_g': (1.0, 0.6),
     'L2_xattn_ln_ff_b': (0.0, 2.0),
     'L3_xattn_ln_in_w': (1.0, 0.6),
     'L3_xattn_ln_post_attn_w': (1.0, 0.6),
     'L3_xattn_ln_post_cross_w': (1.0, 0.6)}
    factors = {'L0_xattn_b_gate': 8.0,
     'L1_xattn_v_qkv': 8.0,
     'L1_xattn_v_dense': 6.424,
     'L1_xattn_cq_w': 64.0,
     'L1_xattn_v_gate': 5.496,
     'L1_xattn_v_up': 5.417,
     'L1_xattn_v_down': 5.449,
     'L2_xattn_W1': 10.839,
     'L3_xattn_v_qkv': 8.0,
     'L3_xattn_v_dense': 5.303,
     'L3_xattn_cq_w': 64.0,
     'L3_xattn_v_gate': 5.588,
     'L3_xattn_v_up': 5.498,
     'L3_xattn_v_down': 5.526,
     'L1_xattn_l_dense': 7.35,
     'L1_xattn_ckv_w': 5.934,
     'L1_xattn_cdense_w': 5.716,
     'L1_xattn_l_gate': 7.697,
     'L1_xattn_l_up': 7.484,
     'L1_xattn_l_down': 7.516,
     'L2_xattn_Wq': 15.815,
     'L2_xattn_W2': 3.267,
     'L3_xattn_l_qkv': 5.152,
     'L3_xattn_l_dense': 8.0,
     'L3_xattn_ckv_w': 8.0,
     'L3_xattn_cdense_w': 8.0,
     'L3_xattn_l_gate': 8.0,
     'L3_xattn_l_up': 8.0,
     'L3_xattn_l_down': 8.0,
     'L2_xattn_Wkv': 4.203,
     'L2_xattn_Wo': 4.199}
    for name, (base, spread) in spreads.items():
        noise = np.random.default_rng([zlib.crc32(name.encode()), seed]).standard_normal(out[name].shape)
        drawn = base * np.exp(spread * noise) if base else spread * noise
        out[name] = jnp.asarray(drawn.astype(out[name].dtype))
    for name, factor in factors.items():
        out[name] = (out[name] * factor).astype(out[name].dtype)
    return out
```

```python
from contextlib import ExitStack

import numpy as np

import concourse.bass as bass
from concourse import mybir

F32 = mybir.dt.float32
BF16 = mybir.dt.bfloat16
I32 = mybir.dt.int32
U8 = mybir.dt.uint8
ALU = mybir.AluOpType
ACT = mybir.ActivationFunctionType
X = mybir.AxisListType.X

P = 128
B, S, D = 8, 256, 256
M, C = 64, 128
KT = D // P
TT = S // P
NH = 16
HD = D // NH
CHD = C // NH
GHD = 64
INNER = NH * GHD
INTER = 688
FULL = INTER // P
TAIL = INTER - FULL * P
NF = 2 * FULL + 1
FF = 4 * D
GT = INNER // P
RMS_EPS, LN_EPS = 1e-6, 1e-5
BIG = -1e30
STREAMS = 2

C_ID, C_ROT, C_EVEN, C_ODD, C_H16, C_ROW, C_TRIG, C_SPREAD = 0, 128, 256, 257, 258, 274, 276, 788
C_END = C_SPREAD + 512


def constants():
    t = np.zeros((P, C_END), np.float32)
    p = np.arange(P)
    t[p, C_ID + p] = 1.0
    for m in range(P):
        i = m % HD
        k = m + HD // 2 if i < HD // 2 else m - HD // 2
        t[k, C_ROT + m] = -1.0 if i < HD // 2 else 1.0
    t[:, C_EVEN] = ((p // HD) % 2 == 0) * HD ** -0.5
    t[:, C_ODD] = ((p // HD) % 2 == 1) * HD ** -0.5
    t[p, C_H16 + p // CHD] = 1.0
    t[:, C_ROW], t[:, C_ROW + 1] = p, p + P
    inv = (1.0 / 10000.0 ** (np.arange(0, HD, 2, dtype=np.float32) / np.float32(HD))).astype(np.float32)
    ang = np.outer(np.arange(S, dtype=np.float32), inv).astype(np.float32)
    for tt in range(TT):
        a = ang[tt * P:(tt + 1) * P][:, (p % HD) % (HD // 2)]
        t[:, C_TRIG + 256 * tt:C_TRIG + 256 * tt + 128] = np.cos(a)
        t[:, C_TRIG + 256 * tt + 128:C_TRIG + 256 * tt + 256] = np.sin(a)
    for e in range(2):
        for k in range(KT):
            at = C_SPREAD + (e * KT + k) * P
            t[e * NH + k * 8 + p // HD, at + p] = 1.0
    return t


class Steps:

    def __init__(self, sems, names):
        self.sems, self.names = sems, list(names)
        self.value = {n: i + 1 for i, n in enumerate(self.names)}
        self.issued = [0, 0]

    def does(self, s, *name):
        assert self.names[self.issued[s]] == name, (name, self.names[self.issued[s]])
        self.issued[s] += 1
        return self.sems[s], 1

    def did(self, s, *name):
        return self.sems[s], self.value[name]

    def last(self, s):
        return self.sems[s], len(self.names)


def names(text):
    return [(w,) for w in text.split()]



UNITS = range(4)
LAG1, LAG2 = 1, 2


def attention_steps(first, *rest):
    out = []
    for h in range(NH + len(rest)):
        for lag, w in enumerate((first, *rest)):
            if 0 <= h - lag < NH:
                out += [(n, h - lag) for n in w.split()]
    return out


def norm_steps(kind, n):
    return [(w, n) for w in kind.split()]


FUSE_PE = names("mem_rows scores probs_t context gate") + norm_steps("sumsq spread", 0)
FUSE_ACT = names("mem_rows exp probs_t context gate0 gate1") + norm_steps("square", 0) + names("x_out")
FUSE_DVE = names("max sub sum recip norm gated fused") + norm_steps("mean diag0 diag1", 0) + names("y0 y1")
FUSE_POOL = names("x_in mem_in") + norm_steps("rstd", 0)

MOT_PE = (norm_steps("sumsq spread", 0) + names("q k v rot_q rot_k") + attention_steps("s", "t", "pv")
          + names("rinv_t rinv_v rinv_l dense") + norm_steps("sumsq spread", 1) + names("cq ck cv")
          + [("cs", u) for u in UNITS] + [("ct", u) for u in UNITS] + names("cpv cdense")
          + norm_steps("sumsq spread", 2) + [("up", f) for f in range(NF)] + names("down"))
MOT_ACT = (norm_steps("square", 0) + names("q k v0 v1 ke ko") + attention_steps("exp0 exp1")
           + names("rinv_v rinv_l") + norm_steps("square", 1) + names("cq ck")
           + [("cexp", u) for u in UNITS] + [("ct", u) for u in UNITS] + names("cctx")
           + norm_steps("square", 2) + [("tanh", f) for f in range(NF)])
MOT_DVE = (norm_steps("mean diag0 diag1 rv rl yv0 yv1 yl0 yl1", 0) + names("qr q2 kr k2")
           + attention_steps("max0 max1", "pt") + names("rinv rvl0 rvl1 rvl2 rvl3 rinv_t cv cl x2")
           + norm_steps("mean diag0 diag1 y0 y1", 1) + [("cv", g) for g in range(4)]
           + [(w, u) for u in UNITS for w in ("cmax", "csub")]
           + [(w, u) for u in UNITS for w in ("csum", "crec")] + names("x3")
           + norm_steps("mean diag0 diag1 rv rl yv0 yv1 yl0 yl1", 2)
           + [(w, f) for f in range(NF) for w in ("silu", "hid")] + names("x4"))
MOT_POOL = (names("x_in flags mem_in0 mem_in1") + norm_steps("rstd", 0) + names("qc kc")
            + norm_steps("rstd", 1) + names("ckd") + [("cnorm", u) for u in UNITS] + norm_steps("rstd", 2))

CA_PE = (norm_steps("mu sumsq spread", 0) + [("q", u) for u in UNITS] + names("k v0 v1")
         + [("cs", u) for u in UNITS] + [("ct", u) for u in UNITS] + [("cpv", u) for u in UNITS]
         + names("wo") + norm_steps("mu sumsq spread", 1) + [("up", u) for u in UNITS] + names("down"))
CA_ACT = (norm_steps("square y0 y1", 0) + [("q", u) for u in UNITS]
          + [("cexp", u) for u in UNITS] + [("ct", u) for u in UNITS] + [("cpv", u) for u in UNITS]
          + norm_steps("square y0 y1", 1) + [("gelu", u) for u in UNITS] + names("x_out"))
CA_DVE = (norm_steps("center mean diag0 diag1 scaled", 0) + names("k0 k1 v00 v01 v10 v11")
          + [(w, u) for u in UNITS for w in ("cmax", "csub")]
          + [(w, u) for u in UNITS for w in ("csum", "crec")] + names("x2")
          + norm_steps("center mean diag0 diag1 scaled", 1) + names("x3"))
CA_POOL = (names("x_in mem_in0 mem_in1") + norm_steps("rstd", 0)
           + [("cnorm", u) for u in UNITS] + norm_steps("rstd", 1))


def program(nc, x_d, ctx_d, pos_d, type_d, media_d, fuse_w, mot_w, ca_w, const_d, out_d):
    ctx = ExitStack()
    with ctx:
        def sb(name, shape, dt=F32):
            return ctx.enter_context(nc.sbuf_tensor(name, shape, dt))

        def sem(name):
            return ctx.enter_context(nc.semaphore(name))

        x_all = sb("x_all", [P, KT, B * S])
        ctx_t = sb("ctx_t", [P, B * M])
        const = sb("const", [P, C_END])
        ident = const[:, C_ID:C_ID + P]
        ident_bf = sb("ident_bf", [P, P], BF16)
        causal_f = sb("causal_f", [P, P])
        causal = sb("causal", [P, P], BF16)
        ones = sb("ones", [P, P])
        ones_bf = sb("ones_bf", [1, P], BF16)
        mean_w = sb("mean_w", [P, P])
        neg_half = sb("neg_half", [P, TT])
        cos_sin = sb("cos_sin", [P, 2, S])
        is_vis = sb("is_vis", [P, B, S])
        flags = sb("flags", [P, B, 4])
        media = sb("media", [P, B * M])
        media_neg = sb("media_neg", [1, B * M], BF16)
        VECS = ("b_gate", "fuse", "in1", "cross1", "post1", "qg", "qb", "fg", "fb", "in3", "cross3", "post3")
        vec_rows = sb("vec_rows", [KT * len(VECS), P])
        vec_t = sb("vec_t", [P, KT * len(VECS)])
        vec = {n: vec_t[:, KT * i:KT * (i + 1)] for i, n in enumerate(VECS)}
        half_b = sb("half_b", [P, KT])
        ca_gate = sb("ca_gate", [P, 2])
        mem_t = sb("mem_t", [P, KT, B * M])
        w_mem_t = sb("w_mem_t", [P, D])
        w_gate_t = sb("w_gate_t", [P, 2 * KT, D])

        qkv = sb("qkv", [P, 2, KT, 3 * D])
        dense = sb("dense", [P, 2, KT, D])
        cq_w = sb("cq_w", [P, KT, C])
        ckv_w = sb("ckv_w", [P, 2 * C])
        cd_w = sb("cd_w", [P, D])
        gate_w = sb("gate_w", [P, KT, NF * P])
        up_w = sb("up_w", [P, KT, NF * P])
        down_w = sb("down_w", [P, NF, D])
        wq = sb("wq", [P, KT, INNER])
        wkv = sb("wkv", [P, 2 * INNER])
        wo = sb("wo", [P, GT, D])
        w1 = up_w[:, :, 0:FF]
        w2 = down_w[:, 0:GT, :]

        x_rows = [w[:].rearrange("p a n -> p (a n)").rearrange("p (t n) -> p t n", n=D) if len(w.shape) == 3
                  else w[:].rearrange("p (t n) -> p t n", n=D) for w in (wq, wkv)]
        small = wo[:].rearrange("p a n -> p (a n)")
        ctx_rows = small[:, 0:512].rearrange("p (t n) -> p t n", n=C)
        w_mem_rows = small[:, 512:768].rearrange("p (t n) -> p t n", n=C)
        w_gate_rows = small[:, 768:1792].rearrange("p (t n) -> p t n", n=2 * D)
        type_i = gate_w[:].rearrange("p a n -> p (a n)")[:, 0:B * S].bitcast(I32)
        type_one = up_w[:].rearrange("p a n -> p (a n)")[:, 0:B * S].rearrange("p (b n) -> p b n", b=B)
        pos_i = small[:, 1792:2048].bitcast(I32)
        one_hot = qkv[:, 0, 0, 0:2 * S].rearrange("p (t n) -> p t n", t=TT)
        pos_f = qkv[:, 0, 1, 0:S]
        pos_g = qkv[:, 0, 1, S:2 * S]
        media_u8 = sb("media_u8", [P, B * M], U8)

        ARENA = 8704
        arena = [sb(f"arena{s}", [P, ARENA]) for s in range(STREAMS)]

        def cut(at, *shape):
            n = int(np.prod(shape))
            assert at + n <= ARENA
            flat = [a[:, at:at + n] for a in arena]
            if len(shape) == 1:
                return flat
            k = "abcd"[:len(shape)]
            spec = f"p ({' '.join(k)}) -> p {' '.join(k)}"
            return [f.rearrange(spec, **dict(zip(k, shape))) for f in flat]

        xw = cut(0, KT, S)
        sq = cut(512, KT, S)
        yv = cut(1024, KT, S)
        yl = cut(1536, KT, S)
        Z = 2048
        v_pad = cut(Z, TT, NH, 32)
        cv_pad = cut(Z + 1024, 8, 32)
        k_diag = cut(Z, GT, 2, M)
        v_diag = cut(Z + 1024, GT, P)
        zeroed = cut(Z, 2048)
        R = 4096
        stat = cut(8192, 512)
        q_sb, k_sb, ke, ko, kc, kr = (cut(R + 512 * i, KT, S) for i in range(6))
        probs = cut(R + 3072, 2, 384)
        c_q = cut(R, S)
        c_kd = cut(R + 256, NH, M)
        c_t = cut(R + 1280, 8, S)
        c_p = [sq, yv, yl, cut(R + 3328, KT, S)]
        probs_t = [sb(f"probs_t{s}", [P, 2, 384]) for s in range(STREAMS)]
        c_ctx = cut(R, S)
        hid = cut(R, NF, S)
        tanh_b = cut(R + NF * S, 2, S)
        silu_b = cut(R + NF * S + 512, 2, S)
        g_q = cut(R, GT, S)
        g_t = cut(R + 2048, GT, S)
        g_p = [sq, yv, yl, [p[:].rearrange("p a n -> p (a n)")[:, 0:512].rearrange("p (a n) -> p a n", a=2)
                            for p in probs_t]]
        g_h = cut(R, GT, S)
        f_mem = cut(R, D)
        f_p = cut(R + 256, TT, M)
        f_pt = cut(R + 384, S)
        f_mc = cut(R + 640, KT, S)
        f_tanh = cut(R + 1152, KT, S)
        f_u = cut(R + 1664, KT, S)
        ms = [a[:, 0:2] for a in stat]
        rstd = [a[:, 2:4] for a in stat]
        diag = [a[:, 4:260].rearrange("p (t n) -> p t n", t=TT) for a in stat]
        rinv_v = [a[:, 260:292].rearrange("p (t n) -> p t n", t=TT) for a in stat]
        negmax = [a[:, 292:324].rearrange("p (t n) -> p t n", t=TT) for a in stat]
        sums = [a[:, 324:356].rearrange("p (t n) -> p t n", t=TT) for a in stat]
        rvl = [a[:, 356:420].rearrange("p (t n) -> p t n", t=TT) for a in stat]
        fl = [a[:, 420:424] for a in stat]
        cmax = [a[:, 424:456].rearrange("p (u n) -> p u n", u=4) for a in stat]
        csum = [a[:, 456:488].rearrange("p (u n) -> p u n", u=4) for a in stat]
        crec = [sb(f"crec{s}", [P, 4, 8]) for s in range(STREAMS)]
        mem_w = [sb(f"mem_w{s}", [P, 2 * M]) for s in range(STREAMS)]
        rv = [sb(f"rv{s}", [P, S]) for s in range(STREAMS)]
        rl = [sb(f"rl{s}", [P, S]) for s in range(STREAMS)]
        rinv_rows = [sb(f"rinv_rows{s}", [2 * NH, S]) for s in range(STREAMS)]
        ck_sb = [sb(f"ck_sb{s}", [P, M]) for s in range(STREAMS)]

        bank = [[ctx.enter_context(nc.psum_tensor(f"bank{s}_{i}", [P, 512], F32)) for i in range(4)]
                for s in range(STREAMS)]
        all_banks = [b for s in range(STREAMS) for b in bank[s]]

        def two(ap):
            return ap.rearrange("p (a n) -> p a n", a=2)

        const_in, w0_in, pos_in, type_in, media_in, vec_in = (
            sem(n) for n in ("const_in", "w0_in", "pos_in", "type_in", "media_in", "vec_in"))
        x_in = [sem(f"x_in{b}") for b in range(B)]
        mot_in, mot_ff_in, ca_in, ca_ff_in, out_sent = (
            sem(n) for n in ("mot_in", "mot_ff_in", "ca_in", "ca_ff_in", "out_sent"))
        pads_zero = sem("pads_zero")
        pro_pe, pro_act, pro_dve, pro_pool = (sem(n) for n in ("pro_pe", "pro_act", "pro_dve", "pro_pool"))
        done = {e: [sem(f"{e}_done{s}") for s in range(STREAMS)] for e in ("pe", "act", "dve", "pool")}
        sent = [sem(f"sent{s}") for s in range(STREAMS)]

        def load_mot(eng, w, first):
            n = 0
            for e, k in enumerate(("v", "l")):
                eng.dma_start(qkv[:, e], w[k + "_qkv"].rearrange("(k p) n -> p k n", p=P)).then_inc(mot_in, 16)
                eng.dma_start(dense[:, e], w[k + "_dense"].rearrange("(k p) n -> p k n", p=P)).then_inc(mot_in, 16)
            eng.dma_start(cq_w[:], w["cq_w"].rearrange("(k p) n -> p k n", p=P)).then_inc(mot_in, 16)
            eng.dma_start(ckv_w[:], w["ckv_w"]).then_inc(mot_in, 16)
            eng.dma_start(cd_w[:], w["cdense_w"]).then_inc(mot_in, 16)
            load_expert_cols(eng, gate_w, w["v_gate"], w["l_gate"], mot_in)

        def load_expert_cols(eng, dst, v, l, into):
            for e, src in enumerate((v, l)):
                rows = src.rearrange("(k p) n -> p k n", p=P)
                eng.dma_start(dst[:, :, e * FULL * P:(e + 1) * FULL * P], rows[:, :, 0:FULL * P]).then_inc(into, 16)
                at = 2 * FULL * P + e * M
                eng.dma_start(dst[:, :, at:at + TAIL], rows[:, :, FULL * P:INTER]).then_inc(into, 16)

        def load_mot_ff(eng, w):
            load_expert_cols(eng, up_w, w["v_up"], w["l_up"], mot_ff_in)
            for e, src in enumerate((w["v_down"], w["l_down"])):
                eng.dma_start(down_w[:, e * FULL:(e + 1) * FULL, :],
                              src[0:FULL * P, :].rearrange("(f p) n -> p f n", p=P)).then_inc(mot_ff_in, 16)
                eng.dma_start(down_w[e * M:e * M + TAIL, 2 * FULL, :], src[FULL * P:INTER, :]).then_inc(mot_ff_in, 16)

        MOT_DMAS, MOT_FF_DMAS, CA_DMAS, CA_FF_DMAS = 11, 8, 3, 2
        N_VEC = len(VECS) + 2

        PRO = ["w_mem_t", "ctx_t", "gate_t0", "gate_t1", "mem_t0", "mem_t1", "trig", "flags", "vec"] + [f"x{b}" for b in range(B)]
        pro_at = {n: i for i, n in enumerate(PRO)}
        ACT_FIRST = 1
        DVE_FIRST = 14

        def evacuated(name):
            i = pro_at[name]
            return (pro_act, ACT_FIRST + i // 2 + 1) if i % 2 == 0 else (pro_dve, DVE_FIRST + i // 2 + 1)

        PRO_DST = {
            "w_mem_t": lambda b: (w_mem_t[:], b[:, 0:D]),
            "ctx_t": lambda b: (ctx_t[:], b[:]),
            "gate_t0": lambda b: (w_gate_t[:, 0:2, :], two(b[:])),
            "gate_t1": lambda b: (w_gate_t[:, 2:4, :], two(b[:])),
            "mem_t0": lambda b: (mem_t[:, 0, :], b[:]),
            "mem_t1": lambda b: (mem_t[:, 1, :], b[:]),
            "vec": lambda b: (vec_t[:], b[:, 0:KT * len(VECS)]),
            "trig": lambda b: (cos_sin[:], two(b[:])),
            "flags": lambda b: (flags[:, :, 0:2], b[:, 0:16].rearrange("p (b t) -> p b t", t=2)),
            **{f"x{i}": (lambda b, i=i: (x_all[:, :, i * S:(i + 1) * S], two(b[:]))) for i in range(B)},
        }

        with nc.Block() as block:
            @block.sync
            def _(sp):
                sp.dma_start(const[:], const_d).then_inc(const_in, 16)
                sp.dma_start(w_mem_rows, fuse_w["W_mem"].rearrange("(k p) n -> p k n", p=P)).then_inc(w0_in, 16)
                sp.dma_start(ctx_rows, ctx_d.rearrange("b m c -> (b m) c").rearrange("(t p) c -> p t c", p=P)).then_inc(w0_in, 16)
                sp.dma_start(w_gate_rows, fuse_w["W_gate"].rearrange("(k p) n -> p k n", p=P)).then_inc(w0_in, 16)
                for b in range(B):
                    sp.dma_start(x_rows[b // 4][:, 2 * (b % 4):2 * (b % 4) + 2, :],
                                 x_d[b].rearrange("(t p) d -> p t d", p=P)).then_inc(x_in[b], 16)
                sp.wait_ge(pads_zero, 3)
                sp.wait_ge(pro_dve, DVE_FIRST)
                sp.wait_ge(*evacuated("trig"))
                load_mot(sp, mot_w[0], True)
                load_mot_ff(sp, mot_w[0])

            @block.scalar
            def _(act):
                act.dma_start(pos_i, pos_d[0, :].partition_broadcast(P)).then_inc(pos_in, 16)
                act.dma_start(type_i, type_d.rearrange("b n -> (b n)").partition_broadcast(P)).then_inc(type_in, 16)
                act.dma_start(media_u8[:], media_d.rearrange("b m -> (b m)").partition_broadcast(P)).then_inc(media_in, 16)
                for i, n in enumerate(VECS):
                    act.dma_start(vec_rows[KT * i:KT * (i + 1), :], (fuse_w | ca_w)[n].rearrange("(k p) -> k p", p=P))\
                       .then_inc(vec_in, 16)
                for i, n in enumerate(("attn_gate", "ff_gate")):
                    act.dma_start(ca_gate[:, i:i + 1], ca_w[n].partition_broadcast(P)).then_inc(vec_in, 16)
                act.wait_ge(vec_in, 16 * N_VEC)
                act.activation(ca_gate[:], ca_gate[:], ACT.Tanh).then_inc(pro_act, 1)
                for i, n in enumerate(PRO):
                    if i % 2 == 0:
                        act.wait_ge(pro_pe, i + 1)
                        dst, src = PRO_DST[n](all_banks[i % 8])
                        act.copy(dst, src).then_inc(pro_act, 1)
                        if n == "vec":
                            act.wait_ge(*evacuated("vec"))
                            act.mul(half_b[:], vec["b_gate"], 0.5)

            @block.vector
            def _(dve):
                n = 0
                dve.wait_ge(const_in, 16)
                dve.tensor_copy(ident_bf[:], ident).then_inc(pro_dve, 1)
                dve.memset(ones[:], 1.0).then_inc(pro_dve, 1)
                dve.memset(ones_bf[:], 1.0).then_inc(pro_dve, 1)
                dve.memset(mean_w[:], 1.0 / D).then_inc(pro_dve, 1)
                dve.wait_ge(pos_in, 16)
                dve.tensor_scalar(pos_f, pos_i, 0.0, float(S), ALU.is_lt, ALU.mult).then_inc(pro_dve, 1)
                dve.wait_ge(pro_dve, 5)
                dve.tensor_tensor(pos_g, pos_i, pos_f, ALU.add).then_inc(pro_dve, 1)
                dve.wait_ge(pro_dve, 6)
                dve.tensor_scalar(pos_f, pos_g, 0.0, S - 1.0, ALU.max, ALU.min).then_inc(pro_dve, 1)
                dve.wait_ge(pro_dve, 7)
                for t in range(TT):
                    dve.tensor_scalar(one_hot[:, t, :], pos_f, const[:, C_ROW + t:C_ROW + t + 1], None,
                                      ALU.is_equal).then_inc(pro_dve, 1)
                dve.wait_ge(type_in, 16)
                dve.tensor_scalar(type_one.rearrange("p b n -> p (b n)"), type_i, 1.0, None, ALU.is_equal).then_inc(pro_dve, 1)
                dve.memset(is_vis[:, :, S - 1:S], 0.0).then_inc(pro_dve, 1)
                dve.wait_ge(pro_dve, 10)
                dve.tensor_tensor(is_vis[:, :, 0:S - 1], type_one[:, :, 0:S - 1], type_one[:, :, 1:S],
                                  ALU.mult).then_inc(pro_dve, 1)
                dve.wait_ge(media_in, 16)
                dve.tensor_copy(media[:], media_u8[:]).then_inc(pro_dve, 1)
                dve.wait_ge(pro_dve, 13)
                dve.tensor_scalar(media_neg[:], media[0:1, :], -BIG, BIG, ALU.mult, ALU.add).then_inc(pro_dve, 1)
                for i, n in enumerate(PRO):
                    if i % 2 == 1:
                        dve.wait_ge(pro_pe, i + 1)
                        dst, src = PRO_DST[n](all_banks[i % 8])
                        dve.tensor_copy(dst, src).then_inc(pro_dve, 1)
                        if n == "flags":
                            dve.wait_ge(*evacuated("flags"))
                            dve.tensor_scalar(flags[:, :, 2:4], flags[:, :, 0:2], -1.0, 1.0, ALU.mult, ALU.add)

            @block.gpsimd
            def _(pool):
                pool.memset(neg_half[:], -0.5)
                pool.memset(causal_f[:], 0.0).then_inc(pro_pool, 1)
                pool.wait_ge(pro_pool, 1)
                pool.affine_select(out=causal_f[:], in_=causal_f[:], compare_op=ALU.is_ge, fill=BIG, base=0,
                                   pattern=[[-1, P]], channel_multiplier=1).then_inc(pro_pool, 1)
                pool.wait_ge(pro_pool, 2)
                pool.tensor_copy(causal[:], causal_f[:])
                for s in range(STREAMS):
                    pool.memset(zeroed[s], 0.0)
                pool.memset(down_w[:, 2 * FULL, :], 0.0).then_inc(pads_zero, 1)
                pool.wait_ge(pro_dve, 12)
                for w in (gate_w, up_w):
                    tail = w[:, :, 2 * FULL * P:NF * P].rearrange("p k (e n) -> p k e n", e=2)
                    pool.memset(tail[:, :, :, TAIL:M], 0.0).then_inc(pads_zero, 1)

            @block.tensor
            def _(pe):
                pe.wait_ge(const_in, 16)
                pe.wait_ge(w0_in, 48)
                for i, n in enumerate(PRO):
                    b = all_banks[i % 8]
                    if i >= 8:
                        pe.wait_ge(*evacuated(PRO[i - 8]))
                    if n == "w_mem_t":
                        for t in range(KT):
                            last = pe.transpose(b[:, t * P:(t + 1) * P], w_mem_rows[:, t, :], ident)
                    elif n == "ctx_t":
                        for t in range(4):
                            last = pe.transpose(b[:, t * P:(t + 1) * P], ctx_rows[:, t, :], ident)
                    elif n in ("gate_t0", "gate_t1"):
                        for f in range(2):
                            for t in range(KT):
                                src = w_gate_rows[:, t, (2 * (n == "gate_t1") + f) * P:][:, 0:P]
                                last = pe.transpose(b[:, f * D + t * P:f * D + (t + 1) * P], src, ident)
                    elif n in ("mem_t0", "mem_t1"):
                        pe.wait_ge(*evacuated("w_mem_t"))
                        pe.wait_ge(*evacuated("ctx_t"))
                        t = int(n[-1])
                        last = pe.matmul(b[:], w_mem_t[:, t * P:(t + 1) * P], ctx_t[:], start=True, stop=True)
                    elif n == "trig":
                        pe.wait_ge(pro_dve, 9)
                        for f in range(2):
                            for t in range(TT):
                                at = C_TRIG + 256 * t + 128 * f
                                last = pe.matmul(b[:, f * S:(f + 1) * S], const[:, at:at + P], one_hot[:, t, :],
                                                 start=(t == 0), stop=(t == TT - 1))
                    elif n == "flags":
                        pe.wait_ge(pro_dve, 12)
                        for e in range(B):
                            for t in range(TT):
                                last = pe.matmul(b[:, 2 * e + t:2 * e + t + 1], is_vis[0:1, e, t * P:(t + 1) * P],
                                                 ones[0:1, 0:1], start=True, stop=True)
                    elif n == "vec":
                        pe.wait_ge(vec_in, 16 * N_VEC)
                        last = pe.transpose(b[:, 0:KT * len(VECS)], vec_rows[:], ident[0:KT * len(VECS), 0:KT * len(VECS)])
                    else:
                        e = int(n[1:])
                        pe.wait_ge(x_in[e], 16)
                        for k in range(KT):
                            for t in range(TT):
                                last = pe.transpose(b[:, k * S + t * P:k * S + (t + 1) * P],
                                                    x_rows[e // 4][:, 2 * (e % 4) + t, k * P:(k + 1) * P], ident)
                    last.then_inc(pro_pe, 1)

        def clear_and_join():
            sems = [q for e in ("pe", "act", "dve", "pool") for q in done[e]] + sent
            nums = [q.num for q in sems]
            assert nums == list(range(nums[0], nums[0] + len(nums)))
            nc.gpsimd.sem_clear(range(nums[0], nums[-1] + 1))
            nc.all_engine_barrier()

        def tokens(e):
            return bass.ds(e * S, S)

        def layer(pe_steps, act_steps, dve_steps, pool_steps):
            return (Steps(done["pe"], pe_steps), Steps(done["act"], act_steps),
                    Steps(done["dve"], dve_steps), Steps(done["pool"], pool_steps))

        def pe_sumsq(pe, K, s, n, out):
            for t in range(TT):
                for k in range(KT):
                    last = pe.matmul(out[:, t:t + 1], sq[s][:, k, t * P:(t + 1) * P], ones[:, 0:1],
                                     start=(k == 0), stop=(k == KT - 1))
            last.then_inc(*K[0].does(s, "sumsq", n))

        def pe_spread(pe, K, s, n, out):
            pe.wait_ge(*K[2].did(s, "diag1", n))
            for t in range(TT):
                last = pe.matmul(out[:, t * P:(t + 1) * P], ones[:], diag[s][:, t, :], start=True, stop=True)
            last.then_inc(*K[0].does(s, "spread", n))

        def dve_rms(dve, K, s, n, src, eps):
            dve.wait_ge(*K[0].did(s, "sumsq", n))
            dve.tensor_scalar(ms[s], src, 1.0 / D, eps, ALU.mult, ALU.add).then_inc(*K[2].does(s, "mean", n))
            dve.wait_ge(*K[3].did(s, "rstd", n))
            for t in range(TT):
                dve.tensor_scalar(diag[s][:, t, :], ident, rstd[s][:, t:t + 1], None, ALU.mult)\
                   .then_inc(*K[2].does(s, f"diag{t}", n))

        def pool_rstd(pool, K, s, n):
            pool.wait_ge(*K[2].did(s, "mean", n))
            pool.tensor_tensor(rstd[s], ms[s], neg_half[:], ALU.pow).then_inc(*K[3].does(s, "rstd", n))

        def dve_softmax_shift(dve, K, s, u, src, dst):
            dve.wait_ge(*K[0].did(s, "cs", u))
            b = src[:].rearrange("p (h m) -> p h m", m=M)
            dve.tensor_reduce(cmax[s][:, u, :], b, X, ALU.max).then_inc(*K[2].does(s, "cmax", u))
            dve.wait_ge(*K[2].did(s, "cmax", u))
            dve.tensor_tensor(dst.rearrange("p a n -> p (a n)").rearrange("p (h m) -> p h m", m=M), b,
                              cmax[s][:, u, :].unsqueeze(2).to_broadcast([P, 8, M]), ALU.subtract)\
               .then_inc(*K[2].does(s, "csub", u))

        def act_softmax_exp(act, K, s, u, buf, scale):
            act.wait_ge(*K[2].did(s, "csub", u))
            act.activation(buf, buf, ACT.Exp, scale=scale).then_inc(*K[1].does(s, "cexp", u))

        def dve_softmax_sum(dve, K, s, u, buf):
            dve.wait_ge(*K[1].did(s, "cexp", u))
            dve.tensor_reduce(csum[s][:, u, :], buf.rearrange("p a n -> p (a n)").rearrange("p (h m) -> p h m", m=M),
                              X, ALU.add).then_inc(*K[2].does(s, "csum", u))
            dve.wait_ge(*K[2].did(s, "csum", u))
            dve.reciprocal(crec[s][:, u, :], csum[s][:, u, :]).then_inc(*K[2].does(s, "crec", u))

        def pool_softmax_norm(pool, K, s, u, buf):
            pool.wait_ge(*K[2].did(s, "crec", u))
            b = buf.rearrange("p a n -> p (a n)").rearrange("p (h m) -> p h m", m=M)
            pool.tensor_tensor(b, b, crec[s][:, u, :].unsqueeze(2).to_broadcast([P, 8, M]), ALU.mult)\
                .then_inc(*K[3].does(s, "cnorm", u))

        def pe_softmax_t(pe, K, s, u, buf, out):
            pe.wait_ge(*K[3].did(s, "cnorm", u))
            flat = buf.rearrange("p a n -> p (a n)")
            for j in range(4):
                last = pe.transpose(out[:, j * P:(j + 1) * P], flat[:, j * P:(j + 1) * P], ident)
            last.then_inc(*K[0].does(s, "ct", u))

        def act_softmax_t(act, K, s, u, src, dst):
            act.wait_ge(*K[0].did(s, "ct", u))
            t, half = u // 2, u % 2
            act.copy(dst[:, 4 * half:4 * half + 4, t * P:(t + 1) * P], src[:].rearrange("p (j n) -> p j n", j=4))\
               .then_inc(*K[1].does(s, "ct", u))

        with nc.Fori(0, B // STREAMS) as it:
            K = PE_, ACT_, DVE_, POOL_ = layer(FUSE_PE, FUSE_ACT, FUSE_DVE, FUSE_POOL)
            with nc.Block() as block:
                @block.gpsimd
                def _(pool):
                    for s in range(STREAMS):
                        e = it * STREAMS + s
                        pool.tensor_copy(xw[s], x_all[:, :, tokens(e)]).then_inc(*POOL_.does(s, "x_in"))
                        pool.tensor_copy(mem_w[s][:, 0:M], ctx_t[:, bass.ds(e * M, M)]).then_inc(*POOL_.does(s, "mem_in"))
                    for s in range(STREAMS):
                        pool_rstd(pool, K, s, 0)

                @block.tensor
                def _(pe):
                    for s in range(STREAMS):
                        e = it * STREAMS + s
                        b = bank[s]
                        pe.wait_ge(*POOL_.did(s, "mem_in"))
                        pe.matmul(b[0][0:M, 0:D], mem_w[s][:, 0:M], w_mem_t[:], start=True, stop=True)\
                          .then_inc(*PE_.does(s, "mem_rows"))
                        for t in range(TT):
                            for k in range(KT):
                                last = pe.matmul(b[1][:, t * M:(t + 1) * M], xw[s][:, k, t * P:(t + 1) * P],
                                                 mem_t[:, k, bass.ds(e * M, M)], start=(k == 0), stop=(k == KT - 1))
                        last.then_inc(*PE_.does(s, "scores"))
                    for s in range(STREAMS):
                        b = bank[s]
                        pe.wait_ge(*DVE_.did(s, "norm"))
                        for t in range(TT):
                            last = pe.transpose(b[2][0:M, t * P:(t + 1) * P], f_p[s][:, t, :], ident)
                        last.then_inc(*PE_.does(s, "probs_t"))
                    for s in range(STREAMS):
                        b = bank[s]
                        pe.wait_ge(*ACT_.did(s, "probs_t"))
                        for t in range(KT):
                            last = pe.matmul(b[3][:, t * S:(t + 1) * S], f_mem[s][0:M, t * P:(t + 1) * P],
                                             f_pt[s][0:M, :], start=True, stop=True)
                        last.then_inc(*PE_.does(s, "context"))
                    for s in range(STREAMS):
                        b = bank[s]
                        pe.wait_ge(*ACT_.did(s, "context"))
                        for t in range(KT):
                            for k in range(2 * KT):
                                last = pe.matmul(b[0][:, t * S:(t + 1) * S], w_gate_t[:, k, t * P:(t + 1) * P],
                                                 xw[s][:, k, :] if k < KT else f_mc[s][:, k - KT, :],
                                                 start=(k == 0), stop=(k == 2 * KT - 1))
                        last.then_inc(*PE_.does(s, "gate"))
                    for s in range(STREAMS):
                        pe.wait_ge(*ACT_.did(s, "square", 0))
                        pe_sumsq(pe, K, s, 0, bank[s][1])
                    for s in range(STREAMS):
                        pe_spread(pe, K, s, 0, bank[s][2])

                @block.scalar
                def _(act):
                    for s in range(STREAMS):
                        act.wait_ge(*PE_.did(s, "mem_rows"))
                        act.copy(f_mem[s][0:M, :], bank[s][0][0:M, 0:D]).then_inc(*ACT_.does(s, "mem_rows"))
                        act.wait_ge(*DVE_.did(s, "sub"))
                        act.activation(f_p[s], f_p[s], ACT.Exp, scale=D ** -0.5).then_inc(*ACT_.does(s, "exp"))
                    for s in range(STREAMS):
                        act.wait_ge(*PE_.did(s, "probs_t"))
                        act.copy(f_pt[s][0:M, :], bank[s][2][0:M, 0:S]).then_inc(*ACT_.does(s, "probs_t"))
                    for s in range(STREAMS):
                        act.wait_ge(*PE_.did(s, "context"))
                        act.copy(f_mc[s], two(bank[s][3][:])).then_inc(*ACT_.does(s, "context"))
                    for s in range(STREAMS):
                        act.wait_ge(*PE_.did(s, "gate"))
                        for t in range(KT):
                            act.activation(f_tanh[s][:, t, :], bank[s][0][:, t * S:(t + 1) * S], ACT.Tanh,
                                           bias=half_b[:, t:t + 1], scale=0.5).then_inc(*ACT_.does(s, f"gate{t}"))
                    for s in range(STREAMS):
                        act.wait_ge(*DVE_.did(s, "fused"))
                        act.activation(sq[s], xw[s], ACT.Square).then_inc(*ACT_.does(s, "square", 0))
                    for s in range(STREAMS):
                        act.wait_ge(*DVE_.did(s, "y1"))
                        act.copy(x_all[:, :, tokens(it * STREAMS + s)], yv[s]).then_inc(*ACT_.does(s, "x_out"))

                @block.vector
                def _(dve):
                    for s in range(STREAMS):
                        b = bank[s][1][:, 0:TT * M].rearrange("p (t m) -> p t m", t=TT)
                        dve.wait_ge(*PE_.did(s, "scores"))
                        dve.tensor_reduce(cmax[s][:, 0, 0:2], b, X, ALU.max).then_inc(*DVE_.does(s, "max"))
                        dve.wait_ge(*DVE_.did(s, "max"))
                        dve.tensor_tensor(f_p[s], b, cmax[s][:, 0, 0:2].unsqueeze(2).to_broadcast([P, TT, M]),
                                          ALU.subtract).then_inc(*DVE_.does(s, "sub"))
                    for s in range(STREAMS):
                        dve.wait_ge(*ACT_.did(s, "exp"))
                        dve.tensor_reduce(csum[s][:, 0, 0:2], f_p[s], X, ALU.add).then_inc(*DVE_.does(s, "sum"))
                        dve.wait_ge(*DVE_.did(s, "sum"))
                        dve.reciprocal(crec[s][:, 0, 0:2], csum[s][:, 0, 0:2]).then_inc(*DVE_.does(s, "recip"))
                        dve.wait_ge(*DVE_.did(s, "recip"))
                        dve.tensor_tensor(f_p[s], f_p[s], crec[s][:, 0, 0:2].unsqueeze(2).to_broadcast([P, TT, M]),
                                          ALU.mult).then_inc(*DVE_.does(s, "norm"))
                    for s in range(STREAMS):
                        dve.wait_ge(*ACT_.did(s, "gate1"))
                        dve.scalar_tensor_tensor(f_u[s], f_tanh[s], 1.0, f_mc[s], ALU.add, ALU.mult)\
                           .then_inc(*DVE_.does(s, "gated"))
                        dve.wait_ge(*DVE_.did(s, "gated"))
                        dve.scalar_tensor_tensor(xw[s], f_u[s], 0.5, xw[s], ALU.mult, ALU.add)\
                           .then_inc(*DVE_.does(s, "fused"))
                    for s in range(STREAMS):
                        dve_rms(dve, K, s, 0, bank[s][1][:, 0:2], RMS_EPS)
                    for s in range(STREAMS):
                        dve.wait_ge(*PE_.did(s, "spread", 0))
                        for t in range(KT):
                            dve.scalar_tensor_tensor(yv[s][:, t, :], xw[s][:, t, :], vec["fuse"][:, t:t + 1],
                                                     bank[s][2][:, 0:S], ALU.mult, ALU.mult)\
                               .then_inc(*DVE_.does(s, f"y{t}"))
            clear_and_join()

        def mot_layer(which, layer_index, on_sync):
            w_in, w_post, w_cross = (vec[f"{n}{layer_index}"] for n in ("in", "post", "cross"))
            final = which == 1
            pe_names = MOT_PE + (names("out_t") if final else [])
            act_names = MOT_ACT + names("x_out")

            on_sync()
            with nc.Fori(0, B // STREAMS) as it:
                K = PE_, ACT_, DVE_, POOL_ = layer(pe_names, act_names, MOT_DVE, MOT_POOL)
                ss = range(STREAMS)
                with nc.Block() as block:
                    @block.gpsimd
                    def _(pool):
                        for s in ss:
                            e = it * STREAMS + s
                            pool.tensor_copy(xw[s], x_all[:, :, tokens(e)]).then_inc(*POOL_.does(s, "x_in"))
                            pool.tensor_copy(fl[s], flags[:, bass.ds(e, 1), :].rearrange("p a n -> p (a n)"))\
                                .then_inc(*POOL_.does(s, "flags"))
                            for i in range(2):
                                pool.tensor_copy(mem_w[s][:, i * M:(i + 1) * M], ctx_t[:, bass.ds(e * M, M)])\
                                    .then_inc(*POOL_.does(s, f"mem_in{i}"))
                        for s in ss:
                            pool_rstd(pool, K, s, 0)
                        for s in ss:
                            for n, src, dst in (("q", q_sb, ke), ("k", k_sb, kc)):
                                pool.wait_ge(*ACT_.did(s, n))
                                pool.tensor_tensor(dst[s], src[s], cos_sin[:, 0:1, :].to_broadcast([P, KT, S]), ALU.mult)\
                                    .then_inc(*POOL_.does(s, n + "c"))
                        for s in ss:
                            pool_rstd(pool, K, s, 1)
                        for s in ss:
                            pool.wait_ge(*ACT_.did(s, "ck"))
                            pool.tensor_tensor(c_kd[s], ck_sb[s][:].unsqueeze(1).to_broadcast([P, NH, M]),
                                               const[:, C_H16:C_H16 + NH].unsqueeze(2).to_broadcast([P, NH, M]), ALU.mult)\
                                .then_inc(*POOL_.does(s, "ckd"))
                        for u in UNITS:
                            for s in ss:
                                pool_softmax_norm(pool, K, s, u, c_p[u][s])
                        for s in ss:
                            pool_rstd(pool, K, s, 2)

                    @block.tensor
                    def _(pe):
                        def to_experts(out, wv, wl, xv, xl):
                            steps = [(w, y, k) for w, y in ((wv, xv), (wl, xl)) for k in range(KT)]
                            for i, (w, y, k) in enumerate(steps):
                                last = pe.matmul(out, w(k), y(k), start=(i == 0), stop=(i == len(steps) - 1))
                            return last

                        def norm(n, sum_bank, spread_bank):
                            for s in ss:
                                pe.wait_ge(*ACT_.did(s, "square", n))
                                pe_sumsq(pe, K, s, n, bank[s][sum_bank])
                            for s in ss:
                                pe_spread(pe, K, s, n, bank[s][spread_bank])

                        pe.wait_ge(mot_in, 16 * MOT_DMAS * (which + 1))
                        norm(0, 0, 1)
                        for s in ss:
                            b = bank[s]
                            pe.wait_ge(*DVE_.did(s, "yl1", 0))
                            for i, (n, out) in enumerate((("q", b[0]), ("k", b[2]))):
                                for t in range(KT):
                                    at = i * D + t * P
                                    last = to_experts(out[:, t * S:(t + 1) * S],
                                                      lambda k: qkv[:, 0, k, at:at + P], lambda k: qkv[:, 1, k, at:at + P],
                                                      lambda k: yv[s][:, k, :], lambda k: yl[s][:, k, :])
                                last.then_inc(*PE_.does(s, n))
                            for t in range(TT):
                                at = t * P
                                last = to_experts(b[3][:, t * D:(t + 1) * D],
                                                  lambda k: yv[s][:, k, at:at + P], lambda k: yl[s][:, k, at:at + P],
                                                  lambda k: qkv[:, 0, k, 2 * D:3 * D], lambda k: qkv[:, 1, k, 2 * D:3 * D])
                            last.then_inc(*PE_.does(s, "v"))
                        for s in ss:
                            b = bank[s]
                            for n, src, out in (("q", q_sb, b[1]), ("k", k_sb, b[0])):
                                pe.wait_ge(*ACT_.did(s, n))
                                for t in range(KT):
                                    last = pe.matmul(out[:, t * S:(t + 1) * S], const[:, C_ROT:C_ROT + P],
                                                     src[s][:, t, :], start=True, stop=True)
                                last.then_inc(*PE_.does(s, f"rot_{n}"))

                        def scores(s, h):
                            t, r = h // 8, 32 * (h % 8 // 2)
                            out, keys = bank[s][2 + h % 2], (ke, ko)[h % 2][s]
                            if h == 0:
                                pe.wait_ge(*ACT_.did(s, "v1"))
                                pe.wait_ge(*ACT_.did(s, "ko"))
                                pe.wait_ge(*DVE_.did(s, "kr"))
                            if h >= 2:
                                pe.wait_ge(*ACT_.did(s, "exp1", h - 2))
                            for q in range(TT):
                                pe.matmul(out[:, P * q:P + S * q], q_sb[s][r:r + 32, t, q * P:(q + 1) * P],
                                          keys[r:r + 32, t, 0:P * (q + 1)], start=(q == 0), stop=False,
                                          skip_group_check=True)
                            for q in range(TT):
                                last = pe.matmul(out[:, 2 * P * q:P + 2 * P * q], ident_bf[:], causal[:],
                                                 start=False, stop=(q == TT - 1), skip_group_check=True)
                            last.then_inc(*PE_.does(s, "s", h))

                        def transposes(s, h):
                            pe.wait_ge(*ACT_.did(s, "exp1", h))
                            if h >= 1:
                                pe.wait_ge(*DVE_.did(s, "pt", h - 1))
                            for j in range(3):
                                last = pe.transpose(bank[s][1][:, j * P:(j + 1) * P], probs[s][:, h % 2, j * P:(j + 1) * P], ident)
                            last.then_inc(*PE_.does(s, "t", h))

                        def values(s, h):
                            t, r = h // 8, 32 * (h % 8 // 2)
                            pe.wait_ge(*DVE_.did(s, "pt", h))
                            out = bank[s][0][r:r + 32, t * S:(t + 1) * S]
                            pt = probs_t[s][:, h % 2, :]
                            pe.matmul(out, v_pad[s][:, 0, h, :], pt[:, 0:S], start=(h % 2 == 0), stop=False,
                                      skip_group_check=True)
                            pe.matmul(out[:, P:S], v_pad[s][:, 1, h, :], pt[:, S:S + P], start=False, stop=(h % 2 == 1),
                                      skip_group_check=True).then_inc(*PE_.does(s, "pv", h))

                        for h in range(NH + LAG2):
                            for s in ss:
                                if h < NH:
                                    scores(s, h)
                                if 0 <= h - LAG1 < NH:
                                    transposes(s, h - LAG1)
                                if 0 <= h - LAG2 < NH:
                                    values(s, h - LAG2)
                        for s in ss:
                            b = bank[s]
                            pe.wait_ge(*DVE_.did(s, "rvl3"))
                            for t in range(TT):
                                last = pe.transpose(b[1][0:2 * NH, t * P:(t + 1) * P], rvl[s][:, t, :], ident)
                            last.then_inc(*PE_.does(s, "rinv_t"))
                        for s in ss:
                            b = bank[s]
                            pe.wait_ge(*DVE_.did(s, "rinv_t"))
                            for e, n in enumerate(("rinv_v", "rinv_l")):
                                for t in range(KT):
                                    at = C_SPREAD + (e * KT + t) * P
                                    last = pe.matmul(b[2 + e][:, t * S:(t + 1) * S], const[0:2 * NH, at:at + P],
                                                     rinv_rows[s][:], start=True, stop=True)
                                last.then_inc(*PE_.does(s, n))
                        for s in ss:
                            b = bank[s]
                            pe.wait_ge(*DVE_.did(s, "cl"))
                            for t in range(KT):
                                at = t * P
                                last = to_experts(b[1][:, t * S:(t + 1) * S],
                                                  lambda k: dense[:, 0, k, at:at + P], lambda k: dense[:, 1, k, at:at + P],
                                                  lambda k: yv[s][:, k, :], lambda k: yl[s][:, k, :])
                            last.then_inc(*PE_.does(s, "dense"))
                        norm(1, 2, 3)
                        for s in ss:
                            b = bank[s]
                            pe.wait_ge(*DVE_.did(s, "y1", 1))
                            for k in range(KT):
                                last = pe.matmul(b[0][:, 0:S], cq_w[:, k, :], yv[s][:, k, :], start=(k == 0), stop=(k == KT - 1))
                            last.then_inc(*PE_.does(s, "cq"))
                            pe.wait_ge(*POOL_.did(s, "mem_in1"))
                            pe.matmul(b[2][:, 0:M], ckv_w[:, 0:C], mem_w[s][:, 0:M], start=True, stop=True)\
                              .then_inc(*PE_.does(s, "ck"))
                            pe.matmul(b[1][:, 0:C], mem_w[s][:], ckv_w[:, C:2 * C], start=True, stop=True)\
                              .then_inc(*PE_.does(s, "cv"))
                        for u in UNITS:
                            for s in ss:
                                if u == 0:
                                    pe.wait_ge(*ACT_.did(s, "cq"))
                                    pe.wait_ge(*POOL_.did(s, "ckd"))
                                    pe.wait_ge(*DVE_.did(s, "cv", 3))
                                pe.matmul(bank[s][u][:], c_q[s][:, (u // 2) * P:(u // 2 + 1) * P],
                                          c_kd[s][:, 8 * (u % 2):8 * (u % 2) + 8, :], start=True, stop=True)\
                                  .then_inc(*PE_.does(s, "cs", u))
                        for u in UNITS:
                            for s in ss:
                                pe_softmax_t(pe, K, s, u, c_p[u][s], bank[s][u])
                        for s in ss:
                            pe.wait_ge(*ACT_.did(s, "ct", 3))
                            for j in range(8):
                                r = 32 * (j // 2)
                                last = pe.matmul(bank[s][0][r:r + 32, 0:S], cv_pad[s][:, j, :], c_t[s][:, j, :],
                                                 start=(j % 2 == 0), stop=(j % 2 == 1), skip_group_check=True)
                            last.then_inc(*PE_.does(s, "cpv"))
                        for s in ss:
                            pe.wait_ge(*ACT_.did(s, "cctx"))
                            for t in range(KT):
                                last = pe.matmul(bank[s][1][:, t * S:(t + 1) * S], cd_w[:, t * P:(t + 1) * P], c_ctx[s],
                                                 start=True, stop=True)
                            last.then_inc(*PE_.does(s, "cdense"))
                        norm(2, 2, 3)
                        pe.wait_ge(mot_ff_in, 16 * MOT_FF_DMAS * (which + 1))
                        ffb = (0, 1, 2)
                        for f in range(NF):
                            for s in ss:
                                b = bank[s][ffb[f % 3]]
                                if f == 0:
                                    pe.wait_ge(*DVE_.did(s, "yl1", 2))
                                if f >= 3:
                                    pe.wait_ge(*DVE_.did(s, "hid", f - 3))
                                for i, w in enumerate((gate_w, up_w)):
                                    out = b[:, i * S:(i + 1) * S]
                                    if f < NF - 1:
                                        y = yv[s] if f < FULL else yl[s]
                                        for k in range(KT):
                                            last = pe.matmul(out, w[:, k, f * P:(f + 1) * P], y[:, k, :],
                                                             start=(k == 0), stop=(k == KT - 1))
                                    else:
                                        for j, y in enumerate((yv[s], yl[s])):
                                            for k in range(KT):
                                                at = f * P + j * M
                                                last = pe.matmul(out[j * M:(j + 1) * M, :], w[:, k, at:at + M], y[:, k, :],
                                                                 start=(k == 0), stop=(k == KT - 1))
                                last.then_inc(*PE_.does(s, "up", f))
                        for s in ss:
                            for t in range(KT):
                                for f in range(NF):
                                    if t == 0:
                                        pe.wait_ge(*DVE_.did(s, "hid", f))
                                    last = pe.matmul(bank[s][3][:, t * S:(t + 1) * S], down_w[:, f, t * P:(t + 1) * P],
                                                     hid[s][:, f, :], start=(f == 0), stop=(f == NF - 1))
                            last.then_inc(*PE_.does(s, "down"))
                        if final:
                            for s in ss:
                                pe.wait_ge(*DVE_.did(s, "x4"))
                                for t in range(TT):
                                    for k in range(KT):
                                        last = pe.transpose(bank[s][2][:, t * D + k * P:t * D + (k + 1) * P],
                                                            xw[s][:, k, t * P:(t + 1) * P], ident)
                                last.then_inc(*PE_.does(s, "out_t"))

                    @block.scalar
                    def _(act):
                        def square(n, ready):
                            for s in ss:
                                act.wait_ge(*ready(s))
                                act.activation(sq[s], xw[s], ACT.Square).then_inc(*ACT_.does(s, "square", n))

                        square(0, lambda s: POOL_.did(s, "x_in"))
                        for s in ss:
                            b = bank[s]
                            act.wait_ge(*PE_.did(s, "q"))
                            act.copy(q_sb[s], two(b[0][:])).then_inc(*ACT_.does(s, "q"))
                            act.wait_ge(*PE_.did(s, "k"))
                            act.copy(k_sb[s], two(b[2][:])).then_inc(*ACT_.does(s, "k"))
                            act.wait_ge(*PE_.did(s, "v"))
                            v = b[3][:].rearrange("p (t h d) -> p t h d", t=TT, h=NH)
                            for i in range(2):
                                for t in range(TT):
                                    last = act.copy(v_pad[s][:, t, i::2, i * HD:(i + 1) * HD], v[:, t, i::2, :])
                                last.then_inc(*ACT_.does(s, f"v{i}"))
                        for s in ss:
                            act.wait_ge(*DVE_.did(s, "k2"))
                            for n, dst, col in (("ke", ke, C_EVEN), ("ko", ko, C_ODD)):
                                act.activation(dst[s], k_sb[s], ACT.Copy, scale=const[:, col:col + 1])\
                                   .then_inc(*ACT_.does(s, n))
                        for h in range(NH + LAG2):
                            if h >= NH:
                                continue
                            for s in ss:
                                b = bank[s][2 + h % 2]
                                if h >= 2:
                                    act.wait_ge(*PE_.did(s, "t", h - 2))
                                act.wait_ge(*DVE_.did(s, "max1", h))
                                for q, (lo, hi) in enumerate(((0, P), (P, 3 * P))):
                                    act.activation(probs[s][:, h % 2, lo:hi], b[:, lo:hi], ACT.Exp,
                                                   bias=negmax[s][:, q, h:h + 1], accum_out=sums[s][:, q, h:h + 1])\
                                       .then_inc(*ACT_.does(s, f"exp{q}", h))
                        for s in ss:
                            for e, (n, dst) in enumerate((("rinv_v", kc), ("rinv_l", kr))):
                                act.wait_ge(*PE_.did(s, n))
                                act.copy(dst[s], two(bank[s][2 + e][:])).then_inc(*ACT_.does(s, n))
                        square(1, lambda s: DVE_.did(s, "x2"))
                        for s in ss:
                            act.wait_ge(*PE_.did(s, "cq"))
                            act.copy(c_q[s], bank[s][0][:, 0:S]).then_inc(*ACT_.does(s, "cq"))
                            act.wait_ge(*PE_.did(s, "ck"))
                            act.copy(ck_sb[s][:], bank[s][2][:, 0:M]).then_inc(*ACT_.does(s, "ck"))
                        for u in UNITS:
                            for s in ss:
                                act_softmax_exp(act, K, s, u, c_p[u][s], CHD ** -0.5)
                        for u in UNITS:
                            for s in ss:
                                act_softmax_t(act, K, s, u, bank[s][u], c_t[s])
                        for s in ss:
                            act.wait_ge(*PE_.did(s, "cpv"))
                            act.copy(c_ctx[s], bank[s][0][:, 0:S]).then_inc(*ACT_.does(s, "cctx"))
                        square(2, lambda s: DVE_.did(s, "x3"))
                        for f in range(NF):
                            for s in ss:
                                act.wait_ge(*PE_.did(s, "up", f))
                                if f >= 2:
                                    act.wait_ge(*DVE_.did(s, "silu", f - 2))
                                act.activation(tanh_b[s][:, f % 2, :], bank[s][f % 3][:, 0:S], ACT.Tanh, scale=0.5)\
                                   .then_inc(*ACT_.does(s, "tanh", f))
                        for s in ss:
                            if final:
                                act.wait_ge(*PE_.did(s, "out_t"))
                                act.copy(yv[s], two(bank[s][2][:])).then_inc(*ACT_.does(s, "x_out"))
                            else:
                                act.wait_ge(*DVE_.did(s, "x4"))
                                act.copy(x_all[:, :, tokens(it * STREAMS + s)], xw[s]).then_inc(*ACT_.does(s, "x_out"))

                    @block.vector
                    def _(dve):
                        def experts_norm(n, w, src_bank):
                            for s in ss:
                                e = it * STREAMS + s
                                b = bank[s][src_bank][:, 0:S]
                                dve.wait_ge(*PE_.did(s, "spread", n))
                                dve.tensor_tensor(rv[s][:], b, is_vis[:, bass.ds(e, 1), :].rearrange("p a n -> p (a n)"),
                                                  ALU.mult).then_inc(*DVE_.does(s, "rv", n))
                                dve.wait_ge(*DVE_.did(s, "rv", n))
                                dve.tensor_tensor(rl[s][:], b, rv[s][:], ALU.subtract).then_inc(*DVE_.does(s, "rl", n))
                                dve.wait_ge(*DVE_.did(s, "rl", n))
                                for m, dst, r in (("yv", yv, rv), ("yl", yl, rl)):
                                    for t in range(KT):
                                        dve.scalar_tensor_tensor(dst[s][:, t, :], xw[s][:, t, :], w[:, t:t + 1], r[s][:],
                                                                 ALU.mult, ALU.mult).then_inc(*DVE_.does(s, f"{m}{t}", n))

                        for s in ss:
                            dve_rms(dve, K, s, 0, bank[s][0][:, 0:2], RMS_EPS)
                        experts_norm(0, w_in, 1)
                        for s in ss:
                            b = bank[s]
                            sin = cos_sin[:, 1:2, :].to_broadcast([P, KT, S])
                            for n, src, tmp, cosine, dst in (("q", b[1], ko, ke, q_sb), ("k", b[0], kr, kc, k_sb)):
                                dve.wait_ge(*PE_.did(s, f"rot_{n}"))
                                dve.tensor_tensor(tmp[s], two(src[:]), sin, ALU.mult).then_inc(*DVE_.does(s, n + "r"))
                                dve.wait_ge(*POOL_.did(s, n + "c"))
                                dve.wait_ge(*DVE_.did(s, n + "r"))
                                dve.tensor_tensor(dst[s], cosine[s], tmp[s], ALU.add).then_inc(*DVE_.does(s, n + "2"))
                        for h in range(NH + 1):
                            for s in ss:
                                if h < NH:
                                    b = bank[s][2 + h % 2]
                                    dve.wait_ge(*PE_.did(s, "s", h))
                                    for q, (lo, hi) in enumerate(((0, P), (P, 3 * P))):
                                        dve.tensor_reduce(negmax[s][:, q, h:h + 1], b[:, lo:hi], X, ALU.max, negate=True)\
                                           .then_inc(*DVE_.does(s, f"max{q}", h))
                                if h >= 1:
                                    dve.wait_ge(*PE_.did(s, "t", h - 1))
                                    if h >= 3:
                                        dve.wait_ge(*PE_.did(s, "pv", h - 3))
                                    dve.tensor_copy(probs_t[s][:, (h - 1) % 2, :], bank[s][1][:, 0:384])\
                                       .then_inc(*DVE_.does(s, "pt", h - 1))
                        for s in ss:
                            dve.wait_ge(*ACT_.did(s, "exp1", NH - 1))
                            dve.reciprocal(rinv_v[s], sums[s]).then_inc(*DVE_.does(s, "rinv"))
                            dve.wait_ge(*DVE_.did(s, "rinv"))
                            for e in range(2):
                                for t in range(TT):
                                    dve.tensor_scalar(rvl[s][:, t, e * NH:(e + 1) * NH], rinv_v[s][:, t, :],
                                                      fl[s][:, 2 * e + t:2 * e + t + 1], None, ALU.mult)\
                                       .then_inc(*DVE_.does(s, f"rvl{2 * e + t}"))
                            dve.wait_ge(*PE_.did(s, "rinv_t"))
                            dve.tensor_copy(rinv_rows[s][:], bank[s][1][0:2 * NH, 0:S]).then_inc(*DVE_.does(s, "rinv_t"))
                        for s in ss:
                            dve.wait_ge(*PE_.did(s, "pv", NH - 1))
                            for n, src, dst in (("v", kc, yv), ("l", kr, yl)):
                                dve.wait_ge(*ACT_.did(s, f"rinv_{n}"))
                                dve.tensor_tensor(dst[s], two(bank[s][0][:]), src[s], ALU.mult).then_inc(*DVE_.does(s, f"c{n}"))
                        for s in ss:
                            dve.wait_ge(*PE_.did(s, "dense"))
                            dve.tensor_tensor(xw[s], two(bank[s][1][:]), xw[s], ALU.add).then_inc(*DVE_.does(s, "x2"))
                        for s in ss:
                            dve_rms(dve, K, s, 1, bank[s][2][:, 0:2], RMS_EPS)
                        for s in ss:
                            dve.wait_ge(*PE_.did(s, "spread", 1))
                            for t in range(KT):
                                dve.scalar_tensor_tensor(yv[s][:, t, :], xw[s][:, t, :], w_cross[:, t:t + 1],
                                                         bank[s][3][:, 0:S], ALU.mult, ALU.mult)\
                                   .then_inc(*DVE_.does(s, f"y{t}", 1))
                        for s in ss:
                            dve.wait_ge(*PE_.did(s, "cv"))
                            src = bank[s][1][:, 0:C].rearrange("p (g n) -> p g n", g=4)
                            dst = cv_pad[s].rearrange("p (g q) n -> p g q n", g=4)
                            for q in range(2):
                                for i in range(2):
                                    at = q * 2 * CHD + i * CHD
                                    dve.tensor_copy(dst[i * M:(i + 1) * M, :, q, at:at + CHD],
                                                    src[i * M:(i + 1) * M, :, at:at + CHD])\
                                       .then_inc(*DVE_.does(s, "cv", 2 * q + i))
                        for u in UNITS:
                            for s in ss:
                                dve_softmax_shift(dve, K, s, u, bank[s][u], c_p[u][s])
                        for u in UNITS:
                            for s in ss:
                                dve_softmax_sum(dve, K, s, u, c_p[u][s])
                        for s in ss:
                            dve.wait_ge(*PE_.did(s, "cdense"))
                            dve.tensor_tensor(xw[s], two(bank[s][1][:]), xw[s], ALU.add).then_inc(*DVE_.does(s, "x3"))
                        for s in ss:
                            dve_rms(dve, K, s, 2, bank[s][2][:, 0:2], RMS_EPS)
                        experts_norm(2, w_post, 3)
                        for f in range(NF):
                            for s in ss:
                                b = bank[s][f % 3]
                                dve.wait_ge(*ACT_.did(s, "tanh", f))
                                dve.scalar_tensor_tensor(silu_b[s][:, f % 2, :], tanh_b[s][:, f % 2, :], 1.0, b[:, 0:S],
                                                         ALU.add, ALU.mult).then_inc(*DVE_.does(s, "silu", f))
                                dve.wait_ge(*DVE_.did(s, "silu", f))
                                dve.tensor_tensor(hid[s][:, f, :], silu_b[s][:, f % 2, :], b[:, S:2 * S], ALU.mult)\
                                   .then_inc(*DVE_.does(s, "hid", f))
                        for s in ss:
                            dve.wait_ge(*PE_.did(s, "down"))
                            dve.scalar_tensor_tensor(xw[s], two(bank[s][3][:]), 0.5, xw[s], ALU.mult, ALU.add)\
                               .then_inc(*DVE_.does(s, "x4"))

                    if final:
                        @block.sync
                        def _(sp):
                            for s in ss:
                                sp.wait_ge(*ACT_.did(s, "x_out"))
                                sp.dma_start(out_d[bass.ds(it * STREAMS + s, 1)].rearrange("a (t p) d -> p (a t) d", p=P), yv[s])\
                                  .then_inc(sent[s], 16)
                            for s in ss:
                                sp.wait_ge(sent[s], 16)
                clear_and_join()

        def before_first():
            with nc.Block() as block:
                @block.sync
                def _(sp):
                    sp.dma_start(wq[:], ca_w["Wq"].rearrange("(k p) n -> p k n", p=P)).then_inc(ca_in, 16)
                    sp.dma_start(wkv[:], ca_w["Wkv"]).then_inc(ca_in, 16)
                    sp.dma_start(wo[:], ca_w["Wo"].rearrange("(k p) n -> p k n", p=P)).then_inc(ca_in, 16)

        mot_layer(0, 1, before_first)

        with nc.Block() as block:
            @block.sync
            def _(sp):
                sp.dma_start(w1, ca_w["W1"].rearrange("(k p) n -> p k n", p=P)).then_inc(ca_ff_in, 16)
                sp.dma_start(w2, ca_w["W2"].rearrange("(k p) n -> p k n", p=P)).then_inc(ca_ff_in, 16)
                load_mot(sp, mot_w[1], False)

            @block.gpsimd
            def _(pool):
                for s in range(STREAMS):
                    pool.memset(zeroed[s], 0.0)

        with nc.Fori(0, B // STREAMS) as it:
            K = PE_, ACT_, DVE_, POOL_ = layer(CA_PE, CA_ACT, CA_DVE, CA_POOL)
            ss = range(STREAMS)
            with nc.Block() as block:
                @block.gpsimd
                def _(pool):
                    for s in ss:
                        e = it * STREAMS + s
                        pool.tensor_copy(xw[s], x_all[:, :, tokens(e)]).then_inc(*POOL_.does(s, "x_in"))
                        for i in range(2):
                            pool.tensor_copy(mem_w[s][:, i * M:(i + 1) * M], ctx_t[:, bass.ds(e * M, M)])\
                                .then_inc(*POOL_.does(s, f"mem_in{i}"))
                    for s in ss:
                        pool_rstd(pool, K, s, 0)
                    for u in UNITS:
                        for s in ss:
                            pool_softmax_norm(pool, K, s, u, g_p[u][s])
                    for s in ss:
                        pool_rstd(pool, K, s, 1)

                @block.tensor
                def _(pe):
                    def norm(n, ready, banks):
                        for s in ss:
                            pe.wait_ge(*ready(s))
                            for k in range(KT):
                                last = pe.matmul(bank[s][banks[0]][:, 0:S], mean_w[:], xw[s][:, k, :],
                                                 start=(k == 0), stop=(k == KT - 1))
                            last.then_inc(*PE_.does(s, "mu", n))
                        for s in ss:
                            pe.wait_ge(*ACT_.did(s, "square", n))
                            pe_sumsq(pe, K, s, n, bank[s][banks[1]])
                        for s in ss:
                            pe_spread(pe, K, s, n, bank[s][banks[2]])

                    norm(0, lambda s: POOL_.did(s, "x_in"), (0, 1, 2))
                    pe.wait_ge(ca_in, 16 * CA_DMAS)
                    for s in ss:
                        b = bank[s]
                        pe.wait_ge(*ACT_.did(s, "y1", 0))
                        for u in UNITS:
                            for j in range(2):
                                for k in range(KT):
                                    at = (2 * u + j) * P
                                    last = pe.matmul(b[(3 + u) % 4][:, j * S:(j + 1) * S], wq[:, k, at:at + P],
                                                     yv[s][:, k, :], start=(k == 0), stop=(k == KT - 1))
                            last.then_inc(*PE_.does(s, "q", u))
                        pe.wait_ge(*POOL_.did(s, "mem_in1"))
                        pe.wait_ge(*ACT_.did(s, "q", 0))
                        for j in range(GT):
                            last = pe.matmul(b[3][:, j * M:(j + 1) * M], wkv[:, j * P:(j + 1) * P], mem_w[s][:, 0:M],
                                             start=True, stop=True)
                        last.then_inc(*PE_.does(s, "k"))
                        for c in range(2):
                            pe.wait_ge(*ACT_.did(s, "q", 1 + c))
                            pe.matmul(b[c][:], mem_w[s][:], wkv[:, INNER + c * 512:INNER + (c + 1) * 512],
                                      start=True, stop=True).then_inc(*PE_.does(s, f"v{c}"))
                    for u in UNITS:
                        for s in ss:
                            e = it * STREAMS + s
                            out = bank[s][(2 + u) % 4]
                            if u == 0:
                                pe.wait_ge(*ACT_.did(s, "q", 3))
                                pe.wait_ge(*DVE_.did(s, "v11"))
                            t, half = u // 2, u % 2
                            for j in range(4):
                                pe.matmul(out[:, j * P:(j + 1) * P], g_q[s][:, 4 * half + j, t * P:(t + 1) * P],
                                          k_diag[s][:, 4 * half + j], start=(j == 0), stop=False, skip_group_check=True)
                            pe.matmul(out[:], ones_bf[:], media_neg[:, bass.ds(e * M, M)].unsqueeze(1).to_broadcast([1, 8, M]),
                                      start=False, stop=True, skip_group_check=True).then_inc(*PE_.does(s, "cs", u))
                    for u in UNITS:
                        for s in ss:
                            pe_softmax_t(pe, K, s, u, g_p[u][s], bank[s][(2 + u) % 4])
                    for s in ss:
                        for u in UNITS:
                            out = bank[s][(2 + u) % 4]
                            pe.wait_ge(*ACT_.did(s, "ct", 3))
                            for j in range(2):
                                last = pe.matmul(out[:, j * S:(j + 1) * S], v_diag[s][:, 2 * u + j, :], g_t[s][:, 2 * u + j, :],
                                                 start=True, stop=True)
                            last.then_inc(*PE_.does(s, "cpv", u))
                    for s in ss:
                        pe.wait_ge(*ACT_.did(s, "cpv", 3))
                        for t in range(KT):
                            for k in range(GT):
                                last = pe.matmul(bank[s][0][:, t * S:(t + 1) * S], wo[:, k, t * P:(t + 1) * P], g_q[s][:, k, :],
                                                 start=(k == 0), stop=(k == GT - 1))
                        last.then_inc(*PE_.does(s, "wo"))
                    norm(1, lambda s: DVE_.did(s, "x2"), (1, 2, 3))
                    pe.wait_ge(ca_ff_in, 16 * CA_FF_DMAS)
                    for s in ss:
                        pe.wait_ge(*ACT_.did(s, "y1", 1))
                        for u in UNITS:
                            for j in range(2):
                                for k in range(KT):
                                    at = (2 * u + j) * P
                                    last = pe.matmul(bank[s][u][:, j * S:(j + 1) * S], w1[:, k, at:at + P], yv[s][:, k, :],
                                                     start=(k == 0), stop=(k == KT - 1))
                            last.then_inc(*PE_.does(s, "up", u))
                    for s in ss:
                        pe.wait_ge(*ACT_.did(s, "gelu", 3))
                        for t in range(KT):
                            for k in range(GT):
                                last = pe.matmul(bank[s][0][:, t * S:(t + 1) * S], w2[:, k, t * P:(t + 1) * P], g_h[s][:, k, :],
                                                 start=(k == 0), stop=(k == GT - 1))
                        last.then_inc(*PE_.does(s, "down"))

                @block.scalar
                def _(act):
                    def norm(n, g, bias):
                        for s in ss:
                            act.wait_ge(*DVE_.did(s, "center", n))
                            act.activation(sq[s], yl[s], ACT.Square).then_inc(*ACT_.does(s, "square", n))
                        for s in ss:
                            act.wait_ge(*DVE_.did(s, "scaled", n))
                            for t in range(KT):
                                act.activation(yv[s][:, t, :], yl[s][:, t, :], ACT.Identity, bias=vec[bias][:, t:t + 1],
                                               scale=vec[g][:, t:t + 1]).then_inc(*ACT_.does(s, f"y{t}", n))

                    norm(0, "qg", "qb")
                    for s in ss:
                        for u in UNITS:
                            act.wait_ge(*PE_.did(s, "q", u))
                            act.copy(g_q[s][:, 2 * u:2 * u + 2, :], two(bank[s][(3 + u) % 4][:])).then_inc(*ACT_.does(s, "q", u))
                    for u in UNITS:
                        for s in ss:
                            act_softmax_exp(act, K, s, u, g_p[u][s], GHD ** -0.5)
                    for u in UNITS:
                        for s in ss:
                            act_softmax_t(act, K, s, u, bank[s][(2 + u) % 4], g_t[s])
                    for s in ss:
                        for u in UNITS:
                            act.wait_ge(*PE_.did(s, "cpv", u))
                            act.copy(g_q[s][:, 2 * u:2 * u + 2, :], two(bank[s][(2 + u) % 4][:])).then_inc(*ACT_.does(s, "cpv", u))
                    norm(1, "fg", "fb")
                    for s in ss:
                        for u in UNITS:
                            act.wait_ge(*PE_.did(s, "up", u))
                            act.activation(g_h[s][:, 2 * u:2 * u + 2, :], two(bank[s][u][:]), ACT.Gelu)\
                               .then_inc(*ACT_.does(s, "gelu", u))
                    for s in ss:
                        act.wait_ge(*DVE_.did(s, "x3"))
                        act.copy(x_all[:, :, tokens(it * STREAMS + s)], xw[s]).then_inc(*ACT_.does(s, "x_out"))

                @block.vector
                def _(dve):
                    def norm(n, banks):
                        for s in ss:
                            dve.wait_ge(*PE_.did(s, "mu", n))
                            dve.tensor_tensor(yl[s], xw[s], bank[s][banks[0]][:, 0:S].unsqueeze(1).to_broadcast([P, KT, S]),
                                              ALU.subtract).then_inc(*DVE_.does(s, "center", n))
                        for s in ss:
                            dve_rms(dve, K, s, n, bank[s][banks[1]][:, 0:2], LN_EPS)
                        for s in ss:
                            dve.wait_ge(*PE_.did(s, "spread", n))
                            dve.tensor_tensor(yl[s], yl[s], bank[s][banks[2]][:, 0:S].unsqueeze(1).to_broadcast([P, KT, S]),
                                              ALU.mult).then_inc(*DVE_.does(s, "scaled", n))

                    norm(0, (0, 1, 2))
                    for s in ss:
                        e = it * STREAMS + s
                        b = bank[s]
                        dve.wait_ge(*PE_.did(s, "k"))
                        for i in range(2):
                            r = slice(i * M, (i + 1) * M)
                            dve.tensor_tensor(k_diag[s][r, :, i, :], b[3][r, :].rearrange("p (j m) -> p j m", j=GT),
                                              media[r, bass.ds(e * M, M)].unsqueeze(1).to_broadcast([M, GT, M]), ALU.mult)\
                               .then_inc(*DVE_.does(s, f"k{i}"))
                        for c in range(2):
                            dve.wait_ge(*PE_.did(s, f"v{c}"))
                            for i in range(2):
                                r = slice(i * M, (i + 1) * M)
                                dve.tensor_copy(v_diag[s][r, 4 * c:4 * c + 4, i * GHD:(i + 1) * GHD],
                                                b[c][r, :].rearrange("p (j i d) -> p j i d", i=2, d=GHD)[:, :, i, :])\
                                   .then_inc(*DVE_.does(s, f"v{c}{i}"))
                    for u in UNITS:
                        for s in ss:
                            dve_softmax_shift(dve, K, s, u, bank[s][(2 + u) % 4], g_p[u][s])
                    for u in UNITS:
                        for s in ss:
                            dve_softmax_sum(dve, K, s, u, g_p[u][s])
                    for s in ss:
                        dve.wait_ge(*PE_.did(s, "wo"))
                        dve.scalar_tensor_tensor(xw[s], two(bank[s][0][:]), ca_gate[:, 0:1], xw[s], ALU.mult, ALU.add)\
                           .then_inc(*DVE_.does(s, "x2"))
                    norm(1, (1, 2, 3))
                    for s in ss:
                        dve.wait_ge(*PE_.did(s, "down"))
                        dve.scalar_tensor_tensor(xw[s], two(bank[s][0][:]), ca_gate[:, 1:2], xw[s], ALU.mult, ALU.add)\
                           .then_inc(*DVE_.does(s, "x3"))
            clear_and_join()

        def before_second():
            with nc.Block() as block:
                @block.gpsimd
                def _(pool):
                    for s in range(STREAMS):
                        pool.memset(zeroed[s], 0.0)
                    pool.memset(down_w[:, 2 * FULL, :], 0.0).then_inc(pads_zero, 1)
                    tail = up_w[:, :, 2 * FULL * P:NF * P].rearrange("p k (e n) -> p k e n", e=2)
                    pool.memset(tail[:, :, :, TAIL:M], 0.0)

                @block.sync
                def _(sp):
                    sp.wait_ge(pads_zero, 4)
                    load_mot_ff(sp, mot_w[1])

        mot_layer(1, 3, before_second)


MOT = ("v_qkv", "l_qkv", "v_dense", "l_dense", "cq_w", "ckv_w", "cdense_w", "v_gate", "v_up", "v_down",
       "l_gate", "l_up", "l_down")
VEC = {"b_gate": "L0_xattn_b_gate", "fuse": "L0_xattn_norm_w", "qg": "L2_xattn_ln_q_g", "qb": "L2_xattn_ln_q_b",
       "fg": "L2_xattn_ln_ff_g", "fb": "L2_xattn_ln_ff_b",
       "in1": "L1_xattn_ln_in_w", "post1": "L1_xattn_ln_post_attn_w", "cross1": "L1_xattn_ln_post_cross_w",
       "in3": "L3_xattn_ln_in_w", "post3": "L3_xattn_ln_post_attn_w", "cross3": "L3_xattn_ln_post_cross_w"}


def kernel(**inputs):
    import concourse.bacc as bacc
    from concourse.bass_utils import run_bass_kernel_spmd

    nc = bacc.Bacc("TRN2", target_bir_lowering=False, num_devices=1)
    arrays, ap = {}, {}
    for name, value in inputs.items():
        a = np.ascontiguousarray(value)
        arrays["in_" + name] = a
        ap[name] = nc.dram_tensor("in_" + name, a.shape, mybir.dt.from_np(a.dtype), kind="ExternalInput").ap()
    table = nc.inline_tensor(constants(), name="table_of_constants").ap()
    out = nc.dram_tensor("out_x", (B, S, D), F32, kind="ExternalOutput").ap()
    program(nc, ap["x"], ap["ctx_1024"], ap["pos_1xS"], ap["mask_BxS_ik0"], ap["mask_BxS2_bk0"],
            {"W_mem": ap["L0_xattn_W_mem"], "W_gate": ap["L0_xattn_W_gate"], **{n: ap[k] for n, k in VEC.items()}},
            [{n: ap[f"L{i}_xattn_{n}"] for n in MOT} for i in (1, 3)],
            {n: ap["L2_xattn_" + n] for n in ("Wq", "Wkv", "Wo", "attn_gate", "W1", "W2", "ff_gate")},
            table, out)
    return run_bass_kernel_spmd(nc, [arrays], core_ids=[0]).results[0]["out_x"]
```

```python
from contextlib import ExitStack

import numpy as np

import concourse.bass as bass
from concourse import mybir

F32 = mybir.dt.float32
BF16 = mybir.dt.bfloat16
I32 = mybir.dt.int32
U8 = mybir.dt.uint8
ALU = mybir.AluOpType
ACT = mybir.ActivationFunctionType
X = mybir.AxisListType.X

P = 128
B, S, D = 8, 256, 256
M, C = 64, 128
KT = D // P
TT = S // P
NH = 16
HD = D // NH
CHD = C // NH
GHD = 64
INNER = NH * GHD
INTER = 688
FULL = INTER // P
TAIL = INTER - FULL * P
FF_ORDER = [f for i in range(FULL) for f in (FULL + i, i)] + [2 * FULL]
NF = 2 * FULL + 1
FF = 4 * D
GT = INNER // P
RMS_EPS, LN_EPS = 1e-6, 1e-5
BIG = -1e30
STREAMS = 2
LATE = S - S // 4

C_ID, C_ROT, C_H8, C_H16, C_ROW, C_TRIG, C_PAIR, C_EPS = 0, 128, 256, 264, 280, 282, 794, 858
C_END = C_EPS + 4


def constants():
    t = np.zeros((P, C_END), np.float32)
    p = np.arange(P)
    t[p, C_ID + p] = 1.0
    for m in range(P):
        i = m % HD
        k = m + HD // 2 if i < HD // 2 else m - HD // 2
        t[k, C_ROT + m] = -1.0 if i < HD // 2 else 1.0
    t[p, C_H8 + p // HD] = HD ** -0.5
    t[p, C_H16 + p // CHD] = 1.0
    t[:, C_ROW], t[:, C_ROW + 1] = p, p + P
    inv = (1.0 / 10000.0 ** (np.arange(0, HD, 2, dtype=np.float32) / np.float32(HD))).astype(np.float32)
    ang = np.outer(np.arange(S, dtype=np.float32), inv).astype(np.float32)
    for tt in range(TT):
        a = ang[tt * P:(tt + 1) * P][:, (p % HD) % (HD // 2)]
        t[:, C_TRIG + 256 * tt:C_TRIG + 256 * tt + 128] = np.cos(a)
        t[:, C_TRIG + 256 * tt + 128:C_TRIG + 256 * tt + 256] = np.sin(a)
    for i, eps in enumerate((RMS_EPS, LN_EPS)):
        t[:, C_EPS + TT * i:C_EPS + TT * (i + 1)] = eps * D / P
    for i in range(2):
        for h in range(2):
            at = C_PAIR + 32 * i + i * 2 * CHD + h * CHD
            t[h * M:(h + 1) * M, at:at + CHD] = 1.0
    return t


class Steps:

    def __init__(self, sems, names):
        self.sems, self.names = sems, list(names)
        self.value = {n: i + 1 for i, n in enumerate(self.names)}
        self.issued = [0, 0]

    def does(self, s, *name):
        assert self.names[self.issued[s]] == name, (name, self.names[self.issued[s]])
        self.issued[s] += 1
        return self.sems[s], 1

    def did(self, s, *name):
        return self.sems[s], self.value[name]

    def last(self, s):
        return self.sems[s], len(self.names)


def names(text):
    return [(w,) for w in text.split()]



UNITS = range(4)
LAG1, LAG2 = 1, 2


def attention_steps(first, *rest):
    out = []
    for h in range(NH + len(rest)):
        for lag, w in enumerate((first, *rest)):
            if 0 <= h - lag < NH:
                out += [(n, h - lag) for n in w.split()]
    return out


def norm_steps(kind, n):
    return [(w, n) for w in kind.split()]


FUSE_PE = names("mem_rows scores probs_t context gate") + norm_steps("sumsq spread", 0)
FUSE_ACT = names("mem_rows exp probs_t context gate0 gate1") + norm_steps("square", 0) + names("x_out")
FUSE_DVE = names("max sub sum recip norm gated fused") + norm_steps("mean", 0) + names("y0 y1")
FUSE_POOL = names("x_in mem_in") + norm_steps("rstd", 0)

MOT_PE = (norm_steps("sumsq spread", 0) + names("q k v rot_q rot_k") + attention_steps("s", "t", "pv")
          + names("rinv dense") + norm_steps("sumsq spread", 1) + names("cq ck cv")
          + [("cs", u) for u in UNITS] + [("ct", u) for u in UNITS] + names("cpv cdense")
          + norm_steps("sumsq spread", 2) + [("up", f) for f in range(NF)] + names("down"))
MOT_ACT = (norm_steps("square", 0) + names("q k v0 v1") + attention_steps("exp0 exp1")
           + names("rinv") + norm_steps("square", 1) + names("cq ck")
           + [("cexp", u) for u in UNITS] + [("ct", u) for u in UNITS]
           + norm_steps("square", 2) + [("tanh", f) for f in range(NF)])
MOT_DVE = (names("x_in") + norm_steps("mean rv rl yl0 yl1 yv0 yv1", 0) + names("qr q2 kr k2")
           + attention_steps("max0 max1", "pt") + names("rinv ctx cv cl x2")
           + norm_steps("mean y0 y1", 1) + [("cv", g) for g in range(4)]
           + [(w, u) for u in UNITS for w in ("cmax", "csub")]
           + names("crec cctx x3") + norm_steps("mean rv rl yl0 yl1 yv0 yv1", 2)
           + [(w, f) for f in range(NF) for w in ("silu", "hid")] + names("x4"))
MOT_POOL = (names("mem_in0 mem_in1") + norm_steps("rstd", 0) + names("qc kc") + [("qm", h) for h in range(NH)]
            + norm_steps("rstd", 1) + names("ckd") + norm_steps("rstd", 2))

CA_PE = (norm_steps("mu sumsq spread", 0) + [("q", u) for u in UNITS] + names("k v0 v1")
         + [("cs", u) for u in UNITS] + [("ct", u) for u in UNITS] + [("cpv", u) for u in UNITS]
         + names("wo") + norm_steps("mu sumsq spread", 1) + [("up", u) for u in UNITS] + names("down"))
CA_ACT = (norm_steps("square y0 y1", 0) + [("q", u) for u in UNITS]
          + [("cexp", u) for u in UNITS] + [("ct", u) for u in UNITS] + [("cpv", u) for u in UNITS]
          + norm_steps("square y0 y1", 1) + [("gelu", u) for u in UNITS] + names("x_out"))
CA_DVE = (norm_steps("center mean scaled", 0) + names("k0 k1 v00 v01 v10 v11")
          + [(w, u) for u in UNITS for w in ("cmax", "csub")]
          + [(w, u) for u in UNITS for w in ("csum", "crec")] + names("x2")
          + norm_steps("center mean scaled", 1) + names("x3"))
CA_POOL = (names("x_in mem_in0 mem_in1") + norm_steps("rstd", 0)
           + [("cnorm", u) for u in UNITS] + norm_steps("rstd", 1))


def program(nc, x_d, ctx_d, pos_d, type_d, media_d, fuse_w, mot_w, ca_w, const_d, out_d):
    ctx = ExitStack()
    with ctx:
        def sb(name, shape, dt=F32):
            return ctx.enter_context(nc.sbuf_tensor(name, shape, dt))

        def sem(name):
            return ctx.enter_context(nc.semaphore(name))

        x_all = sb("x_all", [P, KT, B * S])
        ctx_t = sb("ctx_t", [P, B * M])
        const = sb("const", [P, C_END])
        ident = const[:, C_ID:C_ID + P]
        ident_bf = sb("ident_bf", [P, P], BF16)
        causal_f = sb("causal_f", [P, P])
        causal = sb("causal", [P, P], BF16)
        ones = sb("ones", [P, P])
        ones_bf = sb("ones_bf", [1, P], BF16)
        mean_w = sb("mean_w", [P, P])
        neg_half = sb("neg_half", [P, TT])
        cos_sin = sb("cos_sin", [P, 2, S])
        is_vis = sb("is_vis", [P, B, S])
        early = sb("early", [1, B], I32)
        media = sb("media", [P, B * M])
        media_neg = sb("media_neg", [1, B * M], BF16)
        VECS = ("b_gate", "fuse", "in1", "cross1", "post1", "qg", "qb", "fg", "fb", "in3", "cross3", "post3")
        vec_rows = sb("vec_rows", [KT * len(VECS), P])
        vec_t = sb("vec_t", [P, KT * len(VECS)])
        vec = {n: vec_t[:, KT * i:KT * (i + 1)] for i, n in enumerate(VECS)}
        half_b = sb("half_b", [P, KT])
        ca_gate = sb("ca_gate", [P, 2])
        mem_t = sb("mem_t", [P, KT, B * M])
        w_mem_t = sb("w_mem_t", [P, D])
        w_gate_t = sb("w_gate_t", [P, 2 * KT, D])

        qkv = sb("qkv", [P, 2, KT, 3 * D])
        dense = sb("dense", [P, 2, KT, D])
        cq_w = sb("cq_w", [P, KT, C])
        ckv_w = sb("ckv_w", [P, 2 * C])
        cd_w = sb("cd_w", [P, D])
        gate_w = sb("gate_w", [P, KT, NF * P])
        up_w = sb("up_w", [P, KT, NF * P])
        down_w = sb("down_w", [P, NF, D])
        wq = sb("wq", [P, KT, INNER])
        wkv = sb("wkv", [P, 2 * INNER])
        wo = sb("wo", [P, GT, D])
        w1 = up_w[:, :, 0:FF]
        w2 = down_w[:, 0:GT, :]

        x_rows = [w[:].rearrange("p a n -> p (a n)").rearrange("p (t n) -> p t n", n=D) if len(w.shape) == 3
                  else w[:].rearrange("p (t n) -> p t n", n=D) for w in (wq, wkv)]
        small = wo[:].rearrange("p a n -> p (a n)")
        ctx_rows = small[:, 0:512].rearrange("p (t n) -> p t n", n=C)
        w_mem_rows = small[:, 512:768].rearrange("p (t n) -> p t n", n=C)
        w_gate_rows = small[:, 768:1792].rearrange("p (t n) -> p t n", n=2 * D)
        type_i = gate_w[:].rearrange("p a n -> p (a n)")[:, 0:B * S].bitcast(I32)
        type_one = up_w[:].rearrange("p a n -> p (a n)")[:, 0:B * S].rearrange("p (b n) -> p b n", b=B)
        pos_i = small[:, 1792:2048].bitcast(I32)
        one_hot = qkv[:, 0, 0, 0:2 * S].rearrange("p (t n) -> p t n", t=TT)
        pos_f = qkv[:, 0, 1, 0:S]
        pos_g = qkv[:, 0, 1, S:2 * S]
        media_u8 = sb("media_u8", [P, B * M], U8)

        ARENA = 8704
        arena = [sb(f"arena{s}", [P, ARENA]) for s in range(STREAMS)]

        def cut(at, *shape):
            n = int(np.prod(shape))
            assert at + n <= ARENA
            flat = [a[:, at:at + n] for a in arena]
            if len(shape) == 1:
                return flat
            k = "abcd"[:len(shape)]
            spec = f"p ({' '.join(k)}) -> p {' '.join(k)}"
            return [f.rearrange(spec, **dict(zip(k, shape))) for f in flat]

        xw = cut(0, KT, S)
        sq = cut(512, KT, S)
        yv = cut(1024, KT, S)
        yl = cut(1536, KT, S)
        Z = 2048
        v_pad = cut(Z, TT, NH, 32)
        cv_pad = cut(Z + 1024, 8, 32)
        k_diag = cut(Z, GT, 2, M)
        v_diag = cut(Z + 1024, GT, P)
        zeroed = cut(Z, 2048)
        R = 4096
        stat = cut(8192, 512)
        q_sb, k_sb, qc, qr, kc, kr = (cut(R + 512 * i, KT, S) for i in range(6))
        QM = 4
        q_one = cut(R + 1024, QM, S)
        probs = cut(R + 3072, 2, 384)
        c_q = cut(R, S)
        c_kd = cut(R + 256, NH, M)
        c_t = cut(R + 1280, 8, S)
        c_p = [sq, yv, yl, cut(R + 3328, KT, S)]
        probs_t = [sb(f"probs_t{s}", [P, 2, 384]) for s in range(STREAMS)]
        c_ctx = cut(R, S)
        hid = cut(R, NF, S)
        tanh_b = cut(R + NF * S, 2, S)
        silu_b = cut(R + NF * S + 512, 2, S)
        g_q = cut(R, GT, S)
        g_t = cut(R + 2048, GT, S)
        g_p = [sq, yv, yl, [p[:].rearrange("p a n -> p (a n)")[:, 0:512].rearrange("p (a n) -> p a n", a=2)
                            for p in probs_t]]
        g_h = cut(R, GT, S)
        f_mem = cut(R, D)
        f_p = cut(R + 256, TT, M)
        f_pt = cut(R + 384, S)
        f_mc = cut(R + 640, KT, S)
        f_tanh = cut(R + 1152, KT, S)
        f_u = cut(R + 1664, KT, S)
        ms = [a[:, 0:2] for a in stat]
        rstd = [a[:, 2:4] for a in stat]
        negmax = [a[:, 292:324].rearrange("p (t n) -> p t n", t=TT) for a in stat]
        sums = [a[:, 324:356].rearrange("p (t n) -> p t n", t=TT) for a in stat]
        cmax = [a[:, 424:456].rearrange("p (u n) -> p u n", u=4) for a in stat]
        csum = [a[:, 456:488].rearrange("p (u n) -> p u n", u=4) for a in stat]
        crec = [sb(f"crec{s}", [P, 4, 8]) for s in range(STREAMS)]
        mem_w = [sb(f"mem_w{s}", [P, 2 * M]) for s in range(STREAMS)]
        rv = [sb(f"rv{s}", [P, S]) for s in range(STREAMS)]
        rl = [sb(f"rl{s}", [P, S]) for s in range(STREAMS)]
        ck_sb = [sb(f"ck_sb{s}", [P, M]) for s in range(STREAMS)]

        bank = [[ctx.enter_context(nc.psum_tensor(f"bank{s}_{i}", [P, 512], F32)) for i in range(4)]
                for s in range(STREAMS)]
        all_banks = [b for s in range(STREAMS) for b in bank[s]]

        def two(ap):
            return ap.rearrange("p (a n) -> p a n", a=2)

        const_in, w0_in, pos_in, type_in, media_in, vec_in = (
            sem(n) for n in ("const_in", "w0_in", "pos_in", "type_in", "media_in", "vec_in"))
        x_in = [sem(f"x_in{b}") for b in range(B)]
        mot_in, mot_ff_in, ca_in, ca_ff_in, out_sent = (
            sem(n) for n in ("mot_in", "mot_ff_in", "ca_in", "ca_ff_in", "out_sent"))
        pads_zero = sem("pads_zero")
        pro_pe, pro_act, pro_dve, pro_pool = (sem(n) for n in ("pro_pe", "pro_act", "pro_dve", "pro_pool"))
        done = {e: [sem(f"{e}_done{s}") for s in range(STREAMS)] for e in ("pe", "act", "dve", "pool")}
        sent = [sem(f"sent{s}") for s in range(STREAMS)]

        def load_mot(eng, w, first):
            n = 0
            for e, k in enumerate(("v", "l")):
                eng.dma_start(qkv[:, e], w[k + "_qkv"].rearrange("(k p) n -> p k n", p=P)).then_inc(mot_in, 16)
                eng.dma_start(dense[:, e], w[k + "_dense"].rearrange("(k p) n -> p k n", p=P)).then_inc(mot_in, 16)
            eng.dma_start(cq_w[:], w["cq_w"].rearrange("(k p) n -> p k n", p=P)).then_inc(mot_in, 16)
            eng.dma_start(ckv_w[:], w["ckv_w"]).then_inc(mot_in, 16)
            eng.dma_start(cd_w[:], w["cdense_w"]).then_inc(mot_in, 16)
            load_expert_cols(eng, gate_w, w["v_gate"], w["l_gate"], mot_in)

        def load_expert_cols(eng, dst, v, l, into):
            for e, src in enumerate((v, l)):
                rows = src.rearrange("(k p) n -> p k n", p=P)
                eng.dma_start(dst[:, :, e * FULL * P:(e + 1) * FULL * P], rows[:, :, 0:FULL * P]).then_inc(into, 16)
                at = 2 * FULL * P + e * M
                eng.dma_start(dst[:, :, at:at + TAIL], rows[:, :, FULL * P:INTER]).then_inc(into, 16)

        def load_mot_ff(eng, w):
            load_expert_cols(eng, up_w, w["v_up"], w["l_up"], mot_ff_in)
            for e, src in enumerate((w["v_down"], w["l_down"])):
                eng.dma_start(down_w[:, e * FULL:(e + 1) * FULL, :],
                              src[0:FULL * P, :].rearrange("(f p) n -> p f n", p=P)).then_inc(mot_ff_in, 16)
                eng.dma_start(down_w[e * M:e * M + TAIL, 2 * FULL, :], src[FULL * P:INTER, :]).then_inc(mot_ff_in, 16)

        MOT_DMAS, MOT_FF_DMAS, CA_DMAS, CA_FF_DMAS = 11, 8, 3, 2
        N_VEC = len(VECS) + 2

        PRO = ["w_mem_t", "ctx_t", "gate_t0", "gate_t1", "mem_t0", "mem_t1", "vec", "trig"] + [f"x{b}" for b in range(B)]
        pro_at = {n: i for i, n in enumerate(PRO)}
        ACT_FIRST = 1
        DVE_FIRST = 15

        def evacuated(name):
            i = pro_at[name]
            return (pro_act, ACT_FIRST + i // 2 + 1) if i % 2 == 0 else (pro_dve, DVE_FIRST + i // 2 + 1)

        PRO_DST = {
            "w_mem_t": lambda b: (w_mem_t[:], b[:, 0:D]),
            "ctx_t": lambda b: (ctx_t[:], b[:]),
            "gate_t0": lambda b: (w_gate_t[:, 0:2, :], two(b[:])),
            "gate_t1": lambda b: (w_gate_t[:, 2:4, :], two(b[:])),
            "mem_t0": lambda b: (mem_t[:, 0, :], b[:]),
            "mem_t1": lambda b: (mem_t[:, 1, :], b[:]),
            "vec": lambda b: (vec_t[:], b[:, 0:KT * len(VECS)]),
            "trig": lambda b: (cos_sin[:], two(b[:])),
            **{f"x{i}": (lambda b, i=i: (x_all[:, :, i * S:(i + 1) * S], two(b[:]))) for i in range(B)},
        }

        with nc.Block() as block:
            @block.sync
            def _(sp):
                sp.dma_start(const[:], const_d).then_inc(const_in, 16)
                sp.dma_start(w_mem_rows, fuse_w["W_mem"].rearrange("(k p) n -> p k n", p=P)).then_inc(w0_in, 16)
                sp.dma_start(ctx_rows, ctx_d.rearrange("b m c -> (b m) c").rearrange("(t p) c -> p t c", p=P)).then_inc(w0_in, 16)
                sp.dma_start(w_gate_rows, fuse_w["W_gate"].rearrange("(k p) n -> p k n", p=P)).then_inc(w0_in, 16)
                for b in range(B):
                    sp.dma_start(x_rows[b // 4][:, 2 * (b % 4):2 * (b % 4) + 2, :],
                                 x_d[b].rearrange("(t p) d -> p t d", p=P)).then_inc(x_in[b], 16)
                sp.wait_ge(pads_zero, 3)
                sp.wait_ge(pro_dve, DVE_FIRST)
                sp.wait_ge(*evacuated("trig"))
                load_mot(sp, mot_w[0], True)
                load_mot_ff(sp, mot_w[0])

            @block.scalar
            def _(act):
                act.dma_start(pos_i, pos_d[0, :].partition_broadcast(P)).then_inc(pos_in, 16)
                act.dma_start(type_i, type_d.rearrange("b n -> (b n)").partition_broadcast(P)).then_inc(type_in, 16)
                act.dma_start(media_u8[:], media_d.rearrange("b m -> (b m)").partition_broadcast(P)).then_inc(media_in, 16)
                for i, n in enumerate(VECS):
                    act.dma_start(vec_rows[KT * i:KT * (i + 1), :], (fuse_w | ca_w)[n].rearrange("(k p) -> k p", p=P))\
                       .then_inc(vec_in, 16)
                for i, n in enumerate(("attn_gate", "ff_gate")):
                    act.dma_start(ca_gate[:, i:i + 1], ca_w[n].partition_broadcast(P)).then_inc(vec_in, 16)
                act.wait_ge(vec_in, 16 * N_VEC)
                act.activation(ca_gate[:], ca_gate[:], ACT.Tanh).then_inc(pro_act, 1)
                for i, n in enumerate(PRO):
                    if i % 2 == 0:
                        act.wait_ge(pro_pe, i + 1)
                        dst, src = PRO_DST[n](all_banks[i % 8])
                        act.copy(dst, src).then_inc(pro_act, 1)
                        if n == "vec":
                            act.wait_ge(*evacuated("vec"))
                            act.mul(half_b[:], vec["b_gate"], 0.5)

            @block.vector
            def _(dve):
                n = 0
                dve.wait_ge(const_in, 16)
                dve.tensor_copy(ident_bf[:], ident).then_inc(pro_dve, 1)
                dve.memset(ones[:], 1.0).then_inc(pro_dve, 1)
                dve.memset(ones_bf[:], 1.0).then_inc(pro_dve, 1)
                dve.memset(mean_w[:], 1.0 / D).then_inc(pro_dve, 1)
                dve.wait_ge(pos_in, 16)
                dve.tensor_scalar(pos_f, pos_i, 0.0, float(S), ALU.is_lt, ALU.mult).then_inc(pro_dve, 1)
                dve.wait_ge(pro_dve, 5)
                dve.tensor_tensor(pos_g, pos_i, pos_f, ALU.add).then_inc(pro_dve, 1)
                dve.wait_ge(pro_dve, 6)
                dve.tensor_scalar(pos_f, pos_g, 0.0, S - 1.0, ALU.max, ALU.min).then_inc(pro_dve, 1)
                dve.wait_ge(pro_dve, 7)
                for t in range(TT):
                    dve.tensor_scalar(one_hot[:, t, :], pos_f, const[:, C_ROW + t:C_ROW + t + 1], None,
                                      ALU.is_equal).then_inc(pro_dve, 1)
                dve.wait_ge(type_in, 16)
                dve.tensor_scalar(type_one.rearrange("p b n -> p (b n)"), type_i, 1.0, None, ALU.is_equal).then_inc(pro_dve, 1)
                dve.memset(is_vis[:, :, S - 1:S], 0.0).then_inc(pro_dve, 1)
                dve.wait_ge(pro_dve, 10)
                dve.tensor_tensor(is_vis[:, :, 0:S - 1], type_one[:, :, 0:S - 1], type_one[:, :, 1:S],
                                  ALU.mult).then_inc(pro_dve, 1)
                dve.wait_ge(media_in, 16)
                dve.tensor_copy(media[:], media_u8[:]).then_inc(pro_dve, 1)
                dve.wait_ge(pro_dve, 13)
                dve.tensor_scalar(media_neg[:], media[0:1, :], -BIG, BIG, ALU.mult, ALU.add).then_inc(pro_dve, 1)
                dve.tensor_reduce(early[:], is_vis[0:1, :, 0:LATE], X, ALU.max).then_inc(pro_dve, 1)
                for i, n in enumerate(PRO):
                    if i % 2 == 1:
                        dve.wait_ge(pro_pe, i + 1)
                        dst, src = PRO_DST[n](all_banks[i % 8])
                        dve.tensor_copy(dst, src).then_inc(pro_dve, 1)

            @block.gpsimd
            def _(pool):
                pool.memset(neg_half[:], -0.5)
                pool.memset(causal_f[:], 0.0).then_inc(pro_pool, 1)
                pool.wait_ge(pro_pool, 1)
                pool.affine_select(out=causal_f[:], in_=causal_f[:], compare_op=ALU.is_ge, fill=BIG, base=0,
                                   pattern=[[-1, P]], channel_multiplier=1).then_inc(pro_pool, 1)
                pool.wait_ge(pro_pool, 2)
                pool.tensor_copy(causal[:], causal_f[:])
                for s in range(STREAMS):
                    pool.memset(zeroed[s], 0.0)
                pool.memset(down_w[:, 2 * FULL, :], 0.0).then_inc(pads_zero, 1)
                pool.wait_ge(pro_dve, 12)
                for w in (gate_w, up_w):
                    tail = w[:, :, 2 * FULL * P:NF * P].rearrange("p k (e n) -> p k e n", e=2)
                    pool.memset(tail[:, :, :, TAIL:M], 0.0).then_inc(pads_zero, 1)

            @block.tensor
            def _(pe):
                pe.wait_ge(const_in, 16)
                pe.wait_ge(w0_in, 48)
                for i, n in enumerate(PRO):
                    b = all_banks[i % 8]
                    if i >= 8:
                        pe.wait_ge(*evacuated(PRO[i - 8]))
                    if n == "w_mem_t":
                        for t in range(KT):
                            last = pe.transpose(b[:, t * P:(t + 1) * P], w_mem_rows[:, t, :], ident)
                    elif n == "ctx_t":
                        for t in range(4):
                            last = pe.transpose(b[:, t * P:(t + 1) * P], ctx_rows[:, t, :], ident)
                    elif n in ("gate_t0", "gate_t1"):
                        for f in range(2):
                            for t in range(KT):
                                src = w_gate_rows[:, t, (2 * (n == "gate_t1") + f) * P:][:, 0:P]
                                last = pe.transpose(b[:, f * D + t * P:f * D + (t + 1) * P], src, ident)
                    elif n in ("mem_t0", "mem_t1"):
                        pe.wait_ge(*evacuated("w_mem_t"))
                        pe.wait_ge(*evacuated("ctx_t"))
                        t = int(n[-1])
                        last = pe.matmul(b[:], w_mem_t[:, t * P:(t + 1) * P], ctx_t[:], start=True, stop=True)
                    elif n == "trig":
                        pe.wait_ge(pro_dve, 9)
                        for f in range(2):
                            for t in range(TT):
                                at = C_TRIG + 256 * t + 128 * f
                                last = pe.matmul(b[:, f * S:(f + 1) * S], const[:, at:at + P], one_hot[:, t, :],
                                                 start=(t == 0), stop=(t == TT - 1))
                    elif n == "vec":
                        pe.wait_ge(vec_in, 16 * N_VEC)
                        last = pe.transpose(b[:, 0:KT * len(VECS)], vec_rows[:], ident[0:KT * len(VECS), 0:KT * len(VECS)])
                    else:
                        e = int(n[1:])
                        pe.wait_ge(x_in[e], 16)
                        for k in range(KT):
                            for t in range(TT):
                                last = pe.transpose(b[:, k * S + t * P:k * S + (t + 1) * P],
                                                    x_rows[e // 4][:, 2 * (e % 4) + t, k * P:(k + 1) * P], ident)
                    last.then_inc(pro_pe, 1)

        def clear_and_join():
            sems = [q for e in ("pe", "act", "dve", "pool") for q in done[e]] + sent
            nums = [q.num for q in sems]
            assert nums == list(range(nums[0], nums[0] + len(nums)))
            nc.gpsimd.sem_clear(range(nums[0], nums[-1] + 1))
            nc.all_engine_barrier()

        def tokens(e):
            return bass.ds(e * S, S)

        def layer(pe_steps, act_steps, dve_steps, pool_steps):
            return (Steps(done["pe"], pe_steps), Steps(done["act"], act_steps),
                    Steps(done["dve"], dve_steps), Steps(done["pool"], pool_steps))

        def pe_sumsq(pe, K, s, n, out, eps=C_EPS):
            pe.matmul(out[:, 0:TT], mean_w[:], const[:, eps:eps + TT], start=True, stop=False, skip_group_check=True)
            for t in range(TT):
                for k in range(KT):
                    last = pe.matmul(out[:, t:t + 1], sq[s][:, k, t * P:(t + 1) * P], mean_w[:, 0:1],
                                     start=False, stop=(k == KT - 1), skip_group_check=True)
            last.then_inc(*K[0].does(s, "sumsq", n))

        def pe_spread(pe, K, s, n, out):
            pe.wait_ge(*K[3].did(s, "rstd", n))
            for t in range(TT):
                last = pe.transpose(out[:, t * P:(t + 1) * P], rstd[s][:, t:t + 1].to_broadcast([P, P]), ident)
            last.then_inc(*K[0].does(s, "spread", n))

        def dve_mean(dve, K, s, n, src):
            dve.wait_ge(*K[0].did(s, "sumsq", n))
            dve.tensor_copy(ms[s], src[:, 0:TT]).then_inc(*K[2].does(s, "mean", n))

        def pool_rstd(pool, K, s, n):
            pool.wait_ge(*K[2].did(s, "mean", n))
            pool.tensor_tensor(rstd[s], ms[s], neg_half[:], ALU.pow).then_inc(*K[3].does(s, "rstd", n))

        def dve_softmax_shift(dve, K, s, u, src, dst):
            dve.wait_ge(*K[0].did(s, "cs", u))
            b = src[:].rearrange("p (h m) -> p h m", m=M)
            dve.tensor_reduce(cmax[s][:, u, :], b, X, ALU.max).then_inc(*K[2].does(s, "cmax", u))
            dve.wait_ge(*K[2].did(s, "cmax", u))
            dve.tensor_tensor(dst.rearrange("p a n -> p (a n)").rearrange("p (h m) -> p h m", m=M), b,
                              cmax[s][:, u, :].unsqueeze(2).to_broadcast([P, 8, M]), ALU.subtract)\
               .then_inc(*K[2].does(s, "csub", u))

        def act_softmax_exp(act, K, s, u, buf, scale):
            act.wait_ge(*K[2].did(s, "csub", u))
            act.activation(buf, buf, ACT.Exp, scale=scale).then_inc(*K[1].does(s, "cexp", u))

        def dve_softmax_sum(dve, K, s, u, buf):
            dve.wait_ge(*K[1].did(s, "cexp", u))
            dve.tensor_reduce(csum[s][:, u, :], buf.rearrange("p a n -> p (a n)").rearrange("p (h m) -> p h m", m=M),
                              X, ALU.add).then_inc(*K[2].does(s, "csum", u))
            dve.wait_ge(*K[2].did(s, "csum", u))
            dve.reciprocal(crec[s][:, u, :], csum[s][:, u, :]).then_inc(*K[2].does(s, "crec", u))

        def pool_softmax_norm(pool, K, s, u, buf):
            pool.wait_ge(*K[2].did(s, "crec", u))
            b = buf.rearrange("p a n -> p (a n)").rearrange("p (h m) -> p h m", m=M)
            pool.tensor_tensor(b, b, crec[s][:, u, :].unsqueeze(2).to_broadcast([P, 8, M]), ALU.mult)\
                .then_inc(*K[3].does(s, "cnorm", u))

        def pe_softmax_t(pe, K, s, u, buf, out, ready):
            pe.wait_ge(*ready)
            flat = buf.rearrange("p a n -> p (a n)")
            for j in range(4):
                last = pe.transpose(out[:, j * P:(j + 1) * P], flat[:, j * P:(j + 1) * P], ident)
            last.then_inc(*K[0].does(s, "ct", u))

        def act_softmax_t(act, K, s, u, src, dst):
            act.wait_ge(*K[0].did(s, "ct", u))
            t, half = u // 2, u % 2
            act.copy(dst[:, 4 * half:4 * half + 4, t * P:(t + 1) * P], src[:].rearrange("p (j n) -> p j n", j=4))\
               .then_inc(*K[1].does(s, "ct", u))

        with nc.Fori(0, B // STREAMS) as it:
            K = PE_, ACT_, DVE_, POOL_ = layer(FUSE_PE, FUSE_ACT, FUSE_DVE, FUSE_POOL)
            with nc.Block() as block:
                @block.gpsimd
                def _(pool):
                    for s in range(STREAMS):
                        e = it * STREAMS + s
                        pool.tensor_copy(xw[s], x_all[:, :, tokens(e)]).then_inc(*POOL_.does(s, "x_in"))
                        pool.tensor_copy(mem_w[s][:, 0:M], ctx_t[:, bass.ds(e * M, M)]).then_inc(*POOL_.does(s, "mem_in"))
                    for s in range(STREAMS):
                        pool_rstd(pool, K, s, 0)

                @block.tensor
                def _(pe):
                    for s in range(STREAMS):
                        e = it * STREAMS + s
                        b = bank[s]
                        pe.wait_ge(*POOL_.did(s, "mem_in"))
                        pe.matmul(b[0][0:M, 0:D], mem_w[s][:, 0:M], w_mem_t[:], start=True, stop=True)\
                          .then_inc(*PE_.does(s, "mem_rows"))
                        for t in range(TT):
                            for k in range(KT):
                                last = pe.matmul(b[1][:, t * M:(t + 1) * M], xw[s][:, k, t * P:(t + 1) * P],
                                                 mem_t[:, k, bass.ds(e * M, M)], start=(k == 0), stop=(k == KT - 1))
                        last.then_inc(*PE_.does(s, "scores"))
                    for s in range(STREAMS):
                        b = bank[s]
                        pe.wait_ge(*DVE_.did(s, "norm"))
                        for t in range(TT):
                            last = pe.transpose(b[2][0:M, t * P:(t + 1) * P], f_p[s][:, t, :], ident)
                        last.then_inc(*PE_.does(s, "probs_t"))
                    for s in range(STREAMS):
                        b = bank[s]
                        pe.wait_ge(*ACT_.did(s, "probs_t"))
                        for t in range(KT):
                            last = pe.matmul(b[3][:, t * S:(t + 1) * S], f_mem[s][0:M, t * P:(t + 1) * P],
                                             f_pt[s][0:M, :], start=True, stop=True)
                        last.then_inc(*PE_.does(s, "context"))
                    for s in range(STREAMS):
                        b = bank[s]
                        pe.wait_ge(*ACT_.did(s, "context"))
                        for t in range(KT):
                            for k in range(2 * KT):
                                last = pe.matmul(b[0][:, t * S:(t + 1) * S], w_gate_t[:, k, t * P:(t + 1) * P],
                                                 xw[s][:, k, :] if k < KT else f_mc[s][:, k - KT, :],
                                                 start=(k == 0), stop=(k == 2 * KT - 1))
                        last.then_inc(*PE_.does(s, "gate"))
                    for s in range(STREAMS):
                        pe.wait_ge(*ACT_.did(s, "square", 0))
                        pe_sumsq(pe, K, s, 0, bank[s][1])
                    for s in range(STREAMS):
                        pe_spread(pe, K, s, 0, bank[s][2])

                @block.scalar
                def _(act):
                    for s in range(STREAMS):
                        act.wait_ge(*PE_.did(s, "mem_rows"))
                        act.copy(f_mem[s][0:M, :], bank[s][0][0:M, 0:D]).then_inc(*ACT_.does(s, "mem_rows"))
                        act.wait_ge(*DVE_.did(s, "sub"))
                        act.activation(f_p[s], f_p[s], ACT.Exp, scale=D ** -0.5).then_inc(*ACT_.does(s, "exp"))
                    for s in range(STREAMS):
                        act.wait_ge(*PE_.did(s, "probs_t"))
                        act.copy(f_pt[s][0:M, :], bank[s][2][0:M, 0:S]).then_inc(*ACT_.does(s, "probs_t"))
                    for s in range(STREAMS):
                        act.wait_ge(*PE_.did(s, "context"))
                        act.copy(f_mc[s], two(bank[s][3][:])).then_inc(*ACT_.does(s, "context"))
                    for s in range(STREAMS):
                        act.wait_ge(*PE_.did(s, "gate"))
                        for t in range(KT):
                            act.activation(f_tanh[s][:, t, :], bank[s][0][:, t * S:(t + 1) * S], ACT.Tanh,
                                           bias=half_b[:, t:t + 1], scale=0.5).then_inc(*ACT_.does(s, f"gate{t}"))
                    for s in range(STREAMS):
                        act.wait_ge(*DVE_.did(s, "fused"))
                        act.activation(sq[s], xw[s], ACT.Square).then_inc(*ACT_.does(s, "square", 0))
                    for s in range(STREAMS):
                        act.wait_ge(*DVE_.did(s, "y1"))
                        act.copy(x_all[:, :, tokens(it * STREAMS + s)], yv[s]).then_inc(*ACT_.does(s, "x_out"))

                @block.vector
                def _(dve):
                    for s in range(STREAMS):
                        b = bank[s][1][:, 0:TT * M].rearrange("p (t m) -> p t m", t=TT)
                        dve.wait_ge(*PE_.did(s, "scores"))
                        dve.tensor_reduce(cmax[s][:, 0, 0:2], b, X, ALU.max).then_inc(*DVE_.does(s, "max"))
                        dve.wait_ge(*DVE_.did(s, "max"))
                        dve.tensor_tensor(f_p[s], b, cmax[s][:, 0, 0:2].unsqueeze(2).to_broadcast([P, TT, M]),
                                          ALU.subtract).then_inc(*DVE_.does(s, "sub"))
                    for s in range(STREAMS):
                        dve.wait_ge(*ACT_.did(s, "exp"))
                        dve.tensor_reduce(csum[s][:, 0, 0:2], f_p[s], X, ALU.add).then_inc(*DVE_.does(s, "sum"))
                        dve.wait_ge(*DVE_.did(s, "sum"))
                        dve.reciprocal(crec[s][:, 0, 0:2], csum[s][:, 0, 0:2]).then_inc(*DVE_.does(s, "recip"))
                        dve.wait_ge(*DVE_.did(s, "recip"))
                        dve.tensor_tensor(f_p[s], f_p[s], crec[s][:, 0, 0:2].unsqueeze(2).to_broadcast([P, TT, M]),
                                          ALU.mult).then_inc(*DVE_.does(s, "norm"))
                    for s in range(STREAMS):
                        dve.wait_ge(*ACT_.did(s, "gate1"))
                        dve.scalar_tensor_tensor(f_u[s], f_tanh[s], 1.0, f_mc[s], ALU.add, ALU.mult)\
                           .then_inc(*DVE_.does(s, "gated"))
                        dve.wait_ge(*DVE_.did(s, "gated"))
                        dve.scalar_tensor_tensor(xw[s], f_u[s], 0.5, xw[s], ALU.mult, ALU.add)\
                           .then_inc(*DVE_.does(s, "fused"))
                    for s in range(STREAMS):
                        dve_mean(dve, K, s, 0, bank[s][1])
                    for s in range(STREAMS):
                        dve.wait_ge(*PE_.did(s, "spread", 0))
                        for t in range(KT):
                            dve.scalar_tensor_tensor(yv[s][:, t, :], xw[s][:, t, :], vec["fuse"][:, t:t + 1],
                                                     bank[s][2][:, 0:S], ALU.mult, ALU.mult)\
                               .then_inc(*DVE_.does(s, f"y{t}"))
            clear_and_join()

        def mot_layer(which, layer_index, on_sync):
            w_in, w_post, w_cross = (vec[f"{n}{layer_index}"] for n in ("in", "post", "cross"))
            final = which == 1
            pe_names = MOT_PE + (names("out_t") if final else [])
            act_names = MOT_ACT + names("x_out")

            on_sync()
            with nc.Fori(0, B // STREAMS) as it:
                K = PE_, ACT_, DVE_, POOL_ = layer(pe_names, act_names, MOT_DVE, MOT_POOL)
                ss = range(STREAMS)
                with nc.Block() as block:
                    @block.gpsimd
                    def _(pool):
                        for s in ss:
                            e = it * STREAMS + s
                            for i in range(2):
                                pool.tensor_copy(mem_w[s][:, i * M:(i + 1) * M], ctx_t[:, bass.ds(e * M, M)])\
                                    .then_inc(*POOL_.does(s, f"mem_in{i}"))
                        for s in ss:
                            pool_rstd(pool, K, s, 0)
                        for s in ss:
                            for n, src, dst in (("q", q_sb, qc), ("k", k_sb, kc)):
                                pool.wait_ge(*ACT_.did(s, n))
                                pool.tensor_tensor(dst[s], src[s], cos_sin[:, 0:1, :].to_broadcast([P, KT, S]), ALU.mult)\
                                    .then_inc(*POOL_.does(s, n + "c"))
                        for h in range(NH):
                            for s in ss:
                                if h == 0:
                                    pool.wait_ge(*DVE_.did(s, "q2"))
                                if h >= QM:
                                    pool.wait_ge(*PE_.did(s, "s", h - QM))
                                pool.tensor_scalar(q_one[s][:, h % QM, :], q_sb[s][:, h // 8, :],
                                                   const[:, C_H8 + h % 8:C_H8 + h % 8 + 1], None, ALU.mult)\
                                    .then_inc(*POOL_.does(s, "qm", h))
                        for s in ss:
                            pool_rstd(pool, K, s, 1)
                        for s in ss:
                            pool.wait_ge(*ACT_.did(s, "ck"))
                            pool.tensor_tensor(c_kd[s], ck_sb[s][:].unsqueeze(1).to_broadcast([P, NH, M]),
                                               const[:, C_H16:C_H16 + NH].unsqueeze(2).to_broadcast([P, NH, M]), ALU.mult)\
                                .then_inc(*POOL_.does(s, "ckd"))
                        for s in ss:
                            pool_rstd(pool, K, s, 2)

                    @block.tensor
                    def _(pe):
                        has_early = [pe.value_load(early[0:1, bass.ds(it * STREAMS + s, 1)]) for s in ss]

                        def if_early(s):
                            return pe.If(has_early[s])

                        def to_experts(s, outs, w, at, v_ready):
                            for t in range(KT):
                                for k in range(KT):
                                    pe.matmul(outs[t], w[:, 1, k, at + t * P:at + (t + 1) * P], yl[s][:, k, :],
                                              start=(t == k == 0), stop=False, skip_group_check=True)
                            pe.wait_ge(*v_ready)
                            with if_early(s):
                                for t in range(KT):
                                    for k in range(KT):
                                        pe.matmul(outs[t][:, 0:LATE], w[:, 0, k, at + t * P:at + (t + 1) * P],
                                                  yv[s][:, k, 0:LATE], start=False, stop=False, skip_group_check=True)
                            for t in range(KT):
                                for k in range(KT):
                                    last = pe.matmul(outs[t][:, LATE:S], w[:, 0, k, at + t * P:at + (t + 1) * P],
                                                     yv[s][:, k, LATE:S], start=False, stop=(k == KT - 1),
                                                     skip_group_check=True)
                            return last

                        def norm(n, sum_bank, spread_bank):
                            for s in ss:
                                pe.wait_ge(*ACT_.did(s, "square", n))
                                pe_sumsq(pe, K, s, n, bank[s][sum_bank])
                            for s in ss:
                                pe_spread(pe, K, s, n, bank[s][spread_bank])

                        pe.wait_ge(mot_in, 16 * MOT_DMAS * (which + 1))
                        norm(0, 0, 1)
                        for s in ss:
                            b = bank[s]
                            pe.wait_ge(*DVE_.did(s, "yl1", 0))
                            for i, (n, out) in enumerate((("q", b[0]), ("k", b[2]))):
                                to_experts(s, [out[:, t * S:(t + 1) * S] for t in range(KT)], qkv, i * D, DVE_.did(s, "yv1", 0))\
                                    .then_inc(*PE_.does(s, n))

                            def value_rows(y, e, t, start, stop):
                                for k in range(KT):
                                    last = pe.matmul(b[3][:, t * D:(t + 1) * D], y[s][:, k, t * P:(t + 1) * P],
                                                     qkv[:, e, k, 2 * D:3 * D], start=(start and k == 0),
                                                     stop=(stop and k == KT - 1), skip_group_check=True)
                                return last

                            value_rows(yl, 1, 0, True, False)
                            with if_early(s):
                                value_rows(yv, 0, 0, False, False)
                            value_rows(yl, 1, 1, True, False)
                            value_rows(yv, 0, 1, False, True).then_inc(*PE_.does(s, "v"))
                        for s in ss:
                            b = bank[s]
                            for n, src, out in (("q", q_sb, b[1]), ("k", k_sb, b[0])):
                                pe.wait_ge(*ACT_.did(s, n))
                                for t in range(KT):
                                    last = pe.matmul(out[:, t * S:(t + 1) * S], const[:, C_ROT:C_ROT + P],
                                                     src[s][:, t, :], start=True, stop=True)
                                last.then_inc(*PE_.does(s, f"rot_{n}"))

                        def scores(s, h):
                            out = bank[s][2 + h % 2]
                            if h == 0:
                                pe.wait_ge(*ACT_.did(s, "v1"))
                                pe.wait_ge(*DVE_.did(s, "k2"))
                            pe.wait_ge(*POOL_.did(s, "qm", h))
                            if h >= 2:
                                pe.wait_ge(*ACT_.did(s, "exp1", h - 2))
                            for q in range(TT):
                                pe.matmul(out[:, P * q:P + S * q], q_one[s][:, h % QM, q * P:(q + 1) * P],
                                          k_sb[s][:, h // 8, 0:P * (q + 1)], start=(q == 0), stop=False,
                                          skip_group_check=True)
                            for q in range(TT):
                                last = pe.matmul(out[:, 2 * P * q:P + 2 * P * q], ident_bf[:], causal[:],
                                                 start=False, stop=(q == TT - 1), skip_group_check=True)
                            last.then_inc(*PE_.does(s, "s", h))

                        def transposes(s, h):
                            pe.wait_ge(*ACT_.did(s, "exp1", h))
                            if h >= 1:
                                pe.wait_ge(*DVE_.did(s, "pt", h - 1))
                            for j in range(3):
                                last = pe.transpose(bank[s][1][:, j * P:(j + 1) * P], probs[s][:, h % 2, j * P:(j + 1) * P], ident)
                            last.then_inc(*PE_.does(s, "t", h))

                        def values(s, h):
                            t, r = h // 8, 32 * (h % 8 // 2)
                            pe.wait_ge(*DVE_.did(s, "pt", h))
                            out = bank[s][0][r:r + 32, t * S:(t + 1) * S]
                            pt = probs_t[s][:, h % 2, :]
                            pe.matmul(out, v_pad[s][:, 0, h, :], pt[:, 0:S], start=(h % 2 == 0), stop=False,
                                      skip_group_check=True)
                            pe.matmul(out[:, P:S], v_pad[s][:, 1, h, :], pt[:, S:S + P], start=False, stop=(h % 2 == 1),
                                      skip_group_check=True).then_inc(*PE_.does(s, "pv", h))

                        for h in range(NH + LAG2):
                            for s in ss:
                                if h < NH:
                                    scores(s, h)
                                if 0 <= h - LAG1 < NH:
                                    transposes(s, h - LAG1)
                                if 0 <= h - LAG2 < NH:
                                    values(s, h - LAG2)
                        for s in ss:
                            b = bank[s]
                            pe.wait_ge(*DVE_.did(s, "rinv"))
                            for k in range(KT):
                                for q in range(TT):
                                    last = pe.transpose(b[1][:, k * S + q * P:k * S + (q + 1) * P],
                                                        kc[s][:, q, k * P:(k + 1) * P], ident)
                            last.then_inc(*PE_.does(s, "rinv"))
                        for s in ss:
                            b = bank[s]
                            pe.wait_ge(*DVE_.did(s, "cl"))
                            to_experts(s, [b[1][:, t * S:(t + 1) * S] for t in range(KT)], dense, 0, DVE_.did(s, "cv"))\
                                .then_inc(*PE_.does(s, "dense"))
                        norm(1, 2, 3)
                        for s in ss:
                            b = bank[s]
                            pe.wait_ge(*DVE_.did(s, "y1", 1))
                            for k in range(KT):
                                last = pe.matmul(b[0][:, 0:S], cq_w[:, k, :], yv[s][:, k, :], start=(k == 0), stop=(k == KT - 1))
                            last.then_inc(*PE_.does(s, "cq"))
                            pe.wait_ge(*POOL_.did(s, "mem_in1"))
                            pe.matmul(b[2][:, 0:M], ckv_w[:, 0:C], mem_w[s][:, 0:M], start=True, stop=True)\
                              .then_inc(*PE_.does(s, "ck"))
                            pe.matmul(b[1][:, 0:C], mem_w[s][:], ckv_w[:, C:2 * C], start=True, stop=True)\
                              .then_inc(*PE_.does(s, "cv"))
                        for u in UNITS:
                            for s in ss:
                                if u == 0:
                                    pe.wait_ge(*ACT_.did(s, "cq"))
                                    pe.wait_ge(*POOL_.did(s, "ckd"))
                                    pe.wait_ge(*DVE_.did(s, "cv", 3))
                                pe.matmul(bank[s][u][:], c_q[s][:, (u // 2) * P:(u // 2 + 1) * P],
                                          c_kd[s][:, 8 * (u % 2):8 * (u % 2) + 8, :], start=True, stop=True)\
                                  .then_inc(*PE_.does(s, "cs", u))
                        for u in UNITS:
                            for s in ss:
                                pe_softmax_t(pe, K, s, u, c_p[u][s], bank[s][u], ACT_.did(s, "cexp", u))
                        for s in ss:
                            pe.wait_ge(*ACT_.did(s, "ct", 3))
                            for i in range(2):
                                for j in range(8):
                                    r = 32 * (j // 2)
                                    at = C_PAIR + 32 * (j % 2)
                                    last = pe.matmul(bank[s][0][r:r + 32, i * S:(i + 1) * S],
                                                     cv_pad[s][:, j, :] if i == 0 else const[:, at:at + 32],
                                                     c_t[s][:, j, :], start=(j % 2 == 0), stop=(j % 2 == 1),
                                                     skip_group_check=True)
                            last.then_inc(*PE_.does(s, "cpv"))
                        for s in ss:
                            pe.wait_ge(*DVE_.did(s, "cctx"))
                            for t in range(KT):
                                last = pe.matmul(bank[s][1][:, t * S:(t + 1) * S], cd_w[:, t * P:(t + 1) * P], c_ctx[s],
                                                 start=True, stop=True)
                            last.then_inc(*PE_.does(s, "cdense"))
                        norm(2, 2, 3)
                        pe.wait_ge(mot_ff_in, 16 * MOT_FF_DMAS * (which + 1))
                        ffb = (0, 1, 2)
                        for i, f in enumerate(FF_ORDER):
                            for s in ss:
                                b = bank[s][ffb[i % 3]]
                                if i < 2:
                                    pe.wait_ge(*DVE_.did(s, ("yl1", "yv1")[i], 2))
                                if i >= 3:
                                    pe.wait_ge(*DVE_.did(s, "hid", i - 3))

                                def up(y, lo, hi):
                                    for j, w in enumerate((gate_w, up_w)):
                                        for k in range(KT):
                                            last = pe.matmul(b[:, j * S + lo:j * S + hi], w[:, k, f * P:(f + 1) * P],
                                                             y[s][:, k, lo:hi], start=(k == 0), stop=(k == KT - 1))
                                    return last

                                if f < FULL:
                                    with if_early(s):
                                        up(yv, 0, LATE)
                                    last = up(yv, LATE, S)
                                elif f < 2 * FULL:
                                    last = up(yl, 0, S)
                                else:
                                    for m, w in enumerate((gate_w, up_w)):
                                        out = b[:, m * S:(m + 1) * S]
                                        for j, y in enumerate((yv[s], yl[s])):
                                            for k in range(KT):
                                                at = f * P + j * M
                                                last = pe.matmul(out[j * M:(j + 1) * M, :], w[:, k, at:at + M], y[:, k, :],
                                                                 start=(k == 0), stop=(k == KT - 1))
                                last.then_inc(*PE_.does(s, "up", i))
                        for s in ss:
                            pe.wait_ge(*DVE_.did(s, "hid", NF - 2))

                            def down(tiles, lo, hi, start, stop):
                                for t in range(KT):
                                    for f in tiles:
                                        last = pe.matmul(bank[s][3][:, t * S + lo:t * S + hi],
                                                         down_w[:, f, t * P:(t + 1) * P], hid[s][:, f, lo:hi],
                                                         start=(start and t == 0 and f == tiles[0]), stop=(stop and f == tiles[-1]),
                                                         skip_group_check=True)
                                return last

                            down(range(FULL, 2 * FULL), 0, S, True, False)
                            with if_early(s):
                                down(range(FULL), 0, LATE, False, False)
                            down(range(FULL), LATE, S, False, False)
                            pe.wait_ge(*DVE_.did(s, "hid", NF - 1))
                            down([2 * FULL], 0, S, False, True).then_inc(*PE_.does(s, "down"))
                        if final:
                            for s in ss:
                                pe.wait_ge(*DVE_.did(s, "x4"))
                                for t in range(TT):
                                    for k in range(KT):
                                        last = pe.transpose(bank[s][2][:, t * D + k * P:t * D + (k + 1) * P],
                                                            xw[s][:, k, t * P:(t + 1) * P], ident)
                                last.then_inc(*PE_.does(s, "out_t"))

                    @block.scalar
                    def _(act):
                        def square(n, ready):
                            for s in ss:
                                act.wait_ge(*ready(s))
                                act.activation(sq[s], xw[s], ACT.Square).then_inc(*ACT_.does(s, "square", n))

                        for s in ss:
                            act.activation(sq[s], x_all[:, :, tokens(it * STREAMS + s)], ACT.Square)\
                               .then_inc(*ACT_.does(s, "square", 0))
                        for s in ss:
                            b = bank[s]
                            act.wait_ge(*PE_.did(s, "q"))
                            act.copy(q_sb[s], two(b[0][:])).then_inc(*ACT_.does(s, "q"))
                            act.wait_ge(*PE_.did(s, "k"))
                            act.copy(k_sb[s], two(b[2][:])).then_inc(*ACT_.does(s, "k"))
                            act.wait_ge(*PE_.did(s, "v"))
                            v = b[3][:].rearrange("p (t h d) -> p t h d", t=TT, h=NH)
                            for i in range(2):
                                for t in range(TT):
                                    last = act.copy(v_pad[s][:, t, i::2, i * HD:(i + 1) * HD], v[:, t, i::2, :])
                                last.then_inc(*ACT_.does(s, f"v{i}"))
                        for h in range(NH + LAG2):
                            if h >= NH:
                                continue
                            for s in ss:
                                b = bank[s][2 + h % 2]
                                if h >= 2:
                                    act.wait_ge(*PE_.did(s, "t", h - 2))
                                act.wait_ge(*DVE_.did(s, "max1", h))
                                for q, (lo, hi) in enumerate(((0, P), (P, 3 * P))):
                                    act.activation(probs[s][:, h % 2, lo:hi], b[:, lo:hi], ACT.Exp,
                                                   bias=negmax[s][:, q, h:h + 1], accum_out=sums[s][:, q, h:h + 1])\
                                       .then_inc(*ACT_.does(s, f"exp{q}", h))
                        for s in ss:
                            act.wait_ge(*PE_.did(s, "rinv"))
                            act.copy(kr[s], two(bank[s][1][:])).then_inc(*ACT_.does(s, "rinv"))
                        square(1, lambda s: DVE_.did(s, "x2"))
                        for s in ss:
                            act.wait_ge(*PE_.did(s, "cq"))
                            act.copy(c_q[s], bank[s][0][:, 0:S]).then_inc(*ACT_.does(s, "cq"))
                            act.wait_ge(*PE_.did(s, "ck"))
                            act.copy(ck_sb[s][:], bank[s][2][:, 0:M]).then_inc(*ACT_.does(s, "ck"))
                        for u in UNITS:
                            for s in ss:
                                act_softmax_exp(act, K, s, u, c_p[u][s], CHD ** -0.5)
                        for u in UNITS:
                            for s in ss:
                                act_softmax_t(act, K, s, u, bank[s][u], c_t[s])
                        square(2, lambda s: DVE_.did(s, "x3"))
                        for f in range(NF):
                            for s in ss:
                                act.wait_ge(*PE_.did(s, "up", f))
                                if f >= 2:
                                    act.wait_ge(*DVE_.did(s, "silu", f - 2))
                                act.activation(tanh_b[s][:, f % 2, :], bank[s][f % 3][:, 0:S], ACT.Tanh, scale=0.5)\
                                   .then_inc(*ACT_.does(s, "tanh", f))
                        for s in ss:
                            if final:
                                act.wait_ge(*PE_.did(s, "out_t"))
                                act.copy(yv[s], two(bank[s][2][:])).then_inc(*ACT_.does(s, "x_out"))
                            else:
                                act.wait_ge(*DVE_.did(s, "x4"))
                                act.copy(x_all[:, :, tokens(it * STREAMS + s)], xw[s]).then_inc(*ACT_.does(s, "x_out"))

                    @block.vector
                    def _(dve):
                        def experts_norm(n, w, src_bank):
                            for s in ss:
                                e = it * STREAMS + s
                                b = bank[s][src_bank][:, 0:S]
                                dve.wait_ge(*PE_.did(s, "spread", n))
                                if n == 0:
                                    dve.wait_ge(*DVE_.did(s, "x_in"))
                                dve.tensor_tensor(rv[s][:], b, is_vis[:, bass.ds(e, 1), :].rearrange("p a n -> p (a n)"),
                                                  ALU.mult).then_inc(*DVE_.does(s, "rv", n))
                                dve.wait_ge(*DVE_.did(s, "rv", n))
                                dve.tensor_tensor(rl[s][:], b, rv[s][:], ALU.subtract).then_inc(*DVE_.does(s, "rl", n))
                                dve.wait_ge(*DVE_.did(s, "rl", n))
                                for m, dst, r in (("yl", yl, rl), ("yv", yv, rv)):
                                    for t in range(KT):
                                        dve.scalar_tensor_tensor(dst[s][:, t, :], xw[s][:, t, :], w[:, t:t + 1], r[s][:],
                                                                 ALU.mult, ALU.mult).then_inc(*DVE_.does(s, f"{m}{t}", n))

                        for s in ss:
                            dve.tensor_copy(xw[s], x_all[:, :, tokens(it * STREAMS + s)]).then_inc(*DVE_.does(s, "x_in"))
                        for s in ss:
                            dve_mean(dve, K, s, 0, bank[s][0])
                        experts_norm(0, w_in, 1)
                        for s in ss:
                            b = bank[s]
                            sin = cos_sin[:, 1:2, :].to_broadcast([P, KT, S])
                            for n, src, tmp, cosine, dst in (("q", b[1], qr, qc, q_sb), ("k", b[0], kr, kc, k_sb)):
                                dve.wait_ge(*PE_.did(s, f"rot_{n}"))
                                dve.tensor_tensor(tmp[s], two(src[:]), sin, ALU.mult).then_inc(*DVE_.does(s, n + "r"))
                                dve.wait_ge(*POOL_.did(s, n + "c"))
                                dve.wait_ge(*DVE_.did(s, n + "r"))
                                dve.tensor_tensor(dst[s], cosine[s], tmp[s], ALU.add).then_inc(*DVE_.does(s, n + "2"))
                        for h in range(NH + 1):
                            for s in ss:
                                if h < NH:
                                    b = bank[s][2 + h % 2]
                                    dve.wait_ge(*PE_.did(s, "s", h))
                                    for q, (lo, hi) in enumerate(((0, P), (P, 3 * P))):
                                        dve.tensor_reduce(negmax[s][:, q, h:h + 1], b[:, lo:hi], X, ALU.max, negate=True)\
                                           .then_inc(*DVE_.does(s, f"max{q}", h))
                                if h >= 1:
                                    dve.wait_ge(*PE_.did(s, "t", h - 1))
                                    if h >= 3:
                                        dve.wait_ge(*PE_.did(s, "pv", h - 3))
                                    dve.tensor_copy(probs_t[s][:, (h - 1) % 2, :], bank[s][1][:, 0:384])\
                                       .then_inc(*DVE_.does(s, "pt", h - 1))
                        for s in ss:
                            dve.wait_ge(*ACT_.did(s, "exp1", NH - 1))
                            dve.reciprocal(kc[s].rearrange("p q (h d) -> p q h d", d=HD),
                                           sums[s].unsqueeze(3).to_broadcast([P, TT, NH, HD])).then_inc(*DVE_.does(s, "rinv"))
                        for s in ss:
                            dve.wait_ge(*PE_.did(s, "pv", NH - 1))
                            dve.wait_ge(*ACT_.did(s, "rinv"))
                            dve.tensor_tensor(q_sb[s], two(bank[s][0][:]), kr[s], ALU.mult).then_inc(*DVE_.does(s, "ctx"))
                            dve.wait_ge(*DVE_.did(s, "ctx"))
                            vis = is_vis[:, bass.ds(it * STREAMS + s, 1), :].to_broadcast([P, KT, S])
                            dve.tensor_tensor(yv[s], q_sb[s], vis, ALU.mult).then_inc(*DVE_.does(s, "cv"))
                            dve.wait_ge(*DVE_.did(s, "cv"))
                            dve.tensor_tensor(yl[s], q_sb[s], yv[s], ALU.subtract).then_inc(*DVE_.does(s, "cl"))
                        for s in ss:
                            dve.wait_ge(*PE_.did(s, "dense"))
                            dve.tensor_tensor(xw[s], two(bank[s][1][:]), xw[s], ALU.add).then_inc(*DVE_.does(s, "x2"))
                        for s in ss:
                            dve_mean(dve, K, s, 1, bank[s][2])
                        for s in ss:
                            dve.wait_ge(*PE_.did(s, "spread", 1))
                            for t in range(KT):
                                dve.scalar_tensor_tensor(yv[s][:, t, :], xw[s][:, t, :], w_cross[:, t:t + 1],
                                                         bank[s][3][:, 0:S], ALU.mult, ALU.mult)\
                                   .then_inc(*DVE_.does(s, f"y{t}", 1))
                        for s in ss:
                            dve.wait_ge(*PE_.did(s, "cv"))
                            src = bank[s][1][:, 0:C].rearrange("p (g n) -> p g n", g=4)
                            dst = cv_pad[s].rearrange("p (g q) n -> p g q n", g=4)
                            for q in range(2):
                                for i in range(2):
                                    at = q * 2 * CHD + i * CHD
                                    dve.tensor_copy(dst[i * M:(i + 1) * M, :, q, at:at + CHD],
                                                    src[i * M:(i + 1) * M, :, at:at + CHD])\
                                       .then_inc(*DVE_.does(s, "cv", 2 * q + i))
                        for u in UNITS:
                            for s in ss:
                                dve_softmax_shift(dve, K, s, u, bank[s][u], c_p[u][s])
                        for s in ss:
                            dve.wait_ge(*PE_.did(s, "cpv"))
                            dve.reciprocal(rv[s][:], bank[s][0][:, S:2 * S]).then_inc(*DVE_.does(s, "crec"))
                            dve.wait_ge(*DVE_.did(s, "crec"))
                            dve.tensor_tensor(c_ctx[s], bank[s][0][:, 0:S], rv[s][:], ALU.mult).then_inc(*DVE_.does(s, "cctx"))
                        for s in ss:
                            dve.wait_ge(*PE_.did(s, "cdense"))
                            dve.tensor_tensor(xw[s], two(bank[s][1][:]), xw[s], ALU.add).then_inc(*DVE_.does(s, "x3"))
                        for s in ss:
                            dve_mean(dve, K, s, 2, bank[s][2])
                        experts_norm(2, w_post, 3)
                        for i, f in enumerate(FF_ORDER):
                            for s in ss:
                                b = bank[s][i % 3]
                                dve.wait_ge(*ACT_.did(s, "tanh", i))
                                dve.scalar_tensor_tensor(silu_b[s][:, i % 2, :], tanh_b[s][:, i % 2, :], 1.0, b[:, 0:S],
                                                         ALU.add, ALU.mult).then_inc(*DVE_.does(s, "silu", i))
                                dve.wait_ge(*DVE_.did(s, "silu", i))
                                dve.tensor_tensor(hid[s][:, f, :], silu_b[s][:, i % 2, :], b[:, S:2 * S], ALU.mult)\
                                   .then_inc(*DVE_.does(s, "hid", i))
                        for s in ss:
                            dve.wait_ge(*PE_.did(s, "down"))
                            dve.scalar_tensor_tensor(xw[s], two(bank[s][3][:]), 0.5, xw[s], ALU.mult, ALU.add)\
                               .then_inc(*DVE_.does(s, "x4"))

                    if final:
                        @block.sync
                        def _(sp):
                            for s in ss:
                                sp.wait_ge(*ACT_.did(s, "x_out"))
                                sp.dma_start(out_d[bass.ds(it * STREAMS + s, 1)].rearrange("a (t p) d -> p (a t) d", p=P), yv[s])\
                                  .then_inc(sent[s], 16)
                            for s in ss:
                                sp.wait_ge(sent[s], 16)
                clear_and_join()

        def before_first():
            with nc.Block() as block:
                @block.sync
                def _(sp):
                    sp.dma_start(wq[:], ca_w["Wq"].rearrange("(k p) n -> p k n", p=P)).then_inc(ca_in, 16)
                    sp.dma_start(wkv[:], ca_w["Wkv"]).then_inc(ca_in, 16)
                    sp.dma_start(wo[:], ca_w["Wo"].rearrange("(k p) n -> p k n", p=P)).then_inc(ca_in, 16)

        mot_layer(0, 1, before_first)

        with nc.Block() as block:
            @block.sync
            def _(sp):
                sp.dma_start(w1, ca_w["W1"].rearrange("(k p) n -> p k n", p=P)).then_inc(ca_ff_in, 16)
                sp.dma_start(w2, ca_w["W2"].rearrange("(k p) n -> p k n", p=P)).then_inc(ca_ff_in, 16)
                load_mot(sp, mot_w[1], False)

            @block.gpsimd
            def _(pool):
                for s in range(STREAMS):
                    pool.memset(zeroed[s], 0.0)

        with nc.Fori(0, B // STREAMS) as it:
            K = PE_, ACT_, DVE_, POOL_ = layer(CA_PE, CA_ACT, CA_DVE, CA_POOL)
            ss = range(STREAMS)
            with nc.Block() as block:
                @block.gpsimd
                def _(pool):
                    for s in ss:
                        e = it * STREAMS + s
                        pool.tensor_copy(xw[s], x_all[:, :, tokens(e)]).then_inc(*POOL_.does(s, "x_in"))
                        for i in range(2):
                            pool.tensor_copy(mem_w[s][:, i * M:(i + 1) * M], ctx_t[:, bass.ds(e * M, M)])\
                                .then_inc(*POOL_.does(s, f"mem_in{i}"))
                    for s in ss:
                        pool_rstd(pool, K, s, 0)
                    for u in UNITS:
                        for s in ss:
                            pool_softmax_norm(pool, K, s, u, g_p[u][s])
                    for s in ss:
                        pool_rstd(pool, K, s, 1)

                @block.tensor
                def _(pe):
                    def norm(n, ready, banks):
                        for s in ss:
                            pe.wait_ge(*ready(s))
                            for k in range(KT):
                                last = pe.matmul(bank[s][banks[0]][:, 0:S], mean_w[:], xw[s][:, k, :],
                                                 start=(k == 0), stop=(k == KT - 1))
                            last.then_inc(*PE_.does(s, "mu", n))
                        for s in ss:
                            pe.wait_ge(*ACT_.did(s, "square", n))
                            pe_sumsq(pe, K, s, n, bank[s][banks[1]], C_EPS + TT)
                        for s in ss:
                            pe_spread(pe, K, s, n, bank[s][banks[2]])

                    norm(0, lambda s: POOL_.did(s, "x_in"), (0, 1, 2))
                    pe.wait_ge(ca_in, 16 * CA_DMAS)
                    for s in ss:
                        b = bank[s]
                        pe.wait_ge(*ACT_.did(s, "y1", 0))
                        for u in UNITS:
                            for j in range(2):
                                for k in range(KT):
                                    at = (2 * u + j) * P
                                    last = pe.matmul(b[(3 + u) % 4][:, j * S:(j + 1) * S], wq[:, k, at:at + P],
                                                     yv[s][:, k, :], start=(k == 0), stop=(k == KT - 1))
                            last.then_inc(*PE_.does(s, "q", u))
                        pe.wait_ge(*POOL_.did(s, "mem_in1"))
                        pe.wait_ge(*ACT_.did(s, "q", 0))
                        for j in range(GT):
                            last = pe.matmul(b[3][:, j * M:(j + 1) * M], wkv[:, j * P:(j + 1) * P], mem_w[s][:, 0:M],
                                             start=True, stop=True)
                        last.then_inc(*PE_.does(s, "k"))
                        for c in range(2):
                            pe.wait_ge(*ACT_.did(s, "q", 1 + c))
                            pe.matmul(b[c][:], mem_w[s][:], wkv[:, INNER + c * 512:INNER + (c + 1) * 512],
                                      start=True, stop=True).then_inc(*PE_.does(s, f"v{c}"))
                    for u in UNITS:
                        for s in ss:
                            e = it * STREAMS + s
                            out = bank[s][(2 + u) % 4]
                            if u == 0:
                                pe.wait_ge(*ACT_.did(s, "q", 3))
                                pe.wait_ge(*DVE_.did(s, "v11"))
                            t, half = u // 2, u % 2
                            for j in range(4):
                                pe.matmul(out[:, j * P:(j + 1) * P], g_q[s][:, 4 * half + j, t * P:(t + 1) * P],
                                          k_diag[s][:, 4 * half + j], start=(j == 0), stop=False, skip_group_check=True)
                            pe.matmul(out[:], ones_bf[:], media_neg[:, bass.ds(e * M, M)].unsqueeze(1).to_broadcast([1, 8, M]),
                                      start=False, stop=True, skip_group_check=True).then_inc(*PE_.does(s, "cs", u))
                    for u in UNITS:
                        for s in ss:
                            pe_softmax_t(pe, K, s, u, g_p[u][s], bank[s][(2 + u) % 4], POOL_.did(s, "cnorm", u))
                    for s in ss:
                        for u in UNITS:
                            out = bank[s][(2 + u) % 4]
                            pe.wait_ge(*ACT_.did(s, "ct", 3))
                            for j in range(2):
                                last = pe.matmul(out[:, j * S:(j + 1) * S], v_diag[s][:, 2 * u + j, :], g_t[s][:, 2 * u + j, :],
                                                 start=True, stop=True)
                            last.then_inc(*PE_.does(s, "cpv", u))
                    for s in ss:
                        pe.wait_ge(*ACT_.did(s, "cpv", 3))
                        for t in range(KT):
                            for k in range(GT):
                                last = pe.matmul(bank[s][0][:, t * S:(t + 1) * S], wo[:, k, t * P:(t + 1) * P], g_q[s][:, k, :],
                                                 start=(k == 0), stop=(k == GT - 1))
                        last.then_inc(*PE_.does(s, "wo"))
                    norm(1, lambda s: DVE_.did(s, "x2"), (1, 2, 3))
                    pe.wait_ge(ca_ff_in, 16 * CA_FF_DMAS)
                    for s in ss:
                        pe.wait_ge(*ACT_.did(s, "y1", 1))
                        for u in UNITS:
                            for j in range(2):
                                for k in range(KT):
                                    at = (2 * u + j) * P
                                    last = pe.matmul(bank[s][u][:, j * S:(j + 1) * S], w1[:, k, at:at + P], yv[s][:, k, :],
                                                     start=(k == 0), stop=(k == KT - 1))
                            last.then_inc(*PE_.does(s, "up", u))
                    for s in ss:
                        pe.wait_ge(*ACT_.did(s, "gelu", 3))
                        for t in range(KT):
                            for k in range(GT):
                                last = pe.matmul(bank[s][0][:, t * S:(t + 1) * S], w2[:, k, t * P:(t + 1) * P], g_h[s][:, k, :],
                                                 start=(k == 0), stop=(k == GT - 1))
                        last.then_inc(*PE_.does(s, "down"))

                @block.scalar
                def _(act):
                    def norm(n, g, bias):
                        for s in ss:
                            act.wait_ge(*DVE_.did(s, "center", n))
                            act.activation(sq[s], yl[s], ACT.Square).then_inc(*ACT_.does(s, "square", n))
                        for s in ss:
                            act.wait_ge(*DVE_.did(s, "scaled", n))
                            for t in range(KT):
                                act.activation(yv[s][:, t, :], yl[s][:, t, :], ACT.Identity, bias=vec[bias][:, t:t + 1],
                                               scale=vec[g][:, t:t + 1]).then_inc(*ACT_.does(s, f"y{t}", n))

                    norm(0, "qg", "qb")
                    for s in ss:
                        for u in UNITS:
                            act.wait_ge(*PE_.did(s, "q", u))
                            act.copy(g_q[s][:, 2 * u:2 * u + 2, :], two(bank[s][(3 + u) % 4][:])).then_inc(*ACT_.does(s, "q", u))
                    for u in UNITS:
                        for s in ss:
                            act_softmax_exp(act, K, s, u, g_p[u][s], GHD ** -0.5)
                    for u in UNITS:
                        for s in ss:
                            act_softmax_t(act, K, s, u, bank[s][(2 + u) % 4], g_t[s])
                    for s in ss:
                        for u in UNITS:
                            act.wait_ge(*PE_.did(s, "cpv", u))
                            act.copy(g_q[s][:, 2 * u:2 * u + 2, :], two(bank[s][(2 + u) % 4][:])).then_inc(*ACT_.does(s, "cpv", u))
                    norm(1, "fg", "fb")
                    for s in ss:
                        for u in UNITS:
                            act.wait_ge(*PE_.did(s, "up", u))
                            act.activation(g_h[s][:, 2 * u:2 * u + 2, :], two(bank[s][u][:]), ACT.Gelu)\
                               .then_inc(*ACT_.does(s, "gelu", u))
                    for s in ss:
                        act.wait_ge(*DVE_.did(s, "x3"))
                        act.copy(x_all[:, :, tokens(it * STREAMS + s)], xw[s]).then_inc(*ACT_.does(s, "x_out"))

                @block.vector
                def _(dve):
                    def norm(n, banks):
                        for s in ss:
                            dve.wait_ge(*PE_.did(s, "mu", n))
                            dve.tensor_tensor(yl[s], xw[s], bank[s][banks[0]][:, 0:S].unsqueeze(1).to_broadcast([P, KT, S]),
                                              ALU.subtract).then_inc(*DVE_.does(s, "center", n))
                        for s in ss:
                            dve_mean(dve, K, s, n, bank[s][banks[1]])
                        for s in ss:
                            dve.wait_ge(*PE_.did(s, "spread", n))
                            dve.tensor_tensor(yl[s], yl[s], bank[s][banks[2]][:, 0:S].unsqueeze(1).to_broadcast([P, KT, S]),
                                              ALU.mult).then_inc(*DVE_.does(s, "scaled", n))

                    norm(0, (0, 1, 2))
                    for s in ss:
                        e = it * STREAMS + s
                        b = bank[s]
                        dve.wait_ge(*PE_.did(s, "k"))
                        for i in range(2):
                            r = slice(i * M, (i + 1) * M)
                            dve.tensor_tensor(k_diag[s][r, :, i, :], b[3][r, :].rearrange("p (j m) -> p j m", j=GT),
                                              media[r, bass.ds(e * M, M)].unsqueeze(1).to_broadcast([M, GT, M]), ALU.mult)\
                               .then_inc(*DVE_.does(s, f"k{i}"))
                        for c in range(2):
                            dve.wait_ge(*PE_.did(s, f"v{c}"))
                            for i in range(2):
                                r = slice(i * M, (i + 1) * M)
                                dve.tensor_copy(v_diag[s][r, 4 * c:4 * c + 4, i * GHD:(i + 1) * GHD],
                                                b[c][r, :].rearrange("p (j i d) -> p j i d", i=2, d=GHD)[:, :, i, :])\
                                   .then_inc(*DVE_.does(s, f"v{c}{i}"))
                    for u in UNITS:
                        for s in ss:
                            dve_softmax_shift(dve, K, s, u, bank[s][(2 + u) % 4], g_p[u][s])
                    for u in UNITS:
                        for s in ss:
                            dve_softmax_sum(dve, K, s, u, g_p[u][s])
                    for s in ss:
                        dve.wait_ge(*PE_.did(s, "wo"))
                        dve.scalar_tensor_tensor(xw[s], two(bank[s][0][:]), ca_gate[:, 0:1], xw[s], ALU.mult, ALU.add)\
                           .then_inc(*DVE_.does(s, "x2"))
                    norm(1, (1, 2, 3))
                    for s in ss:
                        dve.wait_ge(*PE_.did(s, "down"))
                        dve.scalar_tensor_tensor(xw[s], two(bank[s][0][:]), ca_gate[:, 1:2], xw[s], ALU.mult, ALU.add)\
                           .then_inc(*DVE_.does(s, "x3"))
            clear_and_join()

        def before_second():
            with nc.Block() as block:
                @block.gpsimd
                def _(pool):
                    for s in range(STREAMS):
                        pool.memset(zeroed[s], 0.0)
                    pool.memset(down_w[:, 2 * FULL, :], 0.0).then_inc(pads_zero, 1)
                    tail = up_w[:, :, 2 * FULL * P:NF * P].rearrange("p k (e n) -> p k e n", e=2)
                    pool.memset(tail[:, :, :, TAIL:M], 0.0)

                @block.sync
                def _(sp):
                    sp.wait_ge(pads_zero, 4)
                    load_mot_ff(sp, mot_w[1])

        mot_layer(1, 3, before_second)


MOT = ("v_qkv", "l_qkv", "v_dense", "l_dense", "cq_w", "ckv_w", "cdense_w", "v_gate", "v_up", "v_down",
       "l_gate", "l_up", "l_down")
VEC = {"b_gate": "L0_xattn_b_gate", "fuse": "L0_xattn_norm_w", "qg": "L2_xattn_ln_q_g", "qb": "L2_xattn_ln_q_b",
       "fg": "L2_xattn_ln_ff_g", "fb": "L2_xattn_ln_ff_b",
       "in1": "L1_xattn_ln_in_w", "post1": "L1_xattn_ln_post_attn_w", "cross1": "L1_xattn_ln_post_cross_w",
       "in3": "L3_xattn_ln_in_w", "post3": "L3_xattn_ln_post_attn_w", "cross3": "L3_xattn_ln_post_cross_w"}


def kernel(**inputs):
    import concourse.bacc as bacc
    from concourse.bass_utils import run_bass_kernel_spmd

    nc = bacc.Bacc("TRN2", target_bir_lowering=False, num_devices=1)
    arrays, ap = {}, {}
    for name, value in inputs.items():
        a = np.ascontiguousarray(value)
        arrays["in_" + name] = a
        ap[name] = nc.dram_tensor("in_" + name, a.shape, mybir.dt.from_np(a.dtype), kind="ExternalInput").ap()
    table = nc.inline_tensor(constants(), name="table_of_constants").ap()
    out = nc.dram_tensor("out_x", (B, S, D), F32, kind="ExternalOutput").ap()
    program(nc, ap["x"], ap["ctx_1024"], ap["pos_1xS"], ap["mask_BxS_ik0"], ap["mask_BxS2_bk0"],
            {"W_mem": ap["L0_xattn_W_mem"], "W_gate": ap["L0_xattn_W_gate"], **{n: ap[k] for n, k in VEC.items()}},
            [{n: ap[f"L{i}_xattn_{n}"] for n in MOT} for i in (1, 3)],
            {n: ap["L2_xattn_" + n] for n in ("Wq", "Wkv", "Wo", "attn_gate", "W1", "W2", "ff_gate")},
            table, out)
    return run_bass_kernel_spmd(nc, [arrays], core_ids=[0]).results[0]["out_x"]
```

```python
from contextlib import ExitStack

import numpy as np

import concourse.bass as bass
from concourse import mybir

F32 = mybir.dt.float32
BF16 = mybir.dt.bfloat16
I32 = mybir.dt.int32
U8 = mybir.dt.uint8
ALU = mybir.AluOpType
ACT = mybir.ActivationFunctionType
X = mybir.AxisListType.X

P = 128
B, S, D = 8, 256, 256
M, C = 64, 128
KT = D // P
TT = S // P
NH = 16
HD = D // NH
CHD = C // NH
GHD = 64
INNER = NH * GHD
INTER = 688
FULL = INTER // P
TAIL = INTER - FULL * P
FF_ORDER = [f for i in range(FULL) for f in (FULL + i, i)] + [2 * FULL]
NF = 2 * FULL + 1
FF = 4 * D
GT = INNER // P
RMS_EPS, LN_EPS = 1e-6, 1e-5
BIG = -1e30
STREAMS = 2
ROUNDS = 2
LATE = S - S // 4

C_ID, C_ROT, C_H8, C_H16, C_ROW, C_TRIG, C_PAIR = 0, 128, 256, 264, 280, 282, 794
C_END = C_PAIR + 64


def constants():
    t = np.zeros((P, C_END), np.float32)
    p = np.arange(P)
    t[p, C_ID + p] = 1.0
    for m in range(P):
        i = m % HD
        k = m + HD // 2 if i < HD // 2 else m - HD // 2
        t[k, C_ROT + m] = -1.0 if i < HD // 2 else 1.0
    t[p, C_H8 + p // HD] = HD ** -0.5
    t[p, C_H16 + p // CHD] = 1.0
    t[:, C_ROW], t[:, C_ROW + 1] = p, p + P
    inv = (1.0 / 10000.0 ** (np.arange(0, HD, 2, dtype=np.float32) / np.float32(HD))).astype(np.float32)
    ang = np.outer(np.arange(S, dtype=np.float32), inv).astype(np.float32)
    for tt in range(TT):
        a = ang[tt * P:(tt + 1) * P][:, (p % HD) % (HD // 2)]
        t[:, C_TRIG + 256 * tt:C_TRIG + 256 * tt + 128] = np.cos(a)
        t[:, C_TRIG + 256 * tt + 128:C_TRIG + 256 * tt + 256] = np.sin(a)
    for i in range(2):
        for h in range(2):
            at = C_PAIR + 32 * i + i * 2 * CHD + h * CHD
            t[h * M:(h + 1) * M, at:at + CHD] = 1.0
    return t


class Steps:

    def __init__(self, sems, names, at_round):
        self.sems, self.round = sems, at_round
        self.names = [list(n) for n in names] if isinstance(names, tuple) else [list(names)] * STREAMS
        self.value = [{n: i + 1 for i, n in enumerate(each)} for each in self.names]
        self.issued = [0, 0]

    def does(self, s, *name):
        due = self.names[s][self.issued[s] % len(self.names[s])]
        assert due == name, (name, due)
        self.issued[s] += 1
        return self.sems[s], 1

    def did(self, s, *name, back=0):
        return self.sems[s], self.value[s][name] + len(self.names[s]) * (self.round[s] - back)


def names(text):
    return [(w,) for w in text.split()]



UNITS = range(4)
LAG1, LAG2 = 1, 2
PT_ON_ACT, QM_ON_POOL = set(), {1}
LEAD = 3


def attention_steps(*parts):
    out = []
    for h in range(NH + LAG2):
        for lag, w in parts:
            if 0 <= h - lag < NH:
                out += [(n, h - lag) for n in w.split()]
    return out


def norm_steps(kind, n):
    return [(w, n) for w in kind.split()]


FUSE_PE = names("mem_rows scores probs_t context gate") + norm_steps("sumsq spread", 0)
FUSE_ACT = names("mem_rows exp probs_t context gate0 gate1") + norm_steps("square", 0) + names("x_out")
FUSE_DVE = names("x_in max sub sum recip norm gated fused") + norm_steps("mean", 0) + names("y0 y1")
FUSE_POOL = names("mem_in") + norm_steps("rstd", 0)

MOT_PE = (norm_steps("sumsq spread", 0) + names("q k v rot_q rot_k") + attention_steps((0, "s"), (LAG1, "t"), (LAG2, "pv"))
          + names("rinv dense") + norm_steps("sumsq spread", 1) + names("cq ck cv")
          + [("cs", u) for u in UNITS] + [("ct", u) for u in UNITS] + names("cpv cdense")
          + norm_steps("sumsq spread", 2) + [("up", f) for f in range(NF)] + names("down"))


def mot_act(s):
    return (norm_steps("square", 0) + names("q k v0 v1") + ([] if s in QM_ON_POOL else [("qm", h) for h in range(LEAD)])
            + attention_steps((0, "exp0 exp1"), *([] if s in QM_ON_POOL else [(-LEAD, "qm")]), *([(LAG1, "pt")] if s in PT_ON_ACT else []))
            + names("rexp rinv") + norm_steps("square", 1) + names("cq ck")
            + [("cexp", u) for u in UNITS] + [("ct", u) for u in UNITS]
            + norm_steps("square", 2) + [("tanh", f) for f in range(NF)] + names("x_out"))


def mot_dve(s):
    return (names("x_in") + norm_steps("mean rv rl yl0 yl1 yv0 yv1", 0) + names("qr q2 kr k2")
            + attention_steps((0, "max0 max1"), *([(LAG1, "pt")] if s not in PT_ON_ACT else [])) + names("rinv ctx cv cl x2")
            + norm_steps("mean y0 y1", 1) + [("cv", g) for g in range(4)]
            + [(w, u) for u in UNITS for w in ("cmax", "csub")]
            + names("crec cctx x3") + norm_steps("mean rv rl yl0 yl1 yv0 yv1", 2)
            + [(w, f) for f in range(NF) for w in ("silu", "hid")] + names("x4"))


def mot_pool(s):
    return (names("mem_in0 mem_in1") + norm_steps("rstd", 0) + names("qc kc")
            + [("qm", h) for h in range(NH) if s in QM_ON_POOL]
            + norm_steps("rstd", 1) + names("ckd") + norm_steps("rstd", 2))


MOT_ACT, MOT_DVE, MOT_POOL = (tuple(f(s) for s in range(STREAMS)) for f in (mot_act, mot_dve, mot_pool))

CA_PE = (norm_steps("mu sumsq spread", 0) + [("q", u) for u in UNITS] + names("k v0 v1")
         + [("cs", u) for u in UNITS] + [("ct", u) for u in UNITS] + [("cpv", u) for u in UNITS]
         + names("wo") + norm_steps("mu sumsq spread", 1) + [("up", u) for u in UNITS] + names("down"))
CA_ACT = (norm_steps("square y0 y1", 0) + [("q", u) for u in UNITS]
          + [("cexp", u) for u in UNITS] + [("ct", u) for u in UNITS] + [("cpv", u) for u in UNITS]
          + norm_steps("square y0 y1", 1) + [("gelu", u) for u in UNITS] + names("x_out"))
CA_DVE = (names("x_in") + norm_steps("center mean scaled", 0) + names("k0 k1 v00 v01 v10 v11")
          + [(w, v) for u in range(5) for w, v in (("cmax", u), ("csub", u), ("csum", u - 1), ("crec", u - 1)) if v in UNITS]
          + names("x2")
          + norm_steps("center mean scaled", 1) + names("x3"))
CA_POOL = (names("mem_in0 mem_in1") + norm_steps("rstd", 0)
           + [("cnorm", u) for u in UNITS] + norm_steps("rstd", 1))


def mot_slots():
    start = [[("take",)], [("mean", 0)], [("normed", 0)], [("q",)], [("k",)], [("v",)], [("rot_q",)], [("rot_k",)]]
    heads = [[("attend", h)] for h in range(NH + LAG2)]
    light = [[("sums_out",)], [("sums_spread",)], [("context",)], [("project",)], [("mean", 1)], [("normed", 1)],
             [("cross_in",)], [("cross_scores", 0), ("cross_scores", 1)], [("cross_scores", 2), ("cross_scores", 3)],
             [("cross_turn", 0), ("cross_turn", 1)], [("cross_turn", 2), ("cross_turn", 3)], [("cross_values",)],
             [("cross_project",)], [("mean", 2)], [("normed", 2)]]
    hidden = [[(w, j) for w, j in (("up", i), ("down", i - FF_LAG)) if 0 <= j < NF] for i in range(NF + FF_LAG)]
    return start + heads + light + hidden + [[("give",)], [], []]


def fuse_slots():
    return [[(w,)] for w in "take memory scores sums turn context gate square".split()] + [
        [("mean", 0)], [("normed", 0)], [("give",)], []]


def ca_slots():
    return ([[("take",)], [("center", 0)], [("mean", 0)], [("normed", 0)]] + [[("q", u)] for u in UNITS] + [[("memory",)]]
            + [[(w, v) for w, v in (("scores", u), ("sums", u - 1)) if v in UNITS] for u in range(5)]
            + [[("turn", u)] for u in UNITS] + [[("values", u)] for u in UNITS]
            + [[("project", k), ("project", k + 1)] for k in range(0, GT, 2)]
            + [[("center", 1)], [("mean", 1)], [("normed", 1)]] + [[("up", u)] for u in UNITS]
            + [[("down", k), ("down", k + 1)] for k in range(0, GT, 2)] + [[("give",)], []])


def in_turn(slots, lag):
    order = []
    for i in range(ROUNDS * len(slots) + lag):
        for s, j in ((0, i), (1, i - lag)):
            if 0 <= j < ROUNDS * len(slots):
                order += [(w, s, j // len(slots), *n) for w, *n in slots[j % len(slots)]]
    return order


FF_LAG = 3
MOT_ORDER = in_turn(mot_slots(), 10)
FUSE_ORDER = in_turn(fuse_slots(), 1)
CA_ORDER = in_turn(ca_slots(), 5)


def program(nc, x_d, ctx_d, pos_d, type_d, media_d, fuse_w, mot_w, ca_w, const_d, out_d):
    ctx = ExitStack()
    with ctx:
        def sb(name, shape, dt=F32):
            return ctx.enter_context(nc.sbuf_tensor(name, shape, dt))

        def sem(name):
            return ctx.enter_context(nc.semaphore(name))

        x_all = sb("x_all", [P, KT, B * S])
        ctx_t = sb("ctx_t", [P, B * M])
        const = sb("const", [P, C_END])
        ident = const[:, C_ID:C_ID + P]
        ident_bf = sb("ident_bf", [P, P], BF16)
        causal_f = sb("causal_f", [P, P])
        causal = sb("causal", [P, P], BF16)
        ones = sb("ones", [P, P])
        ones_bf = sb("ones_bf", [1, P], BF16)
        mean_w = sb("mean_w", [P, P])
        neg_half = sb("neg_half", [P, TT])
        cos_sin = sb("cos_sin", [P, 2, S])
        is_vis = sb("is_vis", [P, B, S])
        early = sb("early", [1, B], I32)
        media = sb("media", [P, B * M])
        media_neg = sb("media_neg", [1, B * M], BF16)
        VECS = ("b_gate", "fuse", "in1", "cross1", "post1", "qg", "qb", "fg", "fb", "in3", "cross3", "post3")
        vec_rows = sb("vec_rows", [KT * len(VECS), P])
        vec_t = sb("vec_t", [P, KT * len(VECS)])
        vec = {n: vec_t[:, KT * i:KT * (i + 1)] for i, n in enumerate(VECS)}
        half_b = sb("half_b", [P, KT])
        ca_gate = sb("ca_gate", [P, 2])
        mem_t = sb("mem_t", [P, KT, B * M])
        w_mem_t = sb("w_mem_t", [P, D])
        w_gate_t = sb("w_gate_t", [P, 2 * KT, D])

        qkv = sb("qkv", [P, 2, KT, 3 * D])
        dense = sb("dense", [P, 2, KT, D])
        cq_w = sb("cq_w", [P, KT, C])
        ckv_w = sb("ckv_w", [P, 2 * C])
        cd_w = sb("cd_w", [P, D])
        gate_w = sb("gate_w", [P, KT, NF * P])
        up_w = sb("up_w", [P, KT, NF * P])
        down_w = sb("down_w", [P, NF, D])
        wq = sb("wq", [P, KT, INNER])
        wkv = sb("wkv", [P, 2 * INNER])
        wo = sb("wo", [P, GT, D])
        w1 = up_w[:, :, 0:FF]
        w2 = down_w[:, 0:GT, :]

        x_rows = [w[:].rearrange("p a n -> p (a n)").rearrange("p (t n) -> p t n", n=D) if len(w.shape) == 3
                  else w[:].rearrange("p (t n) -> p t n", n=D) for w in (wq, wkv)]
        small = wo[:].rearrange("p a n -> p (a n)")
        ctx_rows = small[:, 0:512].rearrange("p (t n) -> p t n", n=C)
        w_mem_rows = small[:, 512:768].rearrange("p (t n) -> p t n", n=C)
        w_gate_rows = small[:, 768:1792].rearrange("p (t n) -> p t n", n=2 * D)
        type_i = gate_w[:].rearrange("p a n -> p (a n)")[:, 0:B * S].bitcast(I32)
        type_one = up_w[:].rearrange("p a n -> p (a n)")[:, 0:B * S].rearrange("p (b n) -> p b n", b=B)
        pos_i = small[:, 1792:2048].bitcast(I32)
        one_hot = qkv[:, 0, 0, 0:2 * S].rearrange("p (t n) -> p t n", t=TT)
        pos_f = qkv[:, 0, 1, 0:S]
        pos_g = qkv[:, 0, 1, S:2 * S]
        media_u8 = sb("media_u8", [P, B * M], U8)

        ARENA = 8704
        arena = [sb(f"arena{s}", [P, ARENA]) for s in range(STREAMS)]

        def cut(at, *shape):
            n = int(np.prod(shape))
            assert at + n <= ARENA
            flat = [a[:, at:at + n] for a in arena]
            if len(shape) == 1:
                return flat
            k = "abcd"[:len(shape)]
            spec = f"p ({' '.join(k)}) -> p {' '.join(k)}"
            return [f.rearrange(spec, **dict(zip(k, shape))) for f in flat]

        xw = cut(0, KT, S)
        sq = cut(512, KT, S)
        yv = cut(1024, KT, S)
        yl = cut(1536, KT, S)
        Z = 2048
        v_pad = cut(Z, TT, NH, 32)
        cv_pad = cut(Z + 1024, 8, 32)
        k_diag = cut(Z, GT, 2, M)
        v_diag = cut(Z + 1024, GT, P)
        zeroed = cut(Z, 2048)
        R = 4096
        stat = cut(8192, 512)
        q_sb, k_sb, qc, qr, kc, kr = (cut(R + 512 * i, KT, S) for i in range(6))
        QM = 4
        q_one = cut(R + 1024, QM, S)
        probs = cut(R + 3072, 2, 384)
        c_q = cut(R, S)
        c_kd = cut(R + 256, NH, M)
        c_t = cut(R + 1280, 8, S)
        c_p = [sq, yv, yl, cut(R + 3328, KT, S)]
        probs_t = [sb(f"probs_t{s}", [P, 2, 384]) for s in range(STREAMS)]
        c_ctx = cut(R, S)
        hid = cut(R, NF, S)
        tanh_b = cut(R + NF * S, 2, S)
        silu_b = cut(R + NF * S + 512, 2, S)
        g_q = cut(R, GT, S)
        g_t = cut(R + 2048, GT, S)
        g_p = [sq, yv, yl, [p[:].rearrange("p a n -> p (a n)")[:, 0:512].rearrange("p (a n) -> p a n", a=2)
                            for p in probs_t]]
        g_h = cut(R, GT, S)
        f_mem = cut(R, D)
        f_p = cut(R + 256, TT, M)
        f_pt = cut(R + 384, S)
        f_mc = cut(R + 640, KT, S)
        f_tanh = cut(R + 1152, KT, S)
        f_u = cut(R + 1664, KT, S)
        ms = [a[:, 0:2] for a in stat]
        rstd = [a[:, 2:4] for a in stat]
        rinv_v = [a[:, 260:292].rearrange("p (t n) -> p t n", t=TT) for a in stat]
        negmax = [a[:, 292:324].rearrange("p (t n) -> p t n", t=TT) for a in stat]
        sums = [a[:, 324:356].rearrange("p (t n) -> p t n", t=TT) for a in stat]
        cmax = [a[:, 424:456].rearrange("p (u n) -> p u n", u=4) for a in stat]
        csum = [a[:, 456:488].rearrange("p (u n) -> p u n", u=4) for a in stat]
        crec = [sb(f"crec{s}", [P, 4, 8]) for s in range(STREAMS)]
        mem_w = [sb(f"mem_w{s}", [P, 2 * M]) for s in range(STREAMS)]
        rv = [sb(f"rv{s}", [P, S]) for s in range(STREAMS)]
        rl = [sb(f"rl{s}", [P, S]) for s in range(STREAMS)]
        ck_sb = [sb(f"ck_sb{s}", [P, M]) for s in range(STREAMS)]

        bank = [[ctx.enter_context(nc.psum_tensor(f"bank{s}_{i}", [P, 512], F32)) for i in range(4)]
                for s in range(STREAMS)]
        all_banks = [b for s in range(STREAMS) for b in bank[s]]

        def two(ap):
            return ap.rearrange("p (a n) -> p a n", a=2)

        const_in, w0_in, pos_in, type_in, media_in, vec_in = (
            sem(n) for n in ("const_in", "w0_in", "pos_in", "type_in", "media_in", "vec_in"))
        x_in = [sem(f"x_in{b}") for b in range(B)]
        mot_in, mot_ff_in, ca_in, ca_ff_in, out_sent = (
            sem(n) for n in ("mot_in", "mot_ff_in", "ca_in", "ca_ff_in", "out_sent"))
        pads_zero = sem("pads_zero")
        pro_pe, pro_act, pro_dve, pro_pool = (sem(n) for n in ("pro_pe", "pro_act", "pro_dve", "pro_pool"))
        done = {e: [sem(f"{e}_done{s}") for s in range(STREAMS)] for e in ("pe", "act", "dve", "pool")}
        sent = [sem(f"sent{s}") for s in range(STREAMS)]

        def load_mot(eng, w, first):
            n = 0
            for e, k in enumerate(("v", "l")):
                eng.dma_start(qkv[:, e], w[k + "_qkv"].rearrange("(k p) n -> p k n", p=P)).then_inc(mot_in, 16)
                eng.dma_start(dense[:, e], w[k + "_dense"].rearrange("(k p) n -> p k n", p=P)).then_inc(mot_in, 16)
            eng.dma_start(cq_w[:], w["cq_w"].rearrange("(k p) n -> p k n", p=P)).then_inc(mot_in, 16)
            eng.dma_start(ckv_w[:], w["ckv_w"]).then_inc(mot_in, 16)
            eng.dma_start(cd_w[:], w["cdense_w"]).then_inc(mot_in, 16)
            load_expert_cols(eng, gate_w, w["v_gate"], w["l_gate"], mot_in)

        def load_expert_cols(eng, dst, v, l, into):
            for e, src in enumerate((v, l)):
                rows = src.rearrange("(k p) n -> p k n", p=P)
                eng.dma_start(dst[:, :, e * FULL * P:(e + 1) * FULL * P], rows[:, :, 0:FULL * P]).then_inc(into, 16)
                at = 2 * FULL * P + e * M
                eng.dma_start(dst[:, :, at:at + TAIL], rows[:, :, FULL * P:INTER]).then_inc(into, 16)

        def load_mot_ff(eng, w):
            load_expert_cols(eng, up_w, w["v_up"], w["l_up"], mot_ff_in)
            for e, src in enumerate((w["v_down"], w["l_down"])):
                eng.dma_start(down_w[:, e * FULL:(e + 1) * FULL, :],
                              src[0:FULL * P, :].rearrange("(f p) n -> p f n", p=P)).then_inc(mot_ff_in, 16)
                eng.dma_start(down_w[e * M:e * M + TAIL, 2 * FULL, :], src[FULL * P:INTER, :]).then_inc(mot_ff_in, 16)

        MOT_DMAS, MOT_FF_DMAS, CA_DMAS, CA_FF_DMAS = 11, 8, 3, 2
        N_VEC = len(VECS) + 2

        PRO = ["w_mem_t", "ctx_t", "gate_t0", "gate_t1", "mem_t0", "mem_t1", "vec", "trig"] + [f"x{b}" for b in range(B)]
        pro_at = {n: i for i, n in enumerate(PRO)}
        ACT_FIRST = 1
        DVE_FIRST = 15

        def evacuated(name):
            i = pro_at[name]
            return (pro_act, ACT_FIRST + i // 2 + 1) if i % 2 == 0 else (pro_dve, DVE_FIRST + i // 2 + 1)

        PRO_DST = {
            "w_mem_t": lambda b: (w_mem_t[:], b[:, 0:D]),
            "ctx_t": lambda b: (ctx_t[:], b[:]),
            "gate_t0": lambda b: (w_gate_t[:, 0:2, :], two(b[:])),
            "gate_t1": lambda b: (w_gate_t[:, 2:4, :], two(b[:])),
            "mem_t0": lambda b: (mem_t[:, 0, :], b[:]),
            "mem_t1": lambda b: (mem_t[:, 1, :], b[:]),
            "vec": lambda b: (vec_t[:], b[:, 0:KT * len(VECS)]),
            "trig": lambda b: (cos_sin[:], two(b[:])),
            **{f"x{i}": (lambda b, i=i: (x_all[:, :, i * S:(i + 1) * S], two(b[:]))) for i in range(B)},
        }

        with nc.Block() as block:
            @block.sync
            def _(sp):
                sp.dma_start(const[:], const_d).then_inc(const_in, 16)
                sp.dma_start(w_mem_rows, fuse_w["W_mem"].rearrange("(k p) n -> p k n", p=P)).then_inc(w0_in, 16)
                sp.dma_start(ctx_rows, ctx_d.rearrange("b m c -> (b m) c").rearrange("(t p) c -> p t c", p=P)).then_inc(w0_in, 16)
                sp.dma_start(w_gate_rows, fuse_w["W_gate"].rearrange("(k p) n -> p k n", p=P)).then_inc(w0_in, 16)
                for b in range(B):
                    sp.dma_start(x_rows[b // 4][:, 2 * (b % 4):2 * (b % 4) + 2, :],
                                 x_d[b].rearrange("(t p) d -> p t d", p=P)).then_inc(x_in[b], 16)
                sp.wait_ge(pads_zero, 3)
                sp.wait_ge(pro_dve, DVE_FIRST)
                sp.wait_ge(*evacuated("trig"))
                load_mot(sp, mot_w[0], True)
                load_mot_ff(sp, mot_w[0])

            @block.scalar
            def _(act):
                act.dma_start(pos_i, pos_d[0, :].partition_broadcast(P)).then_inc(pos_in, 16)
                act.dma_start(type_i, type_d.rearrange("b n -> (b n)").partition_broadcast(P)).then_inc(type_in, 16)
                act.dma_start(media_u8[:], media_d.rearrange("b m -> (b m)").partition_broadcast(P)).then_inc(media_in, 16)
                for i, n in enumerate(VECS):
                    act.dma_start(vec_rows[KT * i:KT * (i + 1), :], (fuse_w | ca_w)[n].rearrange("(k p) -> k p", p=P))\
                       .then_inc(vec_in, 16)
                for i, n in enumerate(("attn_gate", "ff_gate")):
                    act.dma_start(ca_gate[:, i:i + 1], ca_w[n].partition_broadcast(P)).then_inc(vec_in, 16)
                act.wait_ge(vec_in, 16 * N_VEC)
                act.activation(ca_gate[:], ca_gate[:], ACT.Tanh).then_inc(pro_act, 1)
                for i, n in enumerate(PRO):
                    if i % 2 == 0:
                        act.wait_ge(pro_pe, i + 1)
                        dst, src = PRO_DST[n](all_banks[i % 8])
                        act.copy(dst, src).then_inc(pro_act, 1)
                        if n == "vec":
                            act.wait_ge(*evacuated("vec"))
                            act.mul(half_b[:], vec["b_gate"], 0.5)

            @block.vector
            def _(dve):
                n = 0
                dve.wait_ge(const_in, 16)
                dve.tensor_copy(ident_bf[:], ident).then_inc(pro_dve, 1)
                dve.memset(ones[:], 1.0).then_inc(pro_dve, 1)
                dve.memset(ones_bf[:], 1.0).then_inc(pro_dve, 1)
                dve.memset(mean_w[:], 1.0 / D).then_inc(pro_dve, 1)
                dve.wait_ge(pos_in, 16)
                dve.tensor_scalar(pos_f, pos_i, 0.0, float(S), ALU.is_lt, ALU.mult).then_inc(pro_dve, 1)
                dve.wait_ge(pro_dve, 5)
                dve.tensor_tensor(pos_g, pos_i, pos_f, ALU.add).then_inc(pro_dve, 1)
                dve.wait_ge(pro_dve, 6)
                dve.tensor_scalar(pos_f, pos_g, 0.0, S - 1.0, ALU.max, ALU.min).then_inc(pro_dve, 1)
                dve.wait_ge(pro_dve, 7)
                for t in range(TT):
                    dve.tensor_scalar(one_hot[:, t, :], pos_f, const[:, C_ROW + t:C_ROW + t + 1], None,
                                      ALU.is_equal).then_inc(pro_dve, 1)
                dve.wait_ge(type_in, 16)
                dve.tensor_scalar(type_one.rearrange("p b n -> p (b n)"), type_i, 1.0, None, ALU.is_equal).then_inc(pro_dve, 1)
                dve.memset(is_vis[:, :, S - 1:S], 0.0).then_inc(pro_dve, 1)
                dve.wait_ge(pro_dve, 10)
                dve.tensor_tensor(is_vis[:, :, 0:S - 1], type_one[:, :, 0:S - 1], type_one[:, :, 1:S],
                                  ALU.mult).then_inc(pro_dve, 1)
                dve.wait_ge(media_in, 16)
                dve.tensor_copy(media[:], media_u8[:]).then_inc(pro_dve, 1)
                dve.wait_ge(pro_dve, 13)
                dve.tensor_scalar(media_neg[:], media[0:1, :], -BIG, BIG, ALU.mult, ALU.add).then_inc(pro_dve, 1)
                dve.tensor_reduce(early[:], is_vis[0:1, :, 0:LATE], X, ALU.max).then_inc(pro_dve, 1)
                for i, n in enumerate(PRO):
                    if i % 2 == 1:
                        dve.wait_ge(pro_pe, i + 1)
                        dst, src = PRO_DST[n](all_banks[i % 8])
                        dve.tensor_copy(dst, src).then_inc(pro_dve, 1)

            @block.gpsimd
            def _(pool):
                pool.memset(neg_half[:], -0.5)
                pool.memset(causal_f[:], 0.0).then_inc(pro_pool, 1)
                pool.wait_ge(pro_pool, 1)
                pool.affine_select(out=causal_f[:], in_=causal_f[:], compare_op=ALU.is_ge, fill=BIG, base=0,
                                   pattern=[[-1, P]], channel_multiplier=1).then_inc(pro_pool, 1)
                pool.wait_ge(pro_pool, 2)
                pool.tensor_copy(causal[:], causal_f[:])
                for s in range(STREAMS):
                    pool.memset(zeroed[s], 0.0)
                pool.memset(down_w[:, 2 * FULL, :], 0.0).then_inc(pads_zero, 1)
                pool.wait_ge(pro_dve, 12)
                for w in (gate_w, up_w):
                    tail = w[:, :, 2 * FULL * P:NF * P].rearrange("p k (e n) -> p k e n", e=2)
                    pool.memset(tail[:, :, :, TAIL:M], 0.0).then_inc(pads_zero, 1)

            @block.tensor
            def _(pe):
                pe.wait_ge(const_in, 16)
                pe.wait_ge(w0_in, 48)
                for i, n in enumerate(PRO):
                    b = all_banks[i % 8]
                    if i >= 8:
                        pe.wait_ge(*evacuated(PRO[i - 8]))
                    if n == "w_mem_t":
                        for t in range(KT):
                            last = pe.transpose(b[:, t * P:(t + 1) * P], w_mem_rows[:, t, :], ident)
                    elif n == "ctx_t":
                        for t in range(4):
                            last = pe.transpose(b[:, t * P:(t + 1) * P], ctx_rows[:, t, :], ident)
                    elif n in ("gate_t0", "gate_t1"):
                        for f in range(2):
                            for t in range(KT):
                                src = w_gate_rows[:, t, (2 * (n == "gate_t1") + f) * P:][:, 0:P]
                                last = pe.transpose(b[:, f * D + t * P:f * D + (t + 1) * P], src, ident)
                    elif n in ("mem_t0", "mem_t1"):
                        pe.wait_ge(*evacuated("w_mem_t"))
                        pe.wait_ge(*evacuated("ctx_t"))
                        t = int(n[-1])
                        last = pe.matmul(b[:], w_mem_t[:, t * P:(t + 1) * P], ctx_t[:], start=True, stop=True)
                    elif n == "trig":
                        pe.wait_ge(pro_dve, 9)
                        for f in range(2):
                            for t in range(TT):
                                at = C_TRIG + 256 * t + 128 * f
                                last = pe.matmul(b[:, f * S:(f + 1) * S], const[:, at:at + P], one_hot[:, t, :],
                                                 start=(t == 0), stop=(t == TT - 1))
                    elif n == "vec":
                        pe.wait_ge(vec_in, 16 * N_VEC)
                        last = pe.transpose(b[:, 0:KT * len(VECS)], vec_rows[:], ident[0:KT * len(VECS), 0:KT * len(VECS)])
                    else:
                        e = int(n[1:])
                        pe.wait_ge(x_in[e], 16)
                        for k in range(KT):
                            for t in range(TT):
                                last = pe.transpose(b[:, k * S + t * P:k * S + (t + 1) * P],
                                                    x_rows[e // 4][:, 2 * (e % 4) + t, k * P:(k + 1) * P], ident)
                    last.then_inc(pro_pe, 1)

        def clear_and_join():
            sems = [q for e in ("pe", "act", "dve", "pool") for q in done[e]] + sent
            nums = [q.num for q in sems]
            assert nums == list(range(nums[0], nums[0] + len(nums)))
            nc.gpsimd.sem_clear(range(nums[0], nums[-1] + 1))
            nc.all_engine_barrier()

        def tokens(e):
            return bass.ds(e * S, S)

        def layer(pe_steps, act_steps, dve_steps, pool_steps):
            at_round = [0] * STREAMS
            return (Steps(done["pe"], pe_steps, at_round), Steps(done["act"], act_steps, at_round),
                    Steps(done["dve"], dve_steps, at_round), Steps(done["pool"], pool_steps, at_round))

        def stages(engine, part, order, K, last):
            for stage, s, round_, *which in order:
                K[1].round[s] = round_
                if stage == "take" and round_ > 0:
                    engine.wait_ge(*K[1].did(s, last, back=1))
                if stage in part:
                    part[stage](s, *which)

        def pe_sumsq(pe, K, s, n, out):
            pe.wait_ge(*K[1].did(s, "square", n))
            for t in range(TT):
                for k in range(KT):
                    last = pe.matmul(out[:, t:t + 1], sq[s][:, k, t * P:(t + 1) * P], mean_w[:, 0:1],
                                     start=(k == 0), stop=(k == KT - 1))
            last.then_inc(*K[0].does(s, "sumsq", n))

        def pe_spread(pe, K, s, n, out):
            pe.wait_ge(*K[3].did(s, "rstd", n))
            for t in range(TT):
                last = pe.transpose(out[:, t * P:(t + 1) * P], rstd[s][:, t:t + 1].to_broadcast([P, P]), ident)
            last.then_inc(*K[0].does(s, "spread", n))

        def dve_mean(dve, K, s, n, src, eps=RMS_EPS):
            dve.wait_ge(*K[0].did(s, "sumsq", n))
            dve.tensor_scalar(ms[s], src[:, 0:TT], eps, None, ALU.add).then_inc(*K[2].does(s, "mean", n))

        def pool_rstd(pool, K, s, n):
            pool.wait_ge(*K[2].did(s, "mean", n))
            pool.tensor_tensor(rstd[s], ms[s], neg_half[:], ALU.pow).then_inc(*K[3].does(s, "rstd", n))

        def dve_softmax_shift(dve, K, s, u, src, dst):
            dve.wait_ge(*K[0].did(s, "cs", u))
            b = src[:].rearrange("p (h m) -> p h m", m=M)
            dve.tensor_reduce(cmax[s][:, u, :], b, X, ALU.max).then_inc(*K[2].does(s, "cmax", u))
            dve.wait_ge(*K[2].did(s, "cmax", u))
            dve.tensor_tensor(dst.rearrange("p a n -> p (a n)").rearrange("p (h m) -> p h m", m=M), b,
                              cmax[s][:, u, :].unsqueeze(2).to_broadcast([P, 8, M]), ALU.subtract)\
               .then_inc(*K[2].does(s, "csub", u))

        def act_softmax_exp(act, K, s, u, buf, scale):
            act.wait_ge(*K[2].did(s, "csub", u))
            act.activation(buf, buf, ACT.Exp, scale=scale).then_inc(*K[1].does(s, "cexp", u))

        def dve_softmax_sum(dve, K, s, u, buf):
            dve.wait_ge(*K[1].did(s, "cexp", u))
            dve.tensor_reduce(csum[s][:, u, :], buf.rearrange("p a n -> p (a n)").rearrange("p (h m) -> p h m", m=M),
                              X, ALU.add).then_inc(*K[2].does(s, "csum", u))
            dve.wait_ge(*K[2].did(s, "csum", u))
            dve.reciprocal(crec[s][:, u, :], csum[s][:, u, :]).then_inc(*K[2].does(s, "crec", u))

        def pool_softmax_norm(pool, K, s, u, buf):
            pool.wait_ge(*K[2].did(s, "crec", u))
            b = buf.rearrange("p a n -> p (a n)").rearrange("p (h m) -> p h m", m=M)
            pool.tensor_tensor(b, b, crec[s][:, u, :].unsqueeze(2).to_broadcast([P, 8, M]), ALU.mult)\
                .then_inc(*K[3].does(s, "cnorm", u))

        def pe_softmax_t(pe, K, s, u, buf, out, ready):
            pe.wait_ge(*ready)
            flat = buf.rearrange("p a n -> p (a n)")
            for j in range(4):
                last = pe.transpose(out[:, j * P:(j + 1) * P], flat[:, j * P:(j + 1) * P], ident)
            last.then_inc(*K[0].does(s, "ct", u))

        def act_softmax_t(act, K, s, u, src, dst):
            act.wait_ge(*K[0].did(s, "ct", u))
            t, half = u // 2, u % 2
            act.copy(dst[:, 4 * half:4 * half + 4, t * P:(t + 1) * P], src[:].rearrange("p (j n) -> p j n", j=4))\
               .then_inc(*K[1].does(s, "ct", u))

        with nc.Fori(0, B // (STREAMS * ROUNDS)) as it:
            K = PE_, ACT_, DVE_, POOL_ = layer(FUSE_PE, FUSE_ACT, FUSE_DVE, FUSE_POOL)

            def fuse_example(s):
                return it * (STREAMS * ROUNDS) + ACT_.round[s] * STREAMS + s

            with nc.Block() as block:
                @block.gpsimd
                def _(pool):
                    def take(s):
                        pool.tensor_copy(mem_w[s][:, 0:M], ctx_t[:, bass.ds(fuse_example(s) * M, M)])\
                            .then_inc(*POOL_.does(s, "mem_in"))

                    def mean(s, n):
                        pool_rstd(pool, K, s, n)

                    stages(pool, {"take": take, "mean": mean}, FUSE_ORDER, K, "x_out")

                @block.tensor
                def _(pe):
                    def memory(s):
                        pe.wait_ge(*POOL_.did(s, "mem_in"))
                        pe.matmul(bank[s][0][0:M, 0:D], mem_w[s][:, 0:M], w_mem_t[:], start=True, stop=True)\
                          .then_inc(*PE_.does(s, "mem_rows"))

                    def scores(s):
                        pe.wait_ge(*DVE_.did(s, "x_in"))
                        for t in range(TT):
                            for k in range(KT):
                                last = pe.matmul(bank[s][1][:, t * M:(t + 1) * M], xw[s][:, k, t * P:(t + 1) * P],
                                                 mem_t[:, k, bass.ds(fuse_example(s) * M, M)], start=(k == 0), stop=(k == KT - 1))
                        last.then_inc(*PE_.does(s, "scores"))

                    def turn(s):
                        pe.wait_ge(*DVE_.did(s, "norm"))
                        for t in range(TT):
                            last = pe.transpose(bank[s][2][0:M, t * P:(t + 1) * P], f_p[s][:, t, :], ident)
                        last.then_inc(*PE_.does(s, "probs_t"))

                    def context(s):
                        pe.wait_ge(*ACT_.did(s, "probs_t"))
                        for t in range(KT):
                            last = pe.matmul(bank[s][3][:, t * S:(t + 1) * S], f_mem[s][0:M, t * P:(t + 1) * P],
                                             f_pt[s][0:M, :], start=True, stop=True)
                        last.then_inc(*PE_.does(s, "context"))

                    def gate(s):
                        pe.wait_ge(*ACT_.did(s, "context"))
                        for t in range(KT):
                            for k in range(2 * KT):
                                last = pe.matmul(bank[s][0][:, t * S:(t + 1) * S], w_gate_t[:, k, t * P:(t + 1) * P],
                                                 xw[s][:, k, :] if k < KT else f_mc[s][:, k - KT, :],
                                                 start=(k == 0), stop=(k == 2 * KT - 1))
                        last.then_inc(*PE_.does(s, "gate"))

                    def mean(s, n):
                        pe_sumsq(pe, K, s, n, bank[s][1])

                    def normed(s, n):
                        pe_spread(pe, K, s, n, bank[s][2])

                    stages(pe, {"memory": memory, "scores": scores, "turn": turn, "context": context, "gate": gate,
                                "mean": mean, "normed": normed}, FUSE_ORDER, K, "x_out")

                @block.scalar
                def _(act):
                    def memory(s):
                        act.wait_ge(*PE_.did(s, "mem_rows"))
                        act.copy(f_mem[s][0:M, :], bank[s][0][0:M, 0:D]).then_inc(*ACT_.does(s, "mem_rows"))

                    def scores(s):
                        act.wait_ge(*DVE_.did(s, "sub"))
                        act.activation(f_p[s], f_p[s], ACT.Exp, scale=D ** -0.5).then_inc(*ACT_.does(s, "exp"))

                    def turn(s):
                        act.wait_ge(*PE_.did(s, "probs_t"))
                        act.copy(f_pt[s][0:M, :], bank[s][2][0:M, 0:S]).then_inc(*ACT_.does(s, "probs_t"))

                    def context(s):
                        act.wait_ge(*PE_.did(s, "context"))
                        act.copy(f_mc[s], two(bank[s][3][:])).then_inc(*ACT_.does(s, "context"))

                    def gate(s):
                        act.wait_ge(*PE_.did(s, "gate"))
                        for t in range(KT):
                            act.activation(f_tanh[s][:, t, :], bank[s][0][:, t * S:(t + 1) * S], ACT.Tanh,
                                           bias=half_b[:, t:t + 1], scale=0.5).then_inc(*ACT_.does(s, f"gate{t}"))

                    def square(s):
                        act.wait_ge(*DVE_.did(s, "fused"))
                        act.activation(sq[s], xw[s], ACT.Square).then_inc(*ACT_.does(s, "square", 0))

                    def give(s):
                        act.wait_ge(*DVE_.did(s, "y1"))
                        act.copy(x_all[:, :, tokens(fuse_example(s))], yv[s]).then_inc(*ACT_.does(s, "x_out"))

                    stages(act, {"memory": memory, "scores": scores, "turn": turn, "context": context, "gate": gate,
                                 "square": square, "give": give}, FUSE_ORDER, K, "x_out")

                @block.vector
                def _(dve):
                    def take(s):
                        dve.tensor_copy(xw[s], x_all[:, :, tokens(fuse_example(s))]).then_inc(*DVE_.does(s, "x_in"))

                    def scores(s):
                        b = bank[s][1][:, 0:TT * M].rearrange("p (t m) -> p t m", t=TT)
                        dve.wait_ge(*PE_.did(s, "scores"))
                        dve.tensor_reduce(cmax[s][:, 0, 0:2], b, X, ALU.max).then_inc(*DVE_.does(s, "max"))
                        dve.wait_ge(*DVE_.did(s, "max"))
                        dve.tensor_tensor(f_p[s], b, cmax[s][:, 0, 0:2].unsqueeze(2).to_broadcast([P, TT, M]),
                                          ALU.subtract).then_inc(*DVE_.does(s, "sub"))

                    def sums(s):
                        dve.wait_ge(*ACT_.did(s, "exp"))
                        dve.tensor_reduce(csum[s][:, 0, 0:2], f_p[s], X, ALU.add).then_inc(*DVE_.does(s, "sum"))
                        dve.wait_ge(*DVE_.did(s, "sum"))
                        dve.reciprocal(crec[s][:, 0, 0:2], csum[s][:, 0, 0:2]).then_inc(*DVE_.does(s, "recip"))
                        dve.wait_ge(*DVE_.did(s, "recip"))
                        dve.tensor_tensor(f_p[s], f_p[s], crec[s][:, 0, 0:2].unsqueeze(2).to_broadcast([P, TT, M]),
                                          ALU.mult).then_inc(*DVE_.does(s, "norm"))

                    def gate(s):
                        dve.wait_ge(*ACT_.did(s, "gate1"))
                        dve.scalar_tensor_tensor(f_u[s], f_tanh[s], 1.0, f_mc[s], ALU.add, ALU.mult)\
                           .then_inc(*DVE_.does(s, "gated"))
                        dve.wait_ge(*DVE_.did(s, "gated"))
                        dve.scalar_tensor_tensor(xw[s], f_u[s], 0.5, xw[s], ALU.mult, ALU.add)\
                           .then_inc(*DVE_.does(s, "fused"))

                    def mean(s, n):
                        dve_mean(dve, K, s, n, bank[s][1])

                    def normed(s, n):
                        dve.wait_ge(*PE_.did(s, "spread", 0))
                        for t in range(KT):
                            dve.scalar_tensor_tensor(yv[s][:, t, :], xw[s][:, t, :], vec["fuse"][:, t:t + 1],
                                                     bank[s][2][:, 0:S], ALU.mult, ALU.mult)\
                               .then_inc(*DVE_.does(s, f"y{t}"))

                    stages(dve, {"take": take, "scores": scores, "sums": sums, "gate": gate, "mean": mean,
                                 "normed": normed}, FUSE_ORDER, K, "x_out")
            clear_and_join()

        def mot_layer(which, layer_index, before):
            w_in, w_post, w_cross = (vec[f"{n}{layer_index}"] for n in ("in", "post", "cross"))
            final = which == 1
            pe_names = MOT_PE + (names("out_t") if final else [])

            before()
            with nc.Fori(0, B // (STREAMS * ROUNDS)) as it:
                K = PE_, ACT_, DVE_, POOL_ = layer(pe_names, MOT_ACT, MOT_DVE, MOT_POOL)

                def example(s):
                    return it * (STREAMS * ROUNDS) + ACT_.round[s] * STREAMS + s

                with nc.Block() as block:
                    @block.gpsimd
                    def _(pool):
                        def take(s):
                            for i in range(2):
                                pool.tensor_copy(mem_w[s][:, i * M:(i + 1) * M], ctx_t[:, bass.ds(example(s) * M, M)])\
                                    .then_inc(*POOL_.does(s, f"mem_in{i}"))

                        def mean(s, n):
                            pool_rstd(pool, K, s, n)

                        def rotary(n, src, dst):
                            def of(s):
                                pool.wait_ge(*ACT_.did(s, n))
                                pool.tensor_tensor(dst[s], src[s], cos_sin[:, 0:1, :].to_broadcast([P, KT, S]), ALU.mult)\
                                    .then_inc(*POOL_.does(s, n + "c"))
                            return of

                        def one_head(s, h):
                            if h >= QM:
                                pool.wait_ge(*PE_.did(s, "s", h - QM))
                            pool.tensor_scalar(q_one[s][:, h % QM, :], q_sb[s][:, h // 8, :],
                                               const[:, C_H8 + h % 8:C_H8 + h % 8 + 1], None, ALU.mult)\
                                .then_inc(*POOL_.does(s, "qm", h))

                        def first_heads(s):
                            if s in QM_ON_POOL:
                                pool.wait_ge(*DVE_.did(s, "q2"))
                                for h in range(LEAD):
                                    one_head(s, h)

                        def attend(s, h):
                            if s in QM_ON_POOL and h + LEAD < NH:
                                one_head(s, h + LEAD)

                        def cross_in(s):
                            pool.wait_ge(*ACT_.did(s, "ck"))
                            pool.tensor_tensor(c_kd[s], ck_sb[s][:].unsqueeze(1).to_broadcast([P, NH, M]),
                                               const[:, C_H16:C_H16 + NH].unsqueeze(2).to_broadcast([P, NH, M]), ALU.mult)\
                                .then_inc(*POOL_.does(s, "ckd"))

                        part = {"take": take, "mean": mean, "q": rotary("q", q_sb, qc), "k": rotary("k", k_sb, kc),
                                "rot_k": first_heads, "attend": attend,
                                "cross_in": cross_in}
                        stages(pool, part, MOT_ORDER, K, "x_out")

                    @block.tensor
                    def _(pe):
                        turned_by = [ACT_ if s in PT_ON_ACT else DVE_ for s in range(STREAMS)]
                        has_early = [[pe.value_load(early[0:1, bass.ds(it * (STREAMS * ROUNDS) + r * STREAMS + s, 1)])
                                      for r in range(ROUNDS)] for s in range(STREAMS)]

                        def to_experts(s, out, w, at, v_ready):
                            def first_expert(lo, hi, stop):
                                for t in range(KT):
                                    for k in range(KT):
                                        last = pe.matmul(out[:, t * S + lo:t * S + hi],
                                                         w[:, 0, k, at + t * P:at + (t + 1) * P], yv[s][:, k, lo:hi],
                                                         start=False, stop=(stop and k == KT - 1), skip_group_check=True)
                                return last

                            for t in range(KT):
                                for k in range(KT):
                                    pe.matmul(out[:, t * S:(t + 1) * S], w[:, 1, k, at + t * P:at + (t + 1) * P],
                                              yl[s][:, k, :], start=(t == k == 0), stop=False, skip_group_check=True)
                            pe.wait_ge(*v_ready)
                            with pe.If(has_early[s][PE_.round[s]]):
                                first_expert(0, LATE, False)
                            return first_expert(LATE, S, True)

                        def mean(s, n):
                            pe_sumsq(pe, K, s, n, bank[s][0 if n == 0 else 2])

                        def normed(s, n):
                            pe_spread(pe, K, s, n, bank[s][1 if n == 0 else 3])

                        def q(s):
                            if s == PE_.round[s] == 0:
                                pe.wait_ge(mot_in, 16 * MOT_DMAS * (which + 1))
                            pe.wait_ge(*DVE_.did(s, "yl1", 0))
                            to_experts(s, bank[s][0], qkv, 0, DVE_.did(s, "yv1", 0)).then_inc(*PE_.does(s, "q"))

                        def k(s):
                            to_experts(s, bank[s][2], qkv, D, DVE_.did(s, "yv1", 0)).then_inc(*PE_.does(s, "k"))

                        def v(s):
                            def rows(y, e, t, start, stop):
                                for k in range(KT):
                                    last = pe.matmul(bank[s][3][:, t * D:(t + 1) * D], y[s][:, k, t * P:(t + 1) * P],
                                                     qkv[:, e, k, 2 * D:3 * D], start=(start and k == 0),
                                                     stop=(stop and k == KT - 1), skip_group_check=True)
                                return last

                            rows(yl, 1, 0, True, False)
                            with pe.If(has_early[s][PE_.round[s]]):
                                rows(yv, 0, 0, False, False)
                            rows(yl, 1, 1, True, False)
                            rows(yv, 0, 1, False, True).then_inc(*PE_.does(s, "v"))

                        def rotate(n, src, to):
                            def of(s):
                                pe.wait_ge(*ACT_.did(s, n))
                                for t in range(KT):
                                    last = pe.matmul(bank[s][to][:, t * S:(t + 1) * S], const[:, C_ROT:C_ROT + P],
                                                     src[s][:, t, :], start=True, stop=True)
                                last.then_inc(*PE_.does(s, f"rot_{n}"))
                            return of

                        def scores(s, h):
                            out = bank[s][2 + h % 2]
                            if h == 0:
                                pe.wait_ge(*ACT_.did(s, "v1"))
                                pe.wait_ge(*DVE_.did(s, "k2"))
                            pe.wait_ge(*(POOL_ if s in QM_ON_POOL else ACT_).did(s, "qm", h))
                            if h >= 2:
                                pe.wait_ge(*ACT_.did(s, "exp1", h - 2))
                            for q in range(TT):
                                pe.matmul(out[:, P * q:P + S * q], q_one[s][:, h % QM, q * P:(q + 1) * P],
                                          k_sb[s][:, h // 8, 0:P * (q + 1)], start=(q == 0), stop=False,
                                          skip_group_check=True)
                            for q in range(TT):
                                last = pe.matmul(out[:, 2 * P * q:P + 2 * P * q], ident_bf[:], causal[:],
                                                 start=False, stop=(q == TT - 1), skip_group_check=True)
                            last.then_inc(*PE_.does(s, "s", h))

                        def transposes(s, h):
                            pe.wait_ge(*ACT_.did(s, "exp1", h))
                            if h >= 1:
                                pe.wait_ge(*turned_by[s].did(s, "pt", h - 1))
                            for j in range(3):
                                last = pe.transpose(bank[s][1][:, j * P:(j + 1) * P], probs[s][:, h % 2, j * P:(j + 1) * P], ident)
                            last.then_inc(*PE_.does(s, "t", h))

                        def values(s, h):
                            t, r = h // 8, 32 * (h % 8 // 2)
                            pe.wait_ge(*turned_by[s].did(s, "pt", h))
                            out = bank[s][0][r:r + 32, t * S:(t + 1) * S]
                            pt = probs_t[s][:, h % 2, :]
                            pe.matmul(out, v_pad[s][:, 0, h, :], pt[:, 0:S], start=(h % 2 == 0), stop=False,
                                      skip_group_check=True)
                            pe.matmul(out[:, P:S], v_pad[s][:, 1, h, :], pt[:, S:S + P], start=False, stop=(h % 2 == 1),
                                      skip_group_check=True).then_inc(*PE_.does(s, "pv", h))

                        def attend(s, h):
                            if h < NH:
                                scores(s, h)
                            if 0 <= h - LAG1 < NH:
                                transposes(s, h - LAG1)
                            if 0 <= h - LAG2 < NH:
                                values(s, h - LAG2)

                        def sums_spread(s):
                            pe.wait_ge(*ACT_.did(s, "rexp"))
                            for k in range(KT):
                                for q in range(TT):
                                    last = pe.transpose(bank[s][1][:, k * S + q * P:k * S + (q + 1) * P],
                                                        kc[s][:, q, k * P:(k + 1) * P], ident)
                            last.then_inc(*PE_.does(s, "rinv"))

                        def project(s):
                            pe.wait_ge(*DVE_.did(s, "cl"))
                            to_experts(s, bank[s][1], dense, 0, DVE_.did(s, "cv")).then_inc(*PE_.does(s, "dense"))

                        def cross_in(s):
                            b = bank[s]
                            pe.wait_ge(*DVE_.did(s, "y1", 1))
                            for k in range(KT):
                                last = pe.matmul(b[0][:, 0:S], cq_w[:, k, :], yv[s][:, k, :], start=(k == 0), stop=(k == KT - 1))
                            last.then_inc(*PE_.does(s, "cq"))
                            pe.wait_ge(*POOL_.did(s, "mem_in1"))
                            pe.matmul(b[2][:, 0:M], ckv_w[:, 0:C], mem_w[s][:, 0:M], start=True, stop=True)\
                              .then_inc(*PE_.does(s, "ck"))
                            pe.matmul(b[1][:, 0:C], mem_w[s][:], ckv_w[:, C:2 * C], start=True, stop=True)\
                              .then_inc(*PE_.does(s, "cv"))

                        def cross_scores(s, u):
                            if u == 0:
                                pe.wait_ge(*ACT_.did(s, "cq"))
                                pe.wait_ge(*POOL_.did(s, "ckd"))
                                pe.wait_ge(*DVE_.did(s, "cv", 3))
                            pe.matmul(bank[s][u][:], c_q[s][:, (u // 2) * P:(u // 2 + 1) * P],
                                      c_kd[s][:, 8 * (u % 2):8 * (u % 2) + 8, :], start=True, stop=True)\
                              .then_inc(*PE_.does(s, "cs", u))

                        def cross_turn(s, u):
                            pe_softmax_t(pe, K, s, u, c_p[u][s], bank[s][u], ACT_.did(s, "cexp", u))

                        def cross_values(s):
                            pe.wait_ge(*ACT_.did(s, "ct", 3))
                            for i in range(2):
                                for j in range(8):
                                    r = 32 * (j // 2)
                                    at = C_PAIR + 32 * (j % 2)
                                    last = pe.matmul(bank[s][0][r:r + 32, i * S:(i + 1) * S],
                                                     cv_pad[s][:, j, :] if i == 0 else const[:, at:at + 32],
                                                     c_t[s][:, j, :], start=(j % 2 == 0), stop=(j % 2 == 1),
                                                     skip_group_check=True)
                            last.then_inc(*PE_.does(s, "cpv"))

                        def cross_project(s):
                            pe.wait_ge(*DVE_.did(s, "cctx"))
                            for t in range(KT):
                                last = pe.matmul(bank[s][1][:, t * S:(t + 1) * S], cd_w[:, t * P:(t + 1) * P], c_ctx[s],
                                                 start=True, stop=True)
                            last.then_inc(*PE_.does(s, "cdense"))

                        def up(s, i):
                            f = FF_ORDER[i]
                            b = bank[s][i % 3]
                            if i == 0:
                                pe.wait_ge(mot_ff_in, 16 * MOT_FF_DMAS * (which + 1))
                            if i < 2:
                                pe.wait_ge(*DVE_.did(s, ("yl1", "yv1")[i], 2))
                            if i >= 3:
                                pe.wait_ge(*DVE_.did(s, "hid", i - 3))

                            def columns(y, lo, hi):
                                for j, w in enumerate((gate_w, up_w)):
                                    for k in range(KT):
                                        last = pe.matmul(b[:, j * S + lo:j * S + hi], w[:, k, f * P:(f + 1) * P],
                                                         y[s][:, k, lo:hi], start=(k == 0), stop=(k == KT - 1))
                                return last

                            if f < FULL:
                                with pe.If(has_early[s][PE_.round[s]]):
                                    columns(yv, 0, LATE)
                                last = columns(yv, LATE, S)
                            elif f < 2 * FULL:
                                last = columns(yl, 0, S)
                            else:
                                for m, w in enumerate((gate_w, up_w)):
                                    for j, y in enumerate((yv[s], yl[s])):
                                        for k in range(KT):
                                            at = f * P + j * M
                                            last = pe.matmul(b[j * M:(j + 1) * M, m * S:(m + 1) * S], w[:, k, at:at + M],
                                                             y[:, k, :], start=(k == 0), stop=(k == KT - 1))
                            last.then_inc(*PE_.does(s, "up", i))

                        def down(s, i):
                            f = FF_ORDER[i]
                            pe.wait_ge(*DVE_.did(s, "hid", i))

                            def columns(lo, hi):
                                for t in range(KT):
                                    last = pe.matmul(bank[s][3][:, t * S + lo:t * S + hi], down_w[:, f, t * P:(t + 1) * P],
                                                     hid[s][:, f, lo:hi], start=(i == t == 0), stop=(i == NF - 1),
                                                     skip_group_check=True)
                                return last

                            if f < FULL:
                                with pe.If(has_early[s][PE_.round[s]]):
                                    columns(0, LATE)
                                columns(LATE, S)
                            else:
                                last = columns(0, S)
                            if i == NF - 1:
                                last.then_inc(*PE_.does(s, "down"))

                        def give(s):
                            if final:
                                pe.wait_ge(*DVE_.did(s, "x4"))
                                for t in range(TT):
                                    for k in range(KT):
                                        last = pe.transpose(bank[s][2][:, t * D + k * P:t * D + (k + 1) * P],
                                                            xw[s][:, k, t * P:(t + 1) * P], ident)
                                last.then_inc(*PE_.does(s, "out_t"))

                        part = {"mean": mean, "normed": normed, "q": q, "k": k, "v": v,
                                "rot_q": rotate("q", q_sb, 1), "rot_k": rotate("k", k_sb, 0), "attend": attend,
                                "sums_spread": sums_spread, "project": project, "cross_in": cross_in,
                                "cross_scores": cross_scores, "cross_turn": cross_turn, "cross_values": cross_values,
                                "cross_project": cross_project, "up": up, "down": down, "give": give}
                        stages(pe, part, MOT_ORDER, K, "x_out")

                    @block.scalar
                    def _(act):
                        def take(s):
                            act.activation(sq[s], x_all[:, :, tokens(example(s))], ACT.Square)\
                               .then_inc(*ACT_.does(s, "square", 0))

                        def square(s, n, ready):
                            act.wait_ge(*ready)
                            act.activation(sq[s], xw[s], ACT.Square).then_inc(*ACT_.does(s, "square", n))

                        def rows(n, src, dst):
                            def of(s):
                                act.wait_ge(*PE_.did(s, n))
                                act.copy(dst[s], two(bank[s][src][:])).then_inc(*ACT_.does(s, n))
                            return of

                        def v(s):
                            act.wait_ge(*PE_.did(s, "v"))
                            v = bank[s][3][:].rearrange("p (t h d) -> p t h d", t=TT, h=NH)
                            for i in range(2):
                                for t in range(TT):
                                    last = act.copy(v_pad[s][:, t, i::2, i * HD:(i + 1) * HD], v[:, t, i::2, :])
                                last.then_inc(*ACT_.does(s, f"v{i}"))

                        def one_head(s, h):
                            if h >= QM:
                                act.wait_ge(*PE_.did(s, "s", h - QM))
                            act.activation(q_one[s][:, h % QM, :], q_sb[s][:, h // 8, :], ACT.Copy,
                                           scale=const[:, C_H8 + h % 8:C_H8 + h % 8 + 1]).then_inc(*ACT_.does(s, "qm", h))

                        def first_heads(s):
                            if s in QM_ON_POOL:
                                return
                            act.wait_ge(*DVE_.did(s, "q2"))
                            for h in range(LEAD):
                                one_head(s, h)

                        def turned(s, h):
                            act.wait_ge(*PE_.did(s, "t", h))
                            if h >= 2:
                                act.wait_ge(*PE_.did(s, "pv", h - 2))
                            act.copy(probs_t[s][:, h % 2, :], bank[s][1][:, 0:384]).then_inc(*ACT_.does(s, "pt", h))

                        def attend(s, h):
                            if h >= NH:
                                if s in PT_ON_ACT and h - LAG1 < NH:
                                    turned(s, h - LAG1)
                                return
                            b = bank[s][2 + h % 2]
                            if h >= 2:
                                act.wait_ge(*PE_.did(s, "t", h - 2))
                            act.wait_ge(*DVE_.did(s, "max1", h))
                            for q, (lo, hi) in enumerate(((0, P), (P, 3 * P))):
                                act.activation(probs[s][:, h % 2, lo:hi], b[:, lo:hi], ACT.Exp,
                                               bias=negmax[s][:, q, h:h + 1], accum_out=sums[s][:, q, h:h + 1])\
                                   .then_inc(*ACT_.does(s, f"exp{q}", h))
                            if s not in QM_ON_POOL and h + LEAD < NH:
                                one_head(s, h + LEAD)
                            if s in PT_ON_ACT and h >= LAG1:
                                turned(s, h - LAG1)

                        def sums_out(s):
                            act.wait_ge(*DVE_.did(s, "rinv"))
                            act.copy(kc[s].rearrange("p q (h d) -> p q h d", d=HD),
                                     rinv_v[s].unsqueeze(3).to_broadcast([P, TT, NH, HD])).then_inc(*ACT_.does(s, "rexp"))

                        def sums_spread(s):
                            act.wait_ge(*PE_.did(s, "rinv"))
                            act.copy(kr[s], two(bank[s][1][:])).then_inc(*ACT_.does(s, "rinv"))

                        def project(s):
                            square(s, 1, DVE_.did(s, "x2"))

                        def cross_in(s):
                            act.wait_ge(*PE_.did(s, "cq"))
                            act.copy(c_q[s], bank[s][0][:, 0:S]).then_inc(*ACT_.does(s, "cq"))
                            act.wait_ge(*PE_.did(s, "ck"))
                            act.copy(ck_sb[s][:], bank[s][2][:, 0:M]).then_inc(*ACT_.does(s, "ck"))

                        def cross_scores(s, u):
                            act_softmax_exp(act, K, s, u, c_p[u][s], CHD ** -0.5)

                        def cross_turn(s, u):
                            act_softmax_t(act, K, s, u, bank[s][u], c_t[s])

                        def cross_project(s):
                            square(s, 2, DVE_.did(s, "x3"))

                        def up(s, i):
                            act.wait_ge(*PE_.did(s, "up", i))
                            if i >= 2:
                                act.wait_ge(*DVE_.did(s, "silu", i - 2))
                            act.activation(tanh_b[s][:, i % 2, :], bank[s][i % 3][:, 0:S], ACT.Tanh, scale=0.5)\
                               .then_inc(*ACT_.does(s, "tanh", i))

                        def give(s):
                            if final:
                                act.wait_ge(*PE_.did(s, "out_t"))
                                act.copy(yv[s], two(bank[s][2][:])).then_inc(*ACT_.does(s, "x_out"))
                            else:
                                act.wait_ge(*DVE_.did(s, "x4"))
                                act.copy(x_all[:, :, tokens(example(s))], xw[s]).then_inc(*ACT_.does(s, "x_out"))

                        part = {"take": take, "q": rows("q", 0, q_sb), "k": rows("k", 2, k_sb), "v": v, "rot_k": first_heads,
                                "attend": attend, "sums_out": sums_out, "sums_spread": sums_spread, "project": project,
                                "cross_in": cross_in, "cross_scores": cross_scores, "cross_turn": cross_turn,
                                "cross_project": cross_project, "up": up, "give": give}
                        stages(act, part, MOT_ORDER, K, "x_out")

                    @block.vector
                    def _(dve):
                        def take(s):
                            dve.tensor_copy(xw[s], x_all[:, :, tokens(example(s))]).then_inc(*DVE_.does(s, "x_in"))

                        def mean(s, n):
                            dve_mean(dve, K, s, n, bank[s][0 if n == 0 else 2])

                        def normed(s, n):
                            w = (w_in, w_cross, w_post)[n]
                            b = bank[s][1 if n == 0 else 3][:, 0:S]
                            dve.wait_ge(*PE_.did(s, "spread", n))
                            if n == 1:
                                for t in range(KT):
                                    dve.scalar_tensor_tensor(yv[s][:, t, :], xw[s][:, t, :], w[:, t:t + 1], b,
                                                             ALU.mult, ALU.mult).then_inc(*DVE_.does(s, f"y{t}", n))
                                return
                            if n == 0:
                                dve.wait_ge(*DVE_.did(s, "x_in"))
                                if final and DVE_.round[s] > 0:
                                    dve.wait_ge(sent[s], 16 * DVE_.round[s])
                            dve.tensor_tensor(rv[s][:], b, is_vis[:, bass.ds(example(s), 1), :].rearrange("p a n -> p (a n)"),
                                              ALU.mult).then_inc(*DVE_.does(s, "rv", n))
                            dve.wait_ge(*DVE_.did(s, "rv", n))
                            dve.tensor_tensor(rl[s][:], b, rv[s][:], ALU.subtract).then_inc(*DVE_.does(s, "rl", n))
                            dve.wait_ge(*DVE_.did(s, "rl", n))
                            for m, dst, r in (("yl", yl, rl), ("yv", yv, rv)):
                                for t in range(KT):
                                    dve.scalar_tensor_tensor(dst[s][:, t, :], xw[s][:, t, :], w[:, t:t + 1], r[s][:],
                                                             ALU.mult, ALU.mult).then_inc(*DVE_.does(s, f"{m}{t}", n))

                        def rotary(n, src, tmp, cosine, dst):
                            def of(s):
                                dve.wait_ge(*PE_.did(s, f"rot_{n}"))
                                dve.tensor_tensor(tmp[s], two(bank[s][src][:]), cos_sin[:, 1:2, :].to_broadcast([P, KT, S]),
                                                  ALU.mult).then_inc(*DVE_.does(s, n + "r"))
                                dve.wait_ge(*POOL_.did(s, n + "c"))
                                dve.wait_ge(*DVE_.did(s, n + "r"))
                                dve.tensor_tensor(dst[s], cosine[s], tmp[s], ALU.add).then_inc(*DVE_.does(s, n + "2"))
                            return of

                        def attend(s, h):
                            if h < NH:
                                b = bank[s][2 + h % 2]
                                dve.wait_ge(*PE_.did(s, "s", h))
                                for q, (lo, hi) in enumerate(((0, P), (P, 3 * P))):
                                    dve.tensor_reduce(negmax[s][:, q, h:h + 1], b[:, lo:hi], X, ALU.max, negate=True)\
                                       .then_inc(*DVE_.does(s, f"max{q}", h))
                            turned = h - LAG1
                            if s not in PT_ON_ACT and 0 <= turned < NH:
                                dve.wait_ge(*PE_.did(s, "t", turned))
                                if turned >= 2:
                                    dve.wait_ge(*PE_.did(s, "pv", turned - 2))
                                dve.tensor_copy(probs_t[s][:, turned % 2, :], bank[s][1][:, 0:384])\
                                   .then_inc(*DVE_.does(s, "pt", turned))

                        def sums_out(s):
                            dve.wait_ge(*ACT_.did(s, "exp1", NH - 1))
                            dve.reciprocal(rinv_v[s], sums[s]).then_inc(*DVE_.does(s, "rinv"))

                        def context(s):
                            dve.wait_ge(*PE_.did(s, "pv", NH - 1))
                            dve.wait_ge(*ACT_.did(s, "rinv"))
                            dve.tensor_tensor(q_sb[s], two(bank[s][0][:]), kr[s], ALU.mult).then_inc(*DVE_.does(s, "ctx"))
                            dve.wait_ge(*DVE_.did(s, "ctx"))
                            vis = is_vis[:, bass.ds(example(s), 1), :].to_broadcast([P, KT, S])
                            dve.tensor_tensor(yv[s], q_sb[s], vis, ALU.mult).then_inc(*DVE_.does(s, "cv"))
                            dve.wait_ge(*DVE_.did(s, "cv"))
                            dve.tensor_tensor(yl[s], q_sb[s], yv[s], ALU.subtract).then_inc(*DVE_.does(s, "cl"))

                        def project(s):
                            dve.wait_ge(*PE_.did(s, "dense"))
                            dve.tensor_tensor(xw[s], two(bank[s][1][:]), xw[s], ALU.add).then_inc(*DVE_.does(s, "x2"))

                        def cross_in(s):
                            dve.wait_ge(*PE_.did(s, "cv"))
                            src = bank[s][1][:, 0:C].rearrange("p (g n) -> p g n", g=4)
                            dst = cv_pad[s].rearrange("p (g q) n -> p g q n", g=4)
                            for q in range(2):
                                for i in range(2):
                                    at = q * 2 * CHD + i * CHD
                                    dve.tensor_copy(dst[i * M:(i + 1) * M, :, q, at:at + CHD],
                                                    src[i * M:(i + 1) * M, :, at:at + CHD])\
                                       .then_inc(*DVE_.does(s, "cv", 2 * q + i))

                        def cross_scores(s, u):
                            dve_softmax_shift(dve, K, s, u, bank[s][u], c_p[u][s])

                        def cross_values(s):
                            dve.wait_ge(*PE_.did(s, "cpv"))
                            dve.reciprocal(rv[s][:], bank[s][0][:, S:2 * S]).then_inc(*DVE_.does(s, "crec"))
                            dve.wait_ge(*DVE_.did(s, "crec"))
                            dve.tensor_tensor(c_ctx[s], bank[s][0][:, 0:S], rv[s][:], ALU.mult).then_inc(*DVE_.does(s, "cctx"))

                        def cross_project(s):
                            dve.wait_ge(*PE_.did(s, "cdense"))
                            dve.tensor_tensor(xw[s], two(bank[s][1][:]), xw[s], ALU.add).then_inc(*DVE_.does(s, "x3"))

                        def up(s, i):
                            b = bank[s][i % 3]
                            dve.wait_ge(*ACT_.did(s, "tanh", i))
                            dve.scalar_tensor_tensor(silu_b[s][:, i % 2, :], tanh_b[s][:, i % 2, :], 1.0, b[:, 0:S],
                                                     ALU.add, ALU.mult).then_inc(*DVE_.does(s, "silu", i))
                            dve.wait_ge(*DVE_.did(s, "silu", i))
                            dve.tensor_tensor(hid[s][:, FF_ORDER[i], :], silu_b[s][:, i % 2, :], b[:, S:2 * S], ALU.mult)\
                               .then_inc(*DVE_.does(s, "hid", i))

                        def give(s):
                            dve.wait_ge(*PE_.did(s, "down"))
                            dve.scalar_tensor_tensor(xw[s], two(bank[s][3][:]), 0.5, xw[s], ALU.mult, ALU.add)\
                               .then_inc(*DVE_.does(s, "x4"))

                        part = {"take": take, "mean": mean, "normed": normed, "rot_q": rotary("q", 1, qr, qc, q_sb),
                                "rot_k": rotary("k", 0, kr, kc, k_sb), "attend": attend, "sums_out": sums_out,
                                "context": context, "project": project, "cross_in": cross_in,
                                "cross_scores": cross_scores, "cross_values": cross_values,
                                "cross_project": cross_project, "up": up, "give": give}
                        stages(dve, part, MOT_ORDER, K, "x_out")

                    if final:
                        @block.sync
                        def _(sp):
                            for stage, s, round_, *_which in MOT_ORDER:
                                if stage == "give":
                                    ACT_.round[s] = round_
                                    sp.wait_ge(*ACT_.did(s, "x_out"))
                                    sp.dma_start(out_d[bass.ds(example(s), 1)].rearrange("a (t p) d -> p (a t) d", p=P),
                                                 yv[s]).then_inc(sent[s], 16)
                            for s in range(STREAMS):
                                sp.wait_ge(sent[s], 16 * ROUNDS)
                clear_and_join()

        def before_first():
            with nc.Block() as block:
                @block.sync
                def _(sp):
                    sp.dma_start(wq[:], ca_w["Wq"].rearrange("(k p) n -> p k n", p=P)).then_inc(ca_in, 16)
                    sp.dma_start(wkv[:], ca_w["Wkv"]).then_inc(ca_in, 16)
                    sp.dma_start(wo[:], ca_w["Wo"].rearrange("(k p) n -> p k n", p=P)).then_inc(ca_in, 16)

        mot_layer(0, 1, before_first)

        with nc.Block() as block:
            @block.sync
            def _(sp):
                sp.dma_start(w1, ca_w["W1"].rearrange("(k p) n -> p k n", p=P)).then_inc(ca_ff_in, 16)
                sp.dma_start(w2, ca_w["W2"].rearrange("(k p) n -> p k n", p=P)).then_inc(ca_ff_in, 16)
                load_mot(sp, mot_w[1], False)

            @block.gpsimd
            def _(pool):
                for s in range(STREAMS):
                    pool.memset(zeroed[s], 0.0)

        with nc.Fori(0, B // (STREAMS * ROUNDS)) as it:
            K = PE_, ACT_, DVE_, POOL_ = layer(CA_PE, CA_ACT, CA_DVE, CA_POOL)

            def ca_example(s):
                return it * (STREAMS * ROUNDS) + ACT_.round[s] * STREAMS + s

            with nc.Block() as block:
                @block.gpsimd
                def _(pool):
                    def take(s):
                        for i in range(2):
                            pool.tensor_copy(mem_w[s][:, i * M:(i + 1) * M], ctx_t[:, bass.ds(ca_example(s) * M, M)])\
                                .then_inc(*POOL_.does(s, f"mem_in{i}"))

                    def mean(s, n):
                        pool_rstd(pool, K, s, n)

                    def sums(s, u):
                        pool_softmax_norm(pool, K, s, u, g_p[u][s])

                    stages(pool, {"take": take, "mean": mean, "sums": sums}, CA_ORDER, K, "x_out")

                @block.tensor
                def _(pe):
                    def center(s, n):
                        pe.wait_ge(*DVE_.did(s, ("x_in", "x2")[n]))
                        for k in range(KT):
                            last = pe.matmul(bank[s][n][:, 0:S], mean_w[:], xw[s][:, k, :], start=(k == 0), stop=(k == KT - 1))
                        last.then_inc(*PE_.does(s, "mu", n))

                    def mean(s, n):
                        pe_sumsq(pe, K, s, n, bank[s][1 + n])

                    def normed(s, n):
                        pe_spread(pe, K, s, n, bank[s][2 + n])

                    def q(s, u):
                        if u == 0:
                            if s == PE_.round[s] == 0:
                                pe.wait_ge(ca_in, 16 * CA_DMAS)
                            pe.wait_ge(*ACT_.did(s, "y1", 0))
                        for j in range(2):
                            for k in range(KT):
                                at = (2 * u + j) * P
                                last = pe.matmul(bank[s][(3 + u) % 4][:, j * S:(j + 1) * S], wq[:, k, at:at + P],
                                                 yv[s][:, k, :], start=(k == 0), stop=(k == KT - 1))
                        last.then_inc(*PE_.does(s, "q", u))

                    def memory(s):
                        b = bank[s]
                        pe.wait_ge(*POOL_.did(s, "mem_in1"))
                        pe.wait_ge(*ACT_.did(s, "q", 0))
                        for j in range(GT):
                            last = pe.matmul(b[3][:, j * M:(j + 1) * M], wkv[:, j * P:(j + 1) * P], mem_w[s][:, 0:M],
                                             start=True, stop=True)
                        last.then_inc(*PE_.does(s, "k"))
                        for c in range(2):
                            pe.wait_ge(*ACT_.did(s, "q", 1 + c))
                            pe.matmul(b[c][:], mem_w[s][:], wkv[:, INNER + c * 512:INNER + (c + 1) * 512],
                                      start=True, stop=True).then_inc(*PE_.does(s, f"v{c}"))

                    def scores(s, u):
                        out = bank[s][(2 + u) % 4]
                        if u == 0:
                            pe.wait_ge(*ACT_.did(s, "q", 3))
                            pe.wait_ge(*DVE_.did(s, "v11"))
                        t, half = u // 2, u % 2
                        for j in range(4):
                            pe.matmul(out[:, j * P:(j + 1) * P], g_q[s][:, 4 * half + j, t * P:(t + 1) * P],
                                      k_diag[s][:, 4 * half + j], start=(j == 0), stop=False, skip_group_check=True)
                        masked = media_neg[:, bass.ds(ca_example(s) * M, M)].unsqueeze(1).to_broadcast([1, 8, M])
                        pe.matmul(out[:], ones_bf[:], masked, start=False, stop=True, skip_group_check=True)\
                          .then_inc(*PE_.does(s, "cs", u))

                    def turn(s, u):
                        pe_softmax_t(pe, K, s, u, g_p[u][s], bank[s][(2 + u) % 4], POOL_.did(s, "cnorm", u))

                    def values(s, u):
                        out = bank[s][(2 + u) % 4]
                        pe.wait_ge(*ACT_.did(s, "ct", 3))
                        for j in range(2):
                            last = pe.matmul(out[:, j * S:(j + 1) * S], v_diag[s][:, 2 * u + j, :], g_t[s][:, 2 * u + j, :],
                                             start=True, stop=True)
                        last.then_inc(*PE_.does(s, "cpv", u))

                    def project(s, k):
                        pe.wait_ge(*ACT_.did(s, "cpv", 3 if k == 0 else k // 2))
                        for t in range(KT):
                            last = pe.matmul(bank[s][0][:, t * S:(t + 1) * S], wo[:, k, t * P:(t + 1) * P], g_q[s][:, k, :],
                                             start=(k == t == 0), stop=(k == GT - 1), skip_group_check=True)
                        if k == GT - 1:
                            last.then_inc(*PE_.does(s, "wo"))

                    def up(s, u):
                        if u == 0:
                            if s == PE_.round[s] == 0:
                                pe.wait_ge(ca_ff_in, 16 * CA_FF_DMAS)
                            pe.wait_ge(*ACT_.did(s, "y1", 1))
                        for j in range(2):
                            for k in range(KT):
                                at = (2 * u + j) * P
                                last = pe.matmul(bank[s][u][:, j * S:(j + 1) * S], w1[:, k, at:at + P], yv[s][:, k, :],
                                                 start=(k == 0), stop=(k == KT - 1))
                        last.then_inc(*PE_.does(s, "up", u))

                    def down(s, k):
                        pe.wait_ge(*ACT_.did(s, "gelu", k // 2))
                        for t in range(KT):
                            last = pe.matmul(bank[s][0][:, t * S:(t + 1) * S], w2[:, k, t * P:(t + 1) * P], g_h[s][:, k, :],
                                             start=(k == t == 0), stop=(k == GT - 1), skip_group_check=True)
                        if k == GT - 1:
                            last.then_inc(*PE_.does(s, "down"))

                    stages(pe, {"center": center, "mean": mean, "normed": normed, "q": q, "memory": memory,
                                "scores": scores, "turn": turn, "values": values, "project": project, "up": up,
                                "down": down}, CA_ORDER, K, "x_out")

                @block.scalar
                def _(act):
                    def center(s, n):
                        act.wait_ge(*DVE_.did(s, "center", n))
                        act.activation(sq[s], yl[s], ACT.Square).then_inc(*ACT_.does(s, "square", n))

                    def normed(s, n):
                        gain, bias = (("qg", "qb"), ("fg", "fb"))[n]
                        act.wait_ge(*DVE_.did(s, "scaled", n))
                        for t in range(KT):
                            act.activation(yv[s][:, t, :], yl[s][:, t, :], ACT.Identity, bias=vec[bias][:, t:t + 1],
                                           scale=vec[gain][:, t:t + 1]).then_inc(*ACT_.does(s, f"y{t}", n))

                    def q(s, u):
                        act.wait_ge(*PE_.did(s, "q", u))
                        act.copy(g_q[s][:, 2 * u:2 * u + 2, :], two(bank[s][(3 + u) % 4][:])).then_inc(*ACT_.does(s, "q", u))

                    def scores(s, u):
                        act_softmax_exp(act, K, s, u, g_p[u][s], GHD ** -0.5)

                    def turn(s, u):
                        act_softmax_t(act, K, s, u, bank[s][(2 + u) % 4], g_t[s])

                    def values(s, u):
                        act.wait_ge(*PE_.did(s, "cpv", u))
                        act.copy(g_q[s][:, 2 * u:2 * u + 2, :], two(bank[s][(2 + u) % 4][:])).then_inc(*ACT_.does(s, "cpv", u))

                    def up(s, u):
                        act.wait_ge(*PE_.did(s, "up", u))
                        act.activation(g_h[s][:, 2 * u:2 * u + 2, :], two(bank[s][u][:]), ACT.Gelu)\
                           .then_inc(*ACT_.does(s, "gelu", u))

                    def give(s):
                        act.wait_ge(*DVE_.did(s, "x3"))
                        act.copy(x_all[:, :, tokens(ca_example(s))], xw[s]).then_inc(*ACT_.does(s, "x_out"))

                    stages(act, {"center": center, "normed": normed, "q": q, "scores": scores, "turn": turn,
                                 "values": values, "up": up, "give": give}, CA_ORDER, K, "x_out")

                @block.vector
                def _(dve):
                    def take(s):
                        dve.tensor_copy(xw[s], x_all[:, :, tokens(ca_example(s))]).then_inc(*DVE_.does(s, "x_in"))

                    def center(s, n):
                        dve.wait_ge(*PE_.did(s, "mu", n))
                        dve.tensor_tensor(yl[s], xw[s], bank[s][n][:, 0:S].unsqueeze(1).to_broadcast([P, KT, S]),
                                          ALU.subtract).then_inc(*DVE_.does(s, "center", n))

                    def mean(s, n):
                        dve_mean(dve, K, s, n, bank[s][1 + n], LN_EPS)

                    def normed(s, n):
                        dve.wait_ge(*PE_.did(s, "spread", n))
                        dve.tensor_tensor(yl[s], yl[s], bank[s][2 + n][:, 0:S].unsqueeze(1).to_broadcast([P, KT, S]),
                                          ALU.mult).then_inc(*DVE_.does(s, "scaled", n))

                    def memory(s):
                        b = bank[s]
                        dve.wait_ge(*PE_.did(s, "k"))
                        for i in range(2):
                            r = slice(i * M, (i + 1) * M)
                            dve.tensor_tensor(k_diag[s][r, :, i, :], b[3][r, :].rearrange("p (j m) -> p j m", j=GT),
                                              media[r, bass.ds(ca_example(s) * M, M)].unsqueeze(1).to_broadcast([M, GT, M]), ALU.mult)\
                               .then_inc(*DVE_.does(s, f"k{i}"))
                        for c in range(2):
                            dve.wait_ge(*PE_.did(s, f"v{c}"))
                            for i in range(2):
                                r = slice(i * M, (i + 1) * M)
                                dve.tensor_copy(v_diag[s][r, 4 * c:4 * c + 4, i * GHD:(i + 1) * GHD],
                                                b[c][r, :].rearrange("p (j i d) -> p j i d", i=2, d=GHD)[:, :, i, :])\
                                   .then_inc(*DVE_.does(s, f"v{c}{i}"))

                    def scores(s, u):
                        dve_softmax_shift(dve, K, s, u, bank[s][(2 + u) % 4], g_p[u][s])

                    def sums(s, u):
                        dve_softmax_sum(dve, K, s, u, g_p[u][s])

                    def project(s, k):
                        if k == GT - 1:
                            dve.wait_ge(*PE_.did(s, "wo"))
                            dve.scalar_tensor_tensor(xw[s], two(bank[s][0][:]), ca_gate[:, 0:1], xw[s], ALU.mult, ALU.add)\
                               .then_inc(*DVE_.does(s, "x2"))

                    def down(s, k):
                        if k == GT - 1:
                            dve.wait_ge(*PE_.did(s, "down"))
                            dve.scalar_tensor_tensor(xw[s], two(bank[s][0][:]), ca_gate[:, 1:2], xw[s], ALU.mult, ALU.add)\
                               .then_inc(*DVE_.does(s, "x3"))

                    stages(dve, {"take": take, "center": center, "mean": mean, "normed": normed, "memory": memory,
                                 "scores": scores, "sums": sums, "project": project, "down": down}, CA_ORDER, K, "x_out")
            clear_and_join()

        def before_second():
            with nc.Block() as block:
                @block.gpsimd
                def _(pool):
                    for s in range(STREAMS):
                        pool.memset(zeroed[s], 0.0)
                    pool.memset(down_w[:, 2 * FULL, :], 0.0).then_inc(pads_zero, 1)
                    tail = up_w[:, :, 2 * FULL * P:NF * P].rearrange("p k (e n) -> p k e n", e=2)
                    pool.memset(tail[:, :, :, TAIL:M], 0.0)

                @block.sync
                def _(sp):
                    sp.wait_ge(pads_zero, 4)
                    load_mot_ff(sp, mot_w[1])

        mot_layer(1, 3, before_second)


MOT = ("v_qkv", "l_qkv", "v_dense", "l_dense", "cq_w", "ckv_w", "cdense_w", "v_gate", "v_up", "v_down",
       "l_gate", "l_up", "l_down")
VEC = {"b_gate": "L0_xattn_b_gate", "fuse": "L0_xattn_norm_w", "qg": "L2_xattn_ln_q_g", "qb": "L2_xattn_ln_q_b",
       "fg": "L2_xattn_ln_ff_g", "fb": "L2_xattn_ln_ff_b",
       "in1": "L1_xattn_ln_in_w", "post1": "L1_xattn_ln_post_attn_w", "cross1": "L1_xattn_ln_post_cross_w",
       "in3": "L3_xattn_ln_in_w", "post3": "L3_xattn_ln_post_attn_w", "cross3": "L3_xattn_ln_post_cross_w"}


def kernel(**inputs):
    import concourse.bacc as bacc
    from concourse.bass_utils import run_bass_kernel_spmd

    nc = bacc.Bacc("TRN2", target_bir_lowering=False, num_devices=1)
    arrays, ap = {}, {}
    for name, value in inputs.items():
        a = np.ascontiguousarray(value)
        arrays["in_" + name] = a
        ap[name] = nc.dram_tensor("in_" + name, a.shape, mybir.dt.from_np(a.dtype), kind="ExternalInput").ap()
    table = nc.inline_tensor(constants(), name="table_of_constants").ap()
    out = nc.dram_tensor("out_x", (B, S, D), F32, kind="ExternalOutput").ap()
    program(nc, ap["x"], ap["ctx_1024"], ap["pos_1xS"], ap["mask_BxS_ik0"], ap["mask_BxS2_bk0"],
            {"W_mem": ap["L0_xattn_W_mem"], "W_gate": ap["L0_xattn_W_gate"], **{n: ap[k] for n, k in VEC.items()}},
            [{n: ap[f"L{i}_xattn_{n}"] for n in MOT} for i in (1, 3)],
            {n: ap["L2_xattn_" + n] for n in ("Wq", "Wkv", "Wo", "attn_gate", "W1", "W2", "ff_gate")},
            table, out)
    return run_bass_kernel_spmd(nc, [arrays], core_ids=[0]).results[0]["out_x"]
```
